# Optimizing a Trainium2 kernel written in Bass

```python
import numpy as np
import jax
import jax.numpy as jnp

def _softmax(x, axis=-1):
    return jax.nn.softmax(x, axis=axis)

def _gelu(x):
    return jax.nn.gelu(x, approximate=True)

def _silu(x):
    return jax.nn.silu(x)

def _sigmoid(x):
    return jax.nn.sigmoid(x)

def _layernorm(x, axis=-1, eps=1e-05):
    m = jnp.mean(x, axis=axis, keepdims=True)
    v = jnp.var(x, axis=axis, keepdims=True)
    return (x - m) / jnp.sqrt(v + eps)

def _scatter_add(tgt, idx, src, axis=0):
    return tgt.at[idx].add(src)

def _segment_sum(src, seg, n):
    return jax.ops.segment_sum(src, seg, n)
kernel_name = 'mk_gps_d2_gnn_r8_0a0a13'

def setup_inputs(seed: int=0):
    np.random.seed(seed)
    _w = jnp.asarray

    def _rec_inputs():
        import jax
        import jax.numpy as jnp
        _gk = jax.random.key(seed)
        x = -0.0002928 + 1 * jax.random.normal(jax.random.fold_in(_gk, 1), (1024, 512), jnp.float32)
        src = jax.random.randint(jax.random.fold_in(_gk, 2), (32768,), 0, 1024, jnp.int32)
        dst = jnp.minimum((1024 * jax.random.uniform(jax.random.fold_in(_gk, 3), (32768,)) ** 2.0).astype(jnp.int32), 8191)
        _o = jnp.argsort(dst, stable=True)
        src = src[_o]
        dst = dst[_o]
        return (x, src, dst)
    x, src, dst = _rec_inputs()

    def _L0_gnn_setup():
        import jax, jax.numpy as jnp
        import numpy as np
        N = 1024
        D = 512
        E = 32768
        STEPS = 3
        key = jax.random.key(seed)
        k1, k2, k3 = jax.random.split(key, 3)
        x = jax.random.normal(k1, (N, D), dtype=jnp.float32)
        edge_index = jax.random.randint(k2, (2, E), 0, N, dtype=jnp.int32)
        W = jax.random.normal(k3, (D, D), dtype=jnp.float32) / np.sqrt(D)
        b = jnp.zeros((D,), dtype=jnp.float32)
        diffusion_weights = jnp.ones((STEPS + 1,), dtype=jnp.float32) / (STEPS + 1)
        return {'x': x, 'edge_index': edge_index, 'W': W, 'b': b, 'diffusion_weights': diffusion_weights}
    _L0_gnn_all = _L0_gnn_setup()
    _L0_gnn_in = {k: v for k, v in _L0_gnn_all.items() if k in ('W', 'b', 'diffusion_weights')}
    del _L0_gnn_all

    def _L0_mix_setup():
        import jax, jax.numpy as jnp
        import numpy as np
        B, N, C = (8, 512, 512)
        key = jax.random.key(seed)
        ks = jax.random.split(key, 6)
        s = 1.0 / np.sqrt(C)
        return {'x': jax.random.normal(ks[0], (B, N, C), jnp.float32), 'Wq': jax.random.normal(ks[1], (C, C), jnp.float32) * s, 'Wk': jax.random.normal(ks[2], (C, C), jnp.float32) * s, 'Wv': jax.random.normal(ks[3], (C, C), jnp.float32) * s, 'W1': jax.random.normal(ks[4], (C, C), jnp.float32) * s, 'W2': jax.random.normal(ks[5], (C, C), jnp.float32) * s}
    _L0_mix_all = _L0_mix_setup()
    _L0_mix_in = {k: v for k, v in _L0_mix_all.items() if k in ('Wq', 'Wk', 'Wv', 'W1', 'W2')}
    del _L0_mix_all

    def _L0_ffn_setup():
        import jax, jax.numpy as jnp
        import numpy as np
        B, L, H, E, F, C = (8, 1024, 512, 8, 1024, 2)
        key = jax.random.key(seed)
        ks = jax.random.split(key, 4)
        x = jax.random.normal(ks[0], (B, L, H), jnp.float32)
        Wg = jax.random.normal(ks[1], (H, E), jnp.float32) * H ** (-0.5)
        W1 = jax.random.normal(ks[2], (E, H, F), jnp.float32) * H ** (-0.5)
        b1 = jnp.zeros((E, F), jnp.float32)
        W2 = jax.random.normal(ks[3], (E, F, H), jnp.float32) * F ** (-0.5)
        b2 = jnp.zeros((E, H), jnp.float32)
        return {'x': x, 'Wg': Wg, 'W1': W1, 'b1': b1, 'W2': W2, 'b2': b2}
    _L0_ffn_all = _L0_ffn_setup()
    _L0_ffn_in = {k: v for k, v in _L0_ffn_all.items() if k in ('Wg', 'W1', 'b1', 'W2', 'b2')}
    del _L0_ffn_all

    def _L1_gnn_setup():
        import jax, jax.numpy as jnp
        import numpy as np
        N, E, D, H = (1250, 20000, 512, 8)
        C = D // H
        key = jax.random.key(seed)
        ks = jax.random.split(key, 5)
        x = jax.random.normal(ks[0], (N, D), dtype=jnp.float32)
        edge_index = jax.random.randint(ks[1], (2, E), 0, N, dtype=jnp.int64 if jax.config.jax_enable_x64 else jnp.int32)
        scale = 1.0 / np.sqrt(D).astype(np.float32)
        W_l = jax.random.normal(ks[2], (D, D), dtype=jnp.float32) * scale
        W_r = jax.random.normal(ks[3], (D, D), dtype=jnp.float32) * scale
        att = jax.random.normal(ks[4], (H, C), dtype=jnp.float32) * np.float32(1.0 / np.sqrt(C))
        bias = jnp.zeros((D,), dtype=jnp.float32)
        return {'x': x, 'edge_index': edge_index, 'W_l': W_l, 'W_r': W_r, 'att': att, 'bias': bias}
    _L1_gnn_all = _L1_gnn_setup()
    _L1_gnn_in = {k: v for k, v in _L1_gnn_all.items() if k in ('W_l', 'W_r', 'att', 'bias')}
    del _L1_gnn_all

    def _L1_mix_setup():
        import jax, jax.numpy as jnp
        import numpy as np
        NUM_HEADS = 16
        EPS = 1e-15
        key = jax.random.key(seed)
        k1, k2, k3, k4 = jax.random.split(key, 4)
        B, N, C = (4, 2048, 512)
        x = jax.random.normal(k1, (B, N, C), dtype=jnp.float32)
        qkv_weight = jax.random.normal(k2, (3 * C, C), dtype=jnp.float32) * 0.02
        proj_weight = jax.random.normal(k3, (C, C), dtype=jnp.float32) * 0.02
        proj_bias = jax.random.normal(k4, (C,), dtype=jnp.float32) * 0.02
        return {'x': x, 'qkv_weight': qkv_weight, 'proj_weight': proj_weight, 'proj_bias': proj_bias}
    _L1_mix_all = _L1_mix_setup()
    _L1_mix_in = {k: v for k, v in _L1_mix_all.items() if k in ('qkv_weight', 'proj_weight', 'proj_bias')}
    del _L1_mix_all

    def _L1_ffn_setup():
        import jax, jax.numpy as jnp
        import numpy as np
        NUM_TILES = 64
        TPC = 8
        GRID = 16
        EPS = 1e-05
        key = jax.random.key(seed)
        ks = jax.random.split(key, 6)
        B, S, D, T, DH, G = (2, 1024, 512, NUM_TILES, 128, GRID)
        x = jax.random.normal(ks[0], (B, S, D), dtype=jnp.float32)
        gamma = jnp.ones((D,), jnp.float32)
        beta = jnp.zeros((D,), jnp.float32)
        Wd = jax.random.normal(ks[1], (T, DH, D), dtype=jnp.float32) * 0.02
        spline_bases = jax.random.normal(ks[2], (T, DH, G), dtype=jnp.float32) * 0.1
        spline_slopes = jax.random.normal(ks[3], (T, DH, G), dtype=jnp.float32) * 0.1
        Wu = jax.random.normal(ks[4], (T, D, DH), dtype=jnp.float32) * 0.02
        scale = jnp.full((T,), 0.1, jnp.float32)
        return {'x': x, 'gamma': gamma, 'beta': beta, 'Wd': Wd, 'spline_bases': spline_bases, 'spline_slopes': spline_slopes, 'Wu': Wu, 'scale': scale}
    _L1_ffn_all = _L1_ffn_setup()
    _L1_ffn_in = {k: v for k, v in _L1_ffn_all.items() if k in ('gamma', 'beta', 'Wd', 'spline_bases', 'spline_slopes', 'Wu', 'scale')}
    del _L1_ffn_all
    return {'x': x, 'src': src, 'dst': dst, 'L0_gnn_W': _L0_gnn_in['W'], 'L0_gnn_b': _L0_gnn_in['b'], 'L0_gnn_diffusion_weights': _L0_gnn_in['diffusion_weights'], 'L0_mix_Wq': _L0_mix_in['Wq'], 'L0_mix_Wk': _L0_mix_in['Wk'], 'L0_mix_Wv': _L0_mix_in['Wv'], 'L0_mix_W1': _L0_mix_in['W1'], 'L0_mix_W2': _L0_mix_in['W2'], 'L0_ffn_Wg': _L0_ffn_in['Wg'], 'L0_ffn_W1': _L0_ffn_in['W1'], 'L0_ffn_b1': _L0_ffn_in['b1'], 'L0_ffn_W2': _L0_ffn_in['W2'], 'L0_ffn_b2': _L0_ffn_in['b2'], 'L1_gnn_W_l': _L1_gnn_in['W_l'], 'L1_gnn_W_r': _L1_gnn_in['W_r'], 'L1_gnn_att': _L1_gnn_in['att'], 'L1_gnn_bias': _L1_gnn_in['bias'], 'L1_mix_qkv_weight': _L1_mix_in['qkv_weight'], 'L1_mix_proj_weight': _L1_mix_in['proj_weight'], 'L1_mix_proj_bias': _L1_mix_in['proj_bias'], 'L1_ffn_gamma': _L1_ffn_in['gamma'], 'L1_ffn_beta': _L1_ffn_in['beta'], 'L1_ffn_Wd': _L1_ffn_in['Wd'], 'L1_ffn_spline_bases': _L1_ffn_in['spline_bases'], 'L1_ffn_spline_slopes': _L1_ffn_in['spline_slopes'], 'L1_ffn_Wu': _L1_ffn_in['Wu'], 'L1_ffn_scale': _L1_ffn_in['scale']}

def reference(x, src, dst, L0_gnn_W, L0_gnn_b, L0_gnn_diffusion_weights, L0_mix_Wq, L0_mix_Wk, L0_mix_Wv, L0_mix_W1, L0_mix_W2, L0_ffn_Wg, L0_ffn_W1, L0_ffn_b1, L0_ffn_W2, L0_ffn_b2, L1_gnn_W_l, L1_gnn_W_r, L1_gnn_att, L1_gnn_bias, L1_mix_qkv_weight, L1_mix_proj_weight, L1_mix_proj_bias, L1_ffn_gamma, L1_ffn_beta, L1_ffn_Wd, L1_ffn_spline_bases, L1_ffn_spline_slopes, L1_ffn_Wu, L1_ffn_scale):
    import jax
    import jax.numpy as jnp

    def _L0_gnn_ref(x, edge_index, W, b, diffusion_weights):
        import jax, jax.numpy as jnp
        import numpy as np
        N = 1024
        D = 512
        E = 32768
        STEPS = 3
        h = x @ W + b
        row, col = (edge_index[0], edge_index[1])
        adj = jnp.zeros((N, N), dtype=h.dtype)
        adj = adj.at[row, col].set(1.0)
        adj = adj.at[col, row].set(1.0)
        adj = adj + jnp.eye(N, dtype=h.dtype)
        row_sum = adj.sum(axis=1, keepdims=True)
        adj = adj / jnp.maximum(row_sum, 1.0)
        out = diffusion_weights[0] * h
        cur = h
        for i in range(STEPS):
            cur = adj @ cur
            out = out + diffusion_weights[i + 1] * cur
        return jax.nn.relu(out)

    def _L0_mix_ref(x, Wq, Wk, Wv, W1, W2):
        import jax, jax.numpy as jnp
        import numpy as np
        B, N, C = (8, 512, 512)
        q = x @ Wq.T
        k = x @ Wk.T
        v = x @ Wv.T
        dim = q.shape[-1]
        q = jax.nn.softmax(q, axis=-1) * dim ** (-0.5)
        k = jax.nn.softmax(k, axis=-2)
        context = jnp.einsum('bnd,bne->bde', k, v)
        attn = jnp.einsum('bnd,bde->bne', q, context)
        x = attn + x
        return x @ W1.T @ W2.T + x

    def _L0_ffn_ref(x, Wg, W1, b1, W2, b2):
        import jax, jax.numpy as jnp
        import numpy as np
        B, L, H, E, F, C = (8, 1024, 512, 8, 1024, 2)
        b, l, h = x.shape
        e = Wg.shape[1]
        k = min(max(int(l * C / e), 1), l)
        S = jax.nn.softmax(x @ Wg, axis=-1)
        St = jnp.swapaxes(S, 1, 2)
        G, I = jax.lax.top_k(St, k)
        ex = jnp.take_along_axis(x[:, None], I[..., None], axis=2)
        hmid = jax.nn.gelu(jnp.einsum('bekh,ehf->bekf', ex, W1) + b1[None, :, None, :], approximate=False)
        out = jnp.einsum('bekf,efh->bekh', hmid, W2) + b2[None, :, None, :]
        vals = G[..., None] * out
        new_x = jnp.zeros_like(x).at[jnp.arange(b)[:, None, None], I].add(vals)
        return new_x

    def _L1_gnn_ref(x, edge_index, W_l, W_r, att, bias):
        import jax, jax.numpy as jnp
        import numpy as np
        N, E, D, H = (1250, 20000, 512, 8)
        C = D // H
        n = x.shape[0]
        self_idx = jnp.arange(n, dtype=edge_index.dtype)
        src = jnp.concatenate([edge_index[0], self_idx])
        dst = jnp.concatenate([edge_index[1], self_idx])
        x_l = (x @ W_l).reshape(n, H, C)
        x_r = (x @ W_r).reshape(n, H, C)
        m = jax.nn.leaky_relu(x_l[src] + x_r[dst], negative_slope=0.2)
        alpha = jnp.einsum('ehc,hc->eh', m, att)
        amax = jax.lax.stop_gradient(jax.ops.segment_max(alpha, dst, num_segments=n))
        ea = jnp.exp(alpha - amax[dst])
        denom = jax.ops.segment_sum(ea, dst, num_segments=n)
        w = ea / jnp.maximum(denom[dst], 1e-16)
        out = jax.ops.segment_sum(w[:, :, None] * x_l[src], dst, num_segments=n)
        out = out.reshape(n, H * C) + bias
        return jax.nn.elu(out) + x

    def _L1_mix_ref(x, qkv_weight, proj_weight, proj_bias):
        import jax, jax.numpy as jnp
        import numpy as np
        NUM_HEADS = 16
        EPS = 1e-15
        B, N, C = x.shape
        H = NUM_HEADS
        D = C // H
        qkv = (x @ qkv_weight.T).reshape(B, N, 3, C)
        q = jax.nn.relu(qkv[:, :, 0]).reshape(B, N, H, D)
        k = jax.nn.relu(qkv[:, :, 1]).reshape(B, N, H, D)
        v = qkv[:, :, 2].reshape(B, N, H, D)
        qf = q.astype(jnp.float32)
        kf = k.astype(jnp.float32)
        vf = v.astype(jnp.float32)
        v_pad = jnp.concatenate([vf, jnp.ones_like(vf[..., :1])], axis=-1)
        vk = jnp.einsum('bnhc,bnhd->bhcd', v_pad, kf)
        vk_q = jnp.einsum('bnhd,bhcd->bnhc', qf, vk)
        proj_input = (vk_q[..., :-1] / (vk_q[..., -1:] + EPS)).astype(x.dtype).reshape(B, N, C)
        return proj_input @ proj_weight.T + proj_bias

    def _L1_ffn_ref(x, gamma, beta, Wd, spline_bases, spline_slopes, Wu, scale):
        import jax, jax.numpy as jnp
        import numpy as np
        NUM_TILES = 64
        TPC = 8
        GRID = 16
        EPS = 1e-05
        B, S, D = x.shape
        T, DH, _ = Wd.shape
        C = T // TPC
        N = B * S
        mu = x.mean(-1, keepdims=True)
        var = ((x - mu) ** 2).mean(-1, keepdims=True)
        xn = (x - mu) * jax.lax.rsqrt(var + EPS) * gamma + beta
        xf = xn.reshape(N, D)
        tile_sigs = jnp.sign(Wd.mean(axis=1))
        cluster_sigs = jnp.sign(tile_sigs.reshape(C, TPC, D).mean(1))
        in_sigs = jnp.sign(xf)
        best_c = jnp.argmax(in_sigs @ cluster_sigs.T, axis=-1)
        tile_scores = (in_sigs @ tile_sigs.T).reshape(N, C, TPC)
        sc = jnp.take_along_axis(tile_scores, best_c[:, None, None], axis=1)[:, 0, :]
        local_best = jnp.argmax(sc, axis=-1)
        tidx = best_c * TPC + local_best
        h = jnp.einsum('nd,nhd->nh', xf, Wd[tidx])
        hn = jax.nn.sigmoid(h)
        idx = jnp.clip((hn * GRID).astype(jnp.int32), 0, GRID - 1)
        base = jnp.take_along_axis(spline_bases[tidx], idx[..., None], axis=-1)[..., 0]
        slope = jnp.take_along_axis(spline_slopes[tidx], idx[..., None], axis=-1)[..., 0]
        local_pos = hn * GRID - idx.astype(h.dtype)
        hs = base + slope * local_pos
        y = jnp.einsum('nh,ndh->nd', hs, Wu[tidx]) * scale[tidx][:, None]
        return x + y.reshape(B, S, D)
    edge_index = jnp.stack([src, dst])
    xn = _layernorm(x, axis=-1)
    x = x + _L0_gnn_ref(xn, edge_index, L0_gnn_W, L0_gnn_b, L0_gnn_diffusion_weights) + _L0_mix_ref(xn[None], L0_mix_Wq, L0_mix_Wk, L0_mix_Wv, L0_mix_W1, L0_mix_W2)[0]
    x = x + _L0_ffn_ref(_layernorm(x, axis=-1)[None], L0_ffn_Wg, L0_ffn_W1, L0_ffn_b1, L0_ffn_W2, L0_ffn_b2)[0]
    xn = _layernorm(x, axis=-1)
    x = x + _L1_gnn_ref(xn, edge_index, L1_gnn_W_l, L1_gnn_W_r, L1_gnn_att, L1_gnn_bias) + _L1_mix_ref(xn[None], L1_mix_qkv_weight, L1_mix_proj_weight, L1_mix_proj_bias)[0]
    x = x + _L1_ffn_ref(_layernorm(x, axis=-1)[None], L1_ffn_gamma, L1_ffn_beta, L1_ffn_Wd, L1_ffn_spline_bases, L1_ffn_spline_slopes, L1_ffn_Wu, L1_ffn_scale)[0]
    return x

_drawn_inputs = setup_inputs


def setup_inputs(seed=0):
    import zlib

    import numpy as np

    out = dict(_drawn_inputs(seed))
    spreads = {'L0_gnn_b': (0.0, 0.1),
     'L0_gnn_diffusion_weights': (0.25, 0.6),
     'L0_ffn_b1': (0.0, 0.593),
     'L0_ffn_b2': (0.0, 0.393),
     'L1_gnn_bias': (0.0, 0.277),
     'L1_ffn_gamma': (1.0, 0.6),
     'L1_ffn_beta': (0.0, 0.8),
     'L1_ffn_scale': (0.10000000149011612, 0.6)}
    factors = {'L0_mix_Wq': 8.0,
     'L0_mix_Wk': 8.0,
     'L0_mix_Wv': 8.0,
     'L1_gnn_W_r': 3.254,
     'L1_mix_qkv_weight': 8.0,
     'L1_mix_proj_weight': 8.0,
     'L1_mix_proj_bias': 8.0,
     'L1_ffn_Wd': 8.0,
     'L1_ffn_spline_bases': 8.0,
     'L1_ffn_spline_slopes': 8.0,
     'L1_ffn_Wu': 8.0}
    for name, (base, spread) in spreads.items():
        noise = np.random.default_rng([zlib.crc32(name.encode()), seed]).standard_normal(out[name].shape)
        drawn = base * np.exp(spread * noise) if base else spread * noise
        out[name] = jnp.asarray(drawn.astype(out[name].dtype))
    for name, factor in factors.items():
        out[name] = (out[name] * factor).astype(out[name].dtype)
    return out
```

```python
from contextlib import ExitStack, contextmanager

import concourse.bass as bass
from concourse import mybir

P = 128
N = 1024
D = 512
NT = N // P
KD = D // P
E = 32768
EC = E // P
CH = EC + NT
NG = N // P
NB = CH + NG
EP = NB * P
SEG = 16
BS = NB // SEG
SL = BS * P
H8 = 8
HC = D // H8
BIG = 1.0e30

F32 = mybir.dt.float32
F16 = mybir.dt.float16
BF16 = mybir.dt.bfloat16
I32 = mybir.dt.int32
ALU = mybir.AluOpType
ACT = mybir.ActivationFunctionType
AX = mybir.AxisListType


class Chain:

    def __init__(self, eng, sem, base=0):
        self.eng, self.sem, self.base, self.n = eng, sem, base, 0

    def mark(self, ins):
        ins.then_inc(self.sem, 1)
        self.n += 1
        return self.n

    def then(self, ins):
        self.mark(ins)
        self.eng.wait_ge(self.sem, self.base + self.n)


class Mem:

    def __init__(self, nc, ctx, stage):
        self.nc, self.ctx, self.stage = nc, ctx, stage

    def sb(self, name, shape, dt=F32):
        return self.ctx.enter_context(self.nc.sbuf_tensor(f"{self.stage}_{name}", shape, dt))

    def ps(self, name, shape, dt=F32):
        return self.ctx.enter_context(self.nc.psum_tensor(f"{self.stage}_{name}", shape, dt))

    def sem(self, name):
        return self.nc.alloc_semaphore(name=f"{self.stage}_{name}")


@contextmanager
def part(nc):
    with nc.cleanup_on_exit():
        yield
    nc.all_engine_barrier()


def scatter(pool, table, slot, rows, count, idx, buf, staged, sent, filled):
    G = 8
    lots = count // G

    def stage(n, b):
        pool.tensor_copy(idx[:, b, :], slot[:, bass.ds(G * n, G)]).then_inc(staged, 1)
        pool.tensor_copy(buf[:, b, :, :], rows[:, bass.ds(G * n, G), :]).then_inc(staged, 1)

    def send(b):
        for j in range(G):
            pool.indirect_dma_start(out=table, out_offset=bass.IndirectOffsetOnAxis(ap=idx[:, b, j:j + 1], axis=0),
                                    in_=buf[:, b, j, :], in_offset=None).then_inc(sent[b], 16)
    stage(0, 0)
    pool.wait_ge(staged, 2)
    stage(1, 1)
    send(0)
    with pool.Fori(0, lots // 2 - 1) as t:
        for b in range(2):
            pool.wait_ge(staged, 4 * t + 2 * b + 4)
            pool.wait_ge(sent[b], 16 * G * (t + 1))
            stage(2 * t + b + 2, b)
            send(1 - b)
    pool.wait_ge(staged, 4 * (lots // 2))
    if lots % 2:
        pool.wait_ge(sent[0], 16 * G * (lots // 2))
        stage(lots - 1, 0)
    send(1)
    if lots % 2:
        pool.wait_ge(staged, 2 * lots)
        send(0)
    pool.wait_ge(sent[0], 16 * G * (lots - lots // 2))
    pool.wait_ge(sent[1], 16 * G * (lots // 2))


def constants(nc, k):
    with ExitStack() as ctx:
        m = Mem(nc, ctx, "const")
        made, laid = m.sem("made"), m.sem("laid")
        row = m.sb("row", [P, N], I32)
        with nc.Block() as block:
            @block.gpsimd
            def _(pool):
                c = Chain(pool, made)
                c.then(pool.iota(row[:, :], [[1, N]], base=0, channel_multiplier=0))
                c.then(pool.iota(k.lane_i[:, :], [[0, 1]], base=0, channel_multiplier=1))
                c.then(pool.memset(k.ident[:, :], 0.0))
                c.then(pool.memset(k.ones[:, :], 1.0))
                c.then(pool.affine_select(out=k.ident[:, :], in_=k.ident[:, :], compare_op=ALU.not_equal, fill=1.0,
                                          base=0, pattern=[[-1, P]], channel_multiplier=1))
                c.then(pool.affine_select(out=k.before[:, :], in_=k.ones[:, :], compare_op=ALU.is_gt, fill=0.0,
                                          base=0, pattern=[[1, P]], channel_multiplier=-1))

            @block.vector
            def _(dve):
                dve.wait_ge(made, 6)
                c = Chain(dve, laid)
                c.mark(dve.tensor_copy(k.iota16[:, :], row[:, :]))
                c.mark(dve.tensor_copy(k.iotaf[:, :], row[:, :]))
                c.mark(dve.tensor_copy(k.lane[:, :], k.lane_i[:, :]))
                c.mark(dve.tensor_copy(k.ones_b[:, :], k.ones[:, :]))
                c.mark(dve.tensor_copy(k.ident_b[:, :], k.ident[:, :]))
                c.mark(dve.tensor_copy(k.before_b[:, :], k.before[:, :]))
                c.mark(dve.tensor_scalar(k.later[:, :], k.before[:, :], -1.0, 1.0, ALU.mult, ALU.add))
                dve.wait_ge(laid, c.n)
                c.mark(dve.tensor_tensor(k.later[:, :], k.later[:, :], k.ident[:, :], ALU.subtract))
                c.mark(dve.tensor_scalar(k.notbefore_b[:, :], k.before[:, :], -1.0, 1.0, ALU.mult, ALU.add))


def sort_edges(nc, k, src, dst, keys_t):
    with ExitStack() as ctx:
        m = Mem(nc, ctx, "sort")
        S, U = 2, 4
        dst_i = m.sb("dst_i", [P, CH], I32)
        src_i = m.sb("src_i", [P, CH], I32)
        dstf = m.sb("dstf", [P, CH])
        srcf = m.sb("srcf", [P, CH])
        key = m.sb("key", [P, CH])
        slotf = m.sb("slotf", [P, CH])
        slot_i = m.sb("slot_i", [P, CH], I32)
        part_i = m.sb("part_i", [P, 2, CH], I32)
        at_lane = m.sb("at_lane", [P, CH])
        at_block = m.sb("at_block", [P, CH])
        onehot = m.sb("onehot", [P, U, N], BF16)
        lanes = m.sb("lanes", [P, U, P], F16)
        values = m.sb("values", [P, U, 2, NB], F16)
        junk = m.sb("junk", [P, 2, N], BF16)
        zb = m.sb("zb", [P, D], BF16)
        counts = m.sb("counts", [P, S, N])
        base = m.sb("base", [P, S, N])
        incl = m.sb("incl", [P, N])
        total_i = m.sb("total_i", [P, NG], I32)
        nblk = m.sb("nblk", [P, NG])
        gend = m.sb("gend", [P, NG])
        gstart = m.sb("gstart", [P, NG])
        ging = m.sb("ging", [P, NB, NG])
        keyrow = m.sb("keyrow", [SEG, SL])
        guard = m.sb("guard", [1, 2])
        with ExitStack() as inner:
            mi = Mem(nc, inner, "sortp")
            acc = mi.ps("acc", [P, S, N])
            placed = [mi.ps(f"placed{i}", [P, D]) for i in range(2)]
            loaded, ready, made, used = (m.sem(x) for x in ("loaded", "ready", "made", "used"))
            based, before, dotted, after = (m.sem(x) for x in ("based", "before", "dotted", "after"))
            zeroed, steps, laid, placed_n = (m.sem(x) for x in ("zeroed", "steps", "laid", "placed_n"))
            with nc.Block() as block:
                @block.sync
                def _(sp):
                    sp.dma_start(dst_i[:, 0:EC], dst.rearrange("(p c) -> p c", p=P)).then_inc(loaded, 16)
                    sp.dma_start(src_i[:, 0:EC], src.rearrange("(p c) -> p c", p=P)).then_inc(loaded, 16)

                @block.vector
                def _(dve):
                    c = Chain(dve, steps)
                    dve.memset(zb[:, :], 0.0).then_inc(zeroed, 1)
                    for i in range(NT):
                        c.mark(dve.tensor_scalar(dstf[:, EC + i:EC + i + 1], k.lane[:, :], float(P * i), None, ALU.add))
                        c.mark(dve.tensor_scalar(srcf[:, EC + i:EC + i + 1], k.lane[:, :], float(P * i), None, ALU.add))
                    dve.wait_ge(loaded, 32)
                    c.mark(dve.tensor_copy(dstf[:, 0:EC], dst_i[:, 0:EC]))
                    c.then(dve.tensor_copy(srcf[:, 0:EC], src_i[:, 0:EC]))
                    c.mark(dve.tensor_scalar(key[:, :], dstf[:, :], 1.0, None, ALU.add))

                    def hot(n, u):
                        dve.tensor_scalar(onehot[:, u, :], k.iota16[:, :], dstf[:, bass.ds(n, 1)], None,
                                          ALU.is_equal).then_inc(made, 1)
                    for u in range(U):
                        hot(u, u)
                    with dve.Fori(1, CH // U) as t:
                        for u in range(U):
                            dve.wait_ge(used, U * t + u - U + 1)
                            hot(U * t + u, u)
                    dve.wait_ge(used, CH)
                    for u in range(U):
                        hot(u, u)
                    for s in range(S):
                        c.mark(dve.tensor_copy(counts[:, s, :], acc[:, s, :]))
                    dve.wait_ge(steps, c.n)
                    c.then(dve.tensor_tensor(base[:, 1, :], counts[:, 0, :], counts[:, 1, :], ALU.add))
                    for g in range(NG):
                        c.mark(dve.tensor_tensor_scan(incl[:, g * P:(g + 1) * P], base[:, 1, g * P:(g + 1) * P], k.ones[:, :],
                                                      0.0, ALU.add, ALU.mult))
                    dve.wait_ge(steps, c.n)
                    c.then(dve.tensor_scalar(total_i[:, :], incl[:, P - 1::P], float(P - 1), None, ALU.add))
                    c.then(dve.tensor_scalar(total_i[:, :], total_i[:, :], 7, None, ALU.arith_shift_right))
                    c.then(dve.tensor_copy(nblk[:, :], total_i[:, :]))
                    c.then(dve.tensor_tensor_scan(gend[:, :], nblk[:, :], k.ones[:, 0:NG], 0.0, ALU.add, ALU.mult))
                    c.then(dve.tensor_tensor(gstart[:, :], gend[:, :], nblk[:, :], ALU.subtract))
                    c.then(dve.tensor_scalar(gstart[:, :], gstart[:, :], float(P), None, ALU.mult))
                    c.then(dve.tensor_tensor(base[:, 0, :], incl[:, :], base[:, 1, :], ALU.subtract))
                    for g in range(NG):
                        c.mark(dve.tensor_scalar(base[:, 0, g * P:(g + 1) * P], base[:, 0, g * P:(g + 1) * P],
                                                 gstart[:, g:g + 1], None, ALU.add))
                    dve.wait_ge(steps, c.n)
                    dve.tensor_tensor(base[:, 1, :], base[:, 0, :], counts[:, 0, :], ALU.add).then_inc(based, 1)
                    def dot(n, u, b):
                        dve.wait_ge(before, n + 1)
                        dve.scalar_tensor_tensor(junk[:, b, :], k.iota16[:, :], dstf[:, bass.ds(n, 1)],
                                                 acc[:, u % S, :], ALU.is_equal, ALU.mult,
                                                 accum_out=slotf[:, bass.ds(n, 1)]).then_inc(dotted, 1)
                    dot(0, 0, 0)
                    with dve.Fori(0, CH // U - 1) as t:
                        for u in range(U):
                            n = U * t + (u + 1)
                            dve.wait_ge(dotted, n)
                            dot(n, (u + 1) % U, (u + 1) % 2)
                            dve.wait_ge(after, n)
                            hot(n + (U - 1), u)
                    for n in range(CH - U + 1, CH):
                        dve.wait_ge(dotted, n)
                        dot(n, n % U, n % 2)
                    c.then(dve.tensor_tensor(ging[:, :, :], k.iotaf[:, 0:NB].unsqueeze(2).broadcast_to([P, NB, NG]),
                                             gend[:, :].unsqueeze(1).broadcast_to([P, NB, NG]), ALU.is_ge))
                    c.then(dve.tensor_reduce(k.group[:, :], ging[:, :, :], AX.X, ALU.add))
                    c.then(dve.tensor_scalar(k.group[:, :], k.group[:, :], float(NG - 1), None, ALU.min))
                    c.mark(dve.tensor_scalar(k.group_i[:, :], k.group[:, :], float(D), None, ALU.mult))
                    dve.wait_ge(dotted, CH)
                    c.then(dve.tensor_copy(slot_i[:, :], slotf[:, :]))
                    c.mark(dve.tensor_scalar(part_i[:, 0, :], slot_i[:, :], P - 1, None, ALU.bitwise_and))
                    c.then(dve.tensor_scalar(part_i[:, 1, :], slot_i[:, :], P.bit_length() - 1, None, ALU.arith_shift_right))
                    c.mark(dve.tensor_copy(at_lane[:, :], part_i[:, 0, :]))
                    c.then(dve.tensor_copy(at_block[:, :], part_i[:, 1, :]))

                    def lay(n, u):
                        dve.tensor_scalar(lanes[:, u, :], k.iota16[:, 0:P], at_lane[:, bass.ds(n, 1)], None, ALU.is_equal)
                        for f, v in enumerate((srcf, key)):
                            i = dve.tensor_scalar(values[:, u, f, :], k.iota16[:, 0:NB], at_block[:, bass.ds(n, 1)],
                                                  v[:, bass.ds(n, 1)], ALU.is_equal, ALU.mult)
                        i.then_inc(laid, 1)
                    for u in range(U):
                        lay(u, u)
                    with dve.Fori(1, CH // U) as t:
                        for u in range(U):
                            dve.wait_ge(placed_n, U * t + u - U + 1)
                            lay(U * t + u, u)
                    dve.wait_ge(placed_n, CH)
                    c.mark(dve.tensor_copy(k.srcf[:, :], placed[0][:, 0:NB]))
                    c.then(dve.tensor_copy(k.key[:, :], placed[1][:, 0:NB]))
                    c.mark(dve.tensor_copy(k.src_i[:, :], k.srcf[:, :]))
                    c.mark(dve.tensor_scalar(k.dst_i[:, :], k.key[:, :], -1.0, 0.0, ALU.add, ALU.max))
                    c.then(dve.tensor_scalar(k.local[:, :], k.group[:, :], float(-P), -1.0, ALU.mult, ALU.add))
                    c.then(dve.tensor_tensor(k.local[:, :], k.local[:, :], k.key[:, :], ALU.add))

                @block.tensor
                def _(pe):
                    def open_banks(banks):
                        for x in banks:
                            pe.matmul(x, k.ones_b[:, :], zb[:, 0:x.shape[-1]], start=True, stop=False, skip_group_check=True)

                    def add(x, lhsT, rhs):
                        return pe.matmul(x, lhsT, rhs, start=False, stop=False, skip_group_check=True)
                    halves = [slice(h * D, (h + 1) * D) for h in range(2)]
                    pe.wait_ge(zeroed, 1)
                    open_banks([acc[:, s, h] for s in range(S) for h in halves])
                    open_banks([x[:, :] for x in placed])
                    with pe.Fori(0, CH // U) as t:
                        for u in range(U):
                            pe.wait_ge(made, U * t + u + 1)
                            for h in halves:
                                i = add(acc[:, u % S, h], k.ones_b[:, :], onehot[:, u, h])
                            i.then_inc(used, 1)
                    pe.wait_ge(based, 1)
                    for s in range(S):
                        for h in halves:
                            pe.matmul(acc[:, s, h], k.ones[0:1, :], base[0:1, s, h], start=True, stop=False, skip_group_check=True)

                    def chunk(n, u):
                        pe.wait_ge(made, n + (CH + 1))
                        for h in halves:
                            i = add(acc[:, u % S, h], k.before_b[:, :], onehot[:, u, h])
                        i.then_inc(before, 1)

                    def close(n, u):
                        pe.wait_ge(dotted, n + 1)
                        for h in halves:
                            i = add(acc[:, u % S, h], k.notbefore_b[:, :], onehot[:, u, h])
                        i.then_inc(after, 1)
                    chunk(0, 0)
                    with pe.Fori(0, CH // U - 1) as t:
                        for u in range(U):
                            chunk(U * t + (u + 1), (u + 1) % U)
                            close(U * t + u, u)
                    for u in range(U):
                        n = CH - U + u
                        if n + 1 < CH:
                            chunk(n + 1, u + 1)
                        close(n, u)
                    with pe.Fori(0, CH // U) as t:
                        for u in range(U):
                            pe.wait_ge(laid, U * t + u + 1)
                            for f in range(2):
                                i = add(placed[f][:, 0:NB], lanes[:, u, :], values[:, u, f, :])
                            i.then_inc(placed_n, 1)
        keyp = m.ps("keyp", [SEG, 5 * D])
        turned, copied, stored, guarded = (m.sem(x) for x in ("turned", "copied", "stored", "guarded"))
        with nc.Block() as block:
            @block.tensor
            def _(pe):
                for i in range(BS):
                    t = pe.transpose(keyp[:, i * P:(i + 1) * P], k.key[:, i::BS], k.ident[:, :])
                t.then_inc(turned, 1)

            @block.vector
            def _(dve):
                dve.memset(guard[:, 0:1], 0.0).then_inc(guarded, 1)
                dve.memset(guard[:, 1:2], -1.0).then_inc(guarded, 1)
                dve.wait_ge(turned, 1)
                dve.tensor_copy(keyrow[:, :], keyp[:, 0:SL]).then_inc(copied, 1)

            @block.sync
            def _(sp):
                row = keys_t.rearrange("(a n) -> a n", a=1)
                sp.wait_ge(guarded, 2)
                sp.dma_start(row[:, 0:1], guard[:, 0:1]).then_inc(stored, 16)
                sp.dma_start(row[:, EP + 1:EP + 2], guard[:, 1:2]).then_inc(stored, 16)
                sp.wait_ge(copied, 1)
                sp.dma_start(keys_t[1:EP + 1].rearrange("(s n) -> s n", s=SEG), keyrow[:, :]).then_inc(stored, 16)
                sp.wait_ge(stored, 48)


class Keep:
    pass


def keep(nc, ctx):
    k = Keep()
    m = Mem(nc, ctx, "k")
    k.ident = m.sb("ident", [P, P])
    k.ident_b = m.sb("ident_b", [P, P], BF16)
    k.ones = m.sb("ones", [P, P])
    k.ones_b = m.sb("ones_b", [P, P], BF16)
    k.before = m.sb("before", [P, P])
    k.before_b = m.sb("before_b", [P, P], BF16)
    k.notbefore_b = m.sb("notbefore_b", [P, P], BF16)
    k.later = m.sb("later", [P, P])
    k.iota16 = m.sb("iota16", [P, N], F16)
    k.iotaf = m.sb("iotaf", [P, N])
    k.lane_i = m.sb("lane_i", [P, 1], I32)
    k.lane = m.sb("lane", [P, 1])
    k.group = m.sb("group", [P, NB])
    k.group_i = m.sb("group_i", [P, NB], I32)
    k.srcf = m.sb("srcf", [P, NB])
    k.src_i = m.sb("src_i", [P, NB], I32)
    k.dst_i = m.sb("dst_i", [P, NB], I32)
    k.local = m.sb("local", [P, NB])
    k.key = m.sb("key", [P, NB])
    return k


def block_groups(nc, k, first, count):
    _, values = nc.values_load_multi_w_load_instructions(
        k.group_i[0:1, bass.ds(first, count)], engines=[mybir.EngineType.PE], min_val=0, max_val=(NG - 1) * D,
        skip_runtime_bounds_check_because="k.group_i is clamped to the last group where it is made")
    return values


def adjacency(nc, k, adj, rs):
    with ExitStack() as ctx:
        m = Mem(nc, ctx, "adj")
        U = 8
        zb = m.sb("zb", [P, D], BF16)
        to = m.sb("to", [P, U, P], BF16)
        frm = m.sb("frm", [P, U, D], BF16)
        cnt = m.sb("cnt", [P, NG, N], BF16)
        both = m.sb("both", [P, 2, N], BF16)
        two = m.sb("two", [P, P], BF16)
        zeroed, made, used, counted, capped = (m.sem(x) for x in ("zeroed", "made", "used", "counted", "capped"))
        turned, summed, steps = (m.sem(x) for x in ("turned", "summed", "steps"))
        with ExitStack() as inner:
            mi = Mem(nc, inner, "adjc")
            acc = mi.ps("acc", [P, NG * D])
            with nc.Block() as block:
                @block.vector
                def _(dve):
                    dve.memset(zb[:, :], 0.0).then_inc(zeroed, 1)

                    def onehots(n, u, h):
                        dve.tensor_scalar(to[:, u, :], k.iota16[:, 0:P], k.local[:, bass.ds(n, 1)], None,
                                          ALU.is_equal).then_inc(made, 1)
                        dve.tensor_scalar(frm[:, u, :], k.iota16[:, h * D:(h + 1) * D], k.srcf[:, bass.ds(n, 1)], None,
                                          ALU.is_equal).then_inc(made, 1)
                    for h in range(2):
                        for u in range(U):
                            if h:
                                dve.wait_ge(used, NB * h)
                            onehots(u, u, h)
                        with dve.Fori(1, NB // U) as t:
                            for u in range(U):
                                dve.wait_ge(used, U * t + (u + 1 - U + NB * h))
                                onehots(U * t + u, u, h)
                        dve.wait_ge(used, NB * (h + 1))
                        for g in range(NG):
                            dve.tensor_scalar(cnt[:, g, h * D:(h + 1) * D], acc[:, g * D:(g + 1) * D], 3.0, None,
                                              ALU.min).then_inc(capped, 1)

                @block.tensor
                def _(pe):
                    pe.wait_ge(zeroed, 1)
                    for h in range(2):
                        if h:
                            pe.wait_ge(capped, NG)
                        for g in range(NG):
                            pe.matmul(acc[:, g * D:(g + 1) * D], k.ones_b[:, :], zb[:, :], start=True, stop=False,
                                      skip_group_check=True)
                        with pe.Fori(0, NB // U) as t:
                            groups = block_groups(nc, k, U * t, U)
                            for u in range(U):
                                g = groups[u]
                                pe.wait_ge(made, 2 * (U * t + u) + (2 + 2 * NB * h))
                                pe.matmul(acc[:, bass.ds(g, D)], to[:, u, :], frm[:, u, :], start=False, stop=False,
                                          skip_group_check=True).then_inc(used, 1)
        tp = m.ps("tp", [P, 2, N], BF16)
        with nc.Block() as block:
            @block.tensor
            def _(pe):
                for i in range(NT):
                    if i >= 2:
                        pe.wait_ge(summed, i - 1)
                    for j in range(NT):
                        t = pe.transpose(tp[:, i % 2, j * P:(j + 1) * P], cnt[:, j, i * P:(i + 1) * P], k.ident_b[:, :])
                    t.then_inc(turned, 1)

            @block.vector
            def _(dve):
                c = Chain(dve, steps)
                c.then(dve.tensor_scalar(two[:, :], k.ident[:, :], 2.0, None, ALU.mult))
                for i in range(NT):
                    here = slice(i * P, (i + 1) * P)
                    dve.wait_ge(turned, i + 1)
                    dve.tensor_tensor(both[:, i % 2, :], cnt[:, i, :], tp[:, i % 2, :], ALU.add).then_inc(summed, 1)
                    dve.wait_ge(summed, i + 1)
                    c.then(dve.tensor_tensor(both[:, i % 2, here], both[:, i % 2, here], two[:, :], ALU.subtract))
                    c.then(dve.tensor_scalar(adj[:, i, :], both[:, i % 2, :], 0.0, None, ALU.is_gt))
                    c.then(dve.tensor_tensor(adj[:, i, here], adj[:, i, here], k.ident[:, :], ALU.add))
                c.then(dve.tensor_reduce(rs[:, :], adj[:, :, :], AX.X, ALU.add))
                c.then(dve.tensor_scalar(rs[:, :], rs[:, :], 1.0, None, ALU.max))
                c.then(dve.reciprocal(rs[:, :], rs[:, :]))


def products(nc, name, count, produce, evacuate, width=D, dt=F32, ring=4, vector=True, scalar=True, before=None):
    with ExitStack() as ctx:
        m = Mem(nc, ctx, name)
        bank = [m.ps(f"bank{i}", [P, D if dt == F32 else 2 * D], dt) for i in range(ring)]
        full = m.sem("full")
        free = [m.sem("free_even"), m.sem("free_odd")]
        both = vector and scalar
        with nc.Block() as block:
            @block.tensor
            def _(pe):
                for n in range(count):
                    if n >= ring:
                        done = n - ring + 1
                        pe.wait_ge(free[(n - ring) % 2] if both else free[0], (done + 1) // 2 if both and (n - ring) % 2 == 0
                                   else done // 2 if both else done)
                    produce(pe, n, bank[n % ring]).then_inc(full, 1)

            def drain(eng, which):
                for n in range(count):
                    if not both or n % 2 == which:
                        eng.wait_ge(full, n + 1)
                        evacuate(eng, n, bank[n % ring]).then_inc(free[which if both else 0], 1)

            if vector:
                @block.vector
                def _(dve):
                    drain(dve, 0)
            if scalar:
                @block.scalar
                def _(act):
                    drain(act, 1)


def copy(eng, out, in_):
    return eng.activation(out, in_, ACT.Copy) if isinstance(eng, bass.BassScalarEngine) else eng.tensor_copy(out, in_)


def accumulate(pe, bank, terms):
    for i, (lhsT, rhs) in enumerate(terms):
        last = pe.matmul(bank, lhsT, rhs, start=(i == 0), stop=(i == len(terms) - 1))
    return last


def turn(nc, k, name, src, dst):
    def produce(pe, n, bank):
        for c in range(KD):
            t = pe.transpose(bank[:, c * P:(c + 1) * P], src[:, n, c * P:(c + 1) * P], k.ident[:, :])
        return t
    products(nc, name, NT, produce, lambda eng, n, bank: copy(
        eng, dst[:, :, n * P:(n + 1) * P], bank[:, :].rearrange("p (c t) -> p c t", c=KD)))


def unturn(nc, k, name, src, dst):
    def produce(pe, n, bank):
        for c in range(KD):
            t = pe.transpose(bank[:, c * P:(c + 1) * P], src[:, c, n * P:(n + 1) * P], k.ident[:, :])
        return t
    products(nc, name, NT, produce, lambda eng, n, bank: copy(eng, dst[:, n, :], bank[:, :]))


def load(nc, name, pairs):
    with ExitStack() as ctx:
        landed = Mem(nc, ctx, name).sem("landed")
        with nc.Block() as block:
            @block.sync
            def _(sp):
                for out, in_ in pairs:
                    sp.dma_start(out, in_).then_inc(landed, 16)
                sp.wait_ge(landed, 16 * len(pairs))


def layernorm(nc, k, name, x, out, extra=None):
    with ExitStack() as ctx:
        m = Mem(nc, ctx, name)
        stats = m.sb("stats", [P, NT, 6])
        mv = m.sb("mv", [P, NT, 2])
        v = m.sb("v", [P, NT])
        r = m.sb("r", [P, NT])
        w = m.sb("w", [P, NT])
        steps, var, root = m.sem("steps"), m.sem("var"), m.sem("root")
        with nc.Block() as block:
            @block.vector
            def _(dve):
                c = Chain(dve, steps)
                for i in range(NT):
                    c.mark(dve.bn_stats(stats[:, i, :], x[:, i, :]))
                dve.wait_ge(steps, c.n)
                for i in range(NT):
                    c.mark(dve.bn_aggr(mv[:, i, :], stats[:, i, :]))
                dve.wait_ge(steps, c.n)
                dve.tensor_scalar(v[:, :], mv[:, :, 1], 1e-5, None, ALU.add).then_inc(var, 1)
                dve.wait_ge(root, 1)
                c.then(dve.reciprocal(r[:, :], r[:, :]))
                dve.wait_ge(var, 1)
                c.then(dve.tensor_tensor(w[:, :], r[:, :], r[:, :], ALU.mult))
                c.then(dve.tensor_tensor(w[:, :], w[:, :], v[:, :], ALU.mult))
                c.then(dve.tensor_scalar(w[:, :], w[:, :], -0.5, 1.5, ALU.mult, ALU.add))
                c.then(dve.tensor_tensor(r[:, :], r[:, :], w[:, :], ALU.mult))
                for i in range(NT):
                    c.mark(dve.tensor_scalar(out[:, i, :], x[:, i, :], mv[:, i, 0:1], r[:, i:i + 1], ALU.subtract, ALU.mult))
                if extra is not None:
                    dve.wait_ge(steps, c.n)
                    for n, (row, op) in enumerate(zip(extra, (ALU.mult, ALU.add))):
                        for i in range(NT):
                            c.mark(dve.tensor_tensor(out[:, i, :], out[:, i, :], row[:, :], op))
                        dve.wait_ge(steps, c.n)

            @block.scalar
            def _(act):
                act.wait_ge(var, 1)
                act.activation(r[:, :], v[:, :], ACT.Sqrt).then_inc(root, 1)


def softmax_rows(nc, name, x, rows, width, scale):
    with ExitStack() as ctx:
        m = Mem(nc, ctx, name)
        top = m.sb("top", [P, rows])
        total = m.sb("total", [P, rows])
        steps, raised, summed = m.sem("steps"), m.sem("raised"), m.sem("summed")
        with nc.Block() as block:
            @block.vector
            def _(dve):
                c = Chain(dve, steps)
                c.then(dve.tensor_reduce(top[:, :], x[:, :, :], AX.X, ALU.max))
                dve.tensor_scalar(top[:, :], top[:, :], -1.0, None, ALU.mult).then_inc(raised, 1)
                for i in range(rows):
                    dve.wait_ge(summed, i + 1)
                    c.then(dve.reciprocal(total[:, i:i + 1], total[:, i:i + 1]))
                    c.mark(dve.tensor_scalar(x[:, i, :], x[:, i, :], total[:, i:i + 1], scale, ALU.mult, ALU.mult))

            @block.scalar
            def _(act):
                act.wait_ge(raised, 1)
                for i in range(rows):
                    act.activation(x[:, i, :], x[:, i, :], ACT.Exp, bias=top[:, i:i + 1],
                                   accum_out=total[:, i:i + 1]).then_inc(summed, 1)


def chunks(w):
    return w.rearrange("(c p) n -> p c n", p=P)


def tile_terms(lhsT, rhs, n, kd=KD):
    return [(lhsT[:, c, n * P:(n + 1) * P], rhs[:, c, :]) for c in range(kd)]


def layer0_gnn(nc, k, a, x, xn, xt, sum_out):
    with ExitStack() as ctx:
        m = Mem(nc, ctx, "gnn0")
        adj = m.sb("adj", [P, NT, N])
        rs = m.sb("rs", [P, NT])
        adjacency(nc, k, adj, rs)
        w = m.sb("w", [P, KD, D])
        b = m.sb("b", [1, D])
        dw = m.sb("dw", [P, 4])
        cur = [m.sb(f"cur{i}", [P, NT, D]) for i in range(2)]
        acc = m.sb("acc", [P, NT, D])
        load(nc, "gnn0_load", [(w[:, :, :], chunks(a["L0_gnn_W"])), (b[:, :], a["L0_gnn_b"].rearrange("(a n) -> a n", a=1)),
                               (dw[:, :], a["L0_gnn_diffusion_weights"].rearrange("(a n) -> a n", a=1).broadcast_to([P, 4]))])
        products(nc, "gnn0_h", NT,
                 lambda pe, n, bank: accumulate(pe, bank[:, :], tile_terms(xt, w, n) + [(k.ones[0:1, :], b[:, :])]),
                 lambda eng, n, bank: copy(eng, cur[0][:, n, :], bank[:, :]))
        mixed, summed = m.sem("mixed"), m.sem("summed")
        for step in range(3):
            src, dst = cur[step % 2], cur[(step + 1) % 2]
            products(nc, f"gnn0_s{step}", NT,
                     lambda pe, n, bank: accumulate(pe, bank[:, :], tile_terms(adj, src, n, NT)),
                     lambda eng, n, bank: eng.activation(dst[:, n, :], bank[:, :], ACT.Copy, scale=rs[:, n:n + 1])
                     if isinstance(eng, bass.BassScalarEngine)
                     else eng.tensor_scalar(dst[:, n, :], bank[:, :], rs[:, n:n + 1], None, ALU.mult))
            with nc.Block() as block:
                @block.vector
                def _(dve):
                    flat = lambda z: z[:, :, :].rearrange("p t d -> p (t d)")
                    if step == 0:
                        dve.tensor_scalar(flat(acc), flat(src), dw[:, 0:1], None, ALU.mult).then_inc(summed, 1)
                        dve.wait_ge(summed, 1)
                    dve.scalar_tensor_tensor(flat(acc), flat(dst), dw[:, step + 1:step + 2], flat(acc), ALU.mult,
                                             ALU.add).then_inc(summed, 1)
                    if step == 2:
                        dve.wait_ge(summed, 4)
                        dve.scalar_tensor_tensor(flat(sum_out), flat(acc), 0.0, flat(x), ALU.max, ALU.add).then_inc(summed, 1)


def layer0_mix(nc, k, a, xn, xt, x1):
    with ExitStack() as ctx:
        m = Mem(nc, ctx, "mix0")
        w = m.sb("w", [P, 5, KD, D])
        q = m.sb("q", [P, NT, D])
        qt = m.sb("qt", [P, KD, N])
        kt = m.sb("kt", [P, KD, N])
        kk = m.sb("kk", [P, NT, D])
        v = m.sb("v", [P, NT, D])
        context = q[:, 0:KD, :]
        names = ("Wq", "Wk", "Wv", "W1", "W2")
        load(nc, "mix0_load", [(w[:, i, :, :], chunks(a[f"L0_mix_{s}"])) for i, s in enumerate(names)])
        wk = w[:, 1, :, :]
        products(nc, "mix0_q", NT, lambda pe, n, bank: accumulate(pe, bank[:, :], tile_terms(xt, w[:, 0, :, :], n)),
                 lambda eng, n, bank: copy(eng, q[:, n, :], bank[:, :]))

        def halves(out, lhs, rhs, name, extra=None):
            products(nc, name, 2 * KD,
                     lambda pe, n, bank: accumulate(pe, bank[:, :], [
                         (lhs[:, c, (n // 2) * P:(n // 2 + 1) * P], rhs[:, c, (n % 2) * D:(n % 2 + 1) * D]) for c in range(KD)]),
                     lambda eng, n, bank: copy(eng, out[:, n // 2, (n % 2) * D:(n % 2 + 1) * D], bank[:, :])
                     if extra is None else eng.tensor_tensor(
                         out[:, n // 2, (n % 2) * D:(n % 2 + 1) * D], bank[:, :],
                         extra[:, n // 2, (n % 2) * D:(n % 2 + 1) * D], ALU.add), scalar=extra is None)
        halves(kt, wk, xt, "mix0_k")
        products(nc, "mix0_v", NT, lambda pe, n, bank: accumulate(pe, bank[:, :], tile_terms(xt, w[:, 2, :, :], n)),
                 lambda eng, n, bank: copy(eng, v[:, n, :], bank[:, :]))
        softmax_rows(nc, "mix0_sq", q, NT, D, float(D) ** -0.5)
        softmax_rows(nc, "mix0_sk", kt, KD, N, 1.0)
        unturn(nc, k, "mix0_kk", kt, kk)
        turn(nc, k, "mix0_qt", q, qt)
        products(nc, "mix0_c", KD, lambda pe, n, bank: accumulate(pe, bank[:, :], [
            (kk[:, i, n * P:(n + 1) * P], v[:, i, :]) for i in range(NT)]),
                 lambda eng, n, bank: copy(eng, context[:, n, :], bank[:, :]))
        yt, zt = kt, qt
        halves(yt, context, qt, "mix0_a", extra=xt)
        halves(zt, w[:, 3, :, :], yt, "mix0_1")
        products(nc, "mix0_2", NT,
                 lambda pe, n, bank: (accumulate(pe, bank[:, :], tile_terms(zt, w[:, 4, :, :], n)), [
                     pe.matmul(bank[:, c * P:(c + 1) * P], yt[:, c, n * P:(n + 1) * P], k.ident[:, :], start=False,
                               stop=(c == KD - 1), skip_group_check=True) for c in range(KD)][-1])[1],
                 lambda eng, n, bank: eng.tensor_tensor(x1[:, n, :], bank[:, :], x1[:, n, :], ALU.add), scalar=False)


NE = 8
CAP = 256
FF = 1024
CT = CAP // P


def expert_choice(nc, k, a, xt, scores_t, picks, chosen_i, gate):
    with ExitStack() as ctx:
        m = Mem(nc, ctx, "pick")
        wg = m.sb("wg", [P, KD, NE])
        s = m.sb("s", [P, NT, NE])
        w = m.sb("w", [P, NT, NE])
        top = m.sb("top", [P, NT])
        st = m.sb("st", [NE, N])
        sb = m.sb("sb", [P, NE, N])
        junk = m.sb("junk", [P, N], BF16)
        spare = m.sb("spare", [P, 1])
        gt = m.sb("gt", [P, NT, NE])
        ge = m.sb("ge", [P, NT, NE])
        tie = m.sb("tie", [P, NT, NE])
        token = m.sb("token", [P, NT])
        slot_i = m.sb("slot_i", [P, NT * NE], I32)
        recs = m.sb("recs", [P, NT * NE, 2])
        idx = m.sb("idx", [P, 2, 8], I32)
        buf = m.sb("buf", [P, 2, 8, 2])
        back = m.sb("back", [P, NE, CT, 2])
        lg = m.ps("lg", [P, D])
        tp = m.ps("tp", [NE, N])
        loaded, logits, steps, exped, shifted, norm, turned = (m.sem(x) for x in (
            "loaded", "logits", "steps", "exped", "shifted", "norm", "turned"))
        copied, stored, spread, ranked, ready, staged, fetched, out = (m.sem(x) for x in (
            "copied", "stored", "spread", "ranked", "ready", "staged", "fetched", "out"))
        sent = [m.sem(f"sent{i}") for i in range(2)]
        with nc.Block() as block:
            @block.sync
            def _(sp):
                sp.dma_start(wg[:, :, :], chunks(a["L0_ffn_Wg"])).then_inc(loaded, 16)
                sp.wait_ge(copied, 2)
                sp.dma_start(scores_t, st[:, :]).then_inc(stored, 16)
                sp.wait_ge(stored, 16)
                for e in range(NE):
                    sp.dma_start(sb[:, e, :], scores_t[e:e + 1, :].broadcast_to([P, N])).then_inc(spread, 16)

            @block.tensor
            def _(pe):
                pe.wait_ge(loaded, 16)
                for i in range(NT):
                    t = accumulate(pe, lg[:, i * NE:(i + 1) * NE], [(xt[:, c, i * P:(i + 1) * P], wg[:, c, :]) for c in range(KD)])
                t.then_inc(logits, 1)
                pe.wait_ge(norm, 1)
                for i in range(NT):
                    t = pe.transpose(tp[:, i * P:(i + 1) * P], s[:, i, :], k.ident[:, :])
                t.then_inc(turned, 1)

            @block.scalar
            def _(act):
                act.wait_ge(shifted, 1)
                act.activation(w[:, :, :], s[:, :, :], ACT.Exp).then_inc(exped, 1)

            @block.vector
            def _(dve):
                c = Chain(dve, steps)
                wide = [P, NT, NE]
                dve.wait_ge(logits, 1)
                c.then(dve.tensor_copy(s[:, :, :].rearrange("p t e -> p (t e)"), lg[:, 0:NT * NE]))
                c.then(dve.tensor_reduce(top[:, :], s[:, :, :], AX.X, ALU.max))
                dve.tensor_tensor(s[:, :, :], s[:, :, :], top[:, :].unsqueeze(2).broadcast_to(wide), ALU.subtract).then_inc(shifted, 1)
                dve.wait_ge(exped, 1)
                c.then(dve.tensor_reduce(top[:, :], w[:, :, :], AX.X, ALU.add))
                c.then(dve.reciprocal(top[:, :], top[:, :]))
                dve.tensor_tensor(s[:, :, :], w[:, :, :], top[:, :].unsqueeze(2).broadcast_to(wide), ALU.mult).then_inc(norm, 1)
                dve.wait_ge(turned, 1)
                for h in range(2):
                    dve.tensor_copy(st[:, h * D:(h + 1) * D], tp[:, h * D:(h + 1) * D]).then_inc(copied, 1)
                c.mark(dve.memset(ge[:, 0, :], 0.0))
                c.mark(dve.memset(junk[:, :], 0.0))
                dve.wait_ge(norm, 1)
                for i in range(NT):
                    c.mark(dve.tensor_scalar(token[:, i:i + 1], k.lane[:, :], float(i * P), None, ALU.add))
                dve.wait_ge(steps, c.n)
                dve.wait_ge(spread, 16 * NE)
                with dve.Fori(0, NE) as e:
                    for i in range(NT):
                        mine = s[:, i, bass.ds(e, 1)]
                        lo, hi = i * P, (i + 1) * P
                        row = lambda x, n: sb[:, :, :].rearrange("p e n -> p (e n)")[:, bass.ds(e * N + x, n)]
                        if i:
                            dve.tensor_scalar(junk[:, 0:lo], row(0, lo), mine, 0.0, ALU.is_ge, ALU.add,
                                              accum_out=ge[:, i, bass.ds(e, 1)]).then_inc(ranked, 1)
                        else:
                            dve.tensor_copy(spare[:, :], k.lane[:, :]).then_inc(ranked, 1)
                        dve.tensor_scalar(junk[:, lo:N], row(lo, N - lo), mine, 0.0, ALU.is_gt, ALU.add,
                                          accum_out=gt[:, i, bass.ds(e, 1)]).then_inc(ranked, 1)
                        dve.wait_ge(ranked, 3 * NT * e + (3 * i + 2))
                        dve.scalar_tensor_tensor(junk[:, lo:hi], row(lo, P), mine, k.later[:, :], ALU.is_equal, ALU.mult,
                                                 accum_out=tie[:, i, bass.ds(e, 1)]).then_inc(ranked, 1)
                        dve.wait_ge(ranked, 3 * NT * e + (3 * i + 3))
                c.then(dve.tensor_tensor(gt[:, :, :], gt[:, :, :], ge[:, :, :], ALU.add))
                c.then(dve.tensor_tensor(gt[:, :, :], gt[:, :, :], tie[:, :, :], ALU.add))
                c.then(dve.tensor_scalar(w[:, 0, :], k.iotaf[:, 0:NE], float(N), None, ALU.mult))
                c.then(dve.tensor_tensor(gt[:, :, :], gt[:, :, :], w[:, 0:1, :].broadcast_to(wide), ALU.add))
                c.mark(dve.tensor_copy(slot_i[:, :], gt[:, :, :].rearrange("p t e -> p (t e)")))
                c.mark(dve.tensor_copy(recs[:, :, 0].rearrange("p (t e) -> p t e", t=NT), token[:, :].unsqueeze(2).broadcast_to(wide)))
                c.mark(dve.tensor_copy(recs[:, :, 1], s[:, :, :].rearrange("p t e -> p (t e)")))
                dve.wait_ge(steps, c.n)
                dve.sem_inc(ready, 1)

            @block.gpsimd
            def _(pool):
                pool.wait_ge(ready, 1)
                scatter(pool, picks, slot_i, recs, NT * NE, idx, buf, staged, sent, ready)
        with nc.Block() as block:
            @block.sync
            def _(sp):
                for t in range(CT):
                    sp.dma_start(back[:, :, t, :], picks.rearrange("(e t p) c -> p e t c", e=NE, p=P)[:, :, t, :]).then_inc(fetched, 16)

            @block.vector
            def _(dve):
                dve.wait_ge(fetched, 16 * CT)
                dve.tensor_copy(chosen_i[:, :, :], back[:, :, :, 0]).then_inc(out, 1)
                dve.tensor_copy(gate[:, :, :], back[:, :, :, 1]).then_inc(out, 1)


def experts(nc, k, a, rows, total, chosen_i, gate):
    with ExitStack() as ctx:
        m = Mem(nc, ctx, "moe")
        w1 = m.sb("w1", [P, 2, KD, FF])
        w2 = m.sb("w2", [P, 2, FF // P, D])
        b1 = m.sb("b1", [P, NE, FF // P])
        b2 = m.sb("b2", [1, 2, D])
        ex = m.sb("ex", [P, 2, CT, D])
        ext = m.sb("ext", [P, KD, CAP])
        hid = m.sb("hid", [P, FF // P, CAP])
        y = m.sb("y", [P, 2, CT, D])
        R = 4
        tb = [m.ps(f"tb{i}", [P, D]) for i in range(CT)]
        hb = [m.ps(f"hb{i}", [P, D]) for i in range(R)]
        ob = [m.ps(f"ob{i}", [P, D]) for i in range(CT)]
        w_in = [m.sem(f"w_in{i}") for i in range(2)]
        got = [m.sem(f"got{i}") for i in range(2)]
        added = [m.sem(f"added{i}") for i in range(CT)]
        b_in, y_free, turned, laid, hidden, act_done, summed, weighed = (m.sem(x) for x in (
            "b_in", "y_free", "turned", "laid", "hidden", "act_done", "summed", "weighed"))
        FT = FF // P
        with nc.Block() as block:
            @block.sync
            def _(sp):
                def weights(e, b):
                    sp.dma_start(w1[:, b, :, :], a["L0_ffn_W1"][bass.ds(e, 1), :, :].rearrange("a (c p) f -> p (a c) f", p=P)).then_inc(w_in[b], 16)
                    sp.dma_start(w2[:, b, :, :], a["L0_ffn_W2"][bass.ds(e, 1), :, :].rearrange("a (c p) f -> p (a c) f", p=P)).then_inc(w_in[b], 16)
                    sp.dma_start(b2[:, b, :], a["L0_ffn_b2"][bass.ds(e, 1), :]).then_inc(w_in[b], 16)
                sp.dma_start(b1[:, :, :], a["L0_ffn_b1"]).then_inc(b_in, 16)
                for b in range(2):
                    weights(b, b)
                with sp.Fori(1, NE // 2) as t:
                    for b in range(2):
                        sp.wait_ge(summed, CT * (2 * t) + (CT * (b - 1) + 1))
                        weights(2 * t + b, b)

            @block.gpsimd
            def _(pool):
                def gather(e):
                    if e >= 2:
                        pool.wait_ge(turned, CT * (e - 1))
                    for t in range(CT):
                        pool.indirect_dma_start(out=ex[:, e % 2, t, :], out_offset=None, in_=rows,
                                                in_offset=bass.IndirectOffsetOnAxis(ap=chosen_i[:, e, t:t + 1], axis=0)).then_inc(got[e % 2], 16)
                pool.sem_inc(y_free, 2)
                gather(0)
                for e in range(NE):
                    if e + 1 < NE:
                        gather(e + 1)
                    for t in range(CT):
                        pool.wait_ge(weighed, CT * e + t + 1 + CT)
                        if e and t == 0:
                            for o in range(CT):
                                pool.wait_ge(added[o], 16 * e)
                            pool.sem_inc(y_free, 1)
                        pool.indirect_dma_start(out=total, out_offset=bass.IndirectOffsetOnAxis(ap=chosen_i[:, e, t:t + 1], axis=0),
                                                in_=y[:, e % 2, t, :], in_offset=None, compute_op=ALU.add).then_inc(added[t], 16)
                for o in range(CT):
                    pool.wait_ge(added[o], 16 * NE)

            @block.tensor
            def _(pe):
                pe.sem_inc(hidden, 1)
                pe.sem_inc(summed, 1)
                with pe.Fori(0, NE // 2) as tt:
                    for b in range(2):
                        e = 2 * tt + b
                        pe.wait_ge(got[b], 16 * CT * (tt + 1))
                        pe.wait_ge(laid, CT * e + CT)
                        for t in range(CT):
                            for c in range(KD):
                                i = pe.transpose(tb[t][:, c * P:(c + 1) * P], ex[:, b, t, c * P:(c + 1) * P], k.ident[:, :])
                            i.then_inc(turned, 1)
                        pe.wait_ge(w_in[b], 48 * (tt + 1))
                        pe.wait_ge(laid, CT * e + 2 * CT)
                        for f in range(FT):
                            pe.wait_ge(act_done, FT * e + (f + 1))
                            accumulate(pe, hb[f % R][:, 0:CAP],
                                       [(w1[:, b, c, f * P:(f + 1) * P], ext[:, c, :]) for c in range(KD)]).then_inc(hidden, 1)
                        pe.wait_ge(act_done, FT * e + (FT + R))
                        for t in range(CT):
                            pe.wait_ge(weighed, CT * e + t + 1)
                            pe.matmul(ob[t][:, :], k.ones[0:1, :], b2[0:1, b, :], start=True, stop=False)
                            for f in range(FT):
                                i = pe.matmul(ob[t][:, :], hid[:, f, t * P:(t + 1) * P], w2[:, b, f, :], start=False, stop=(f == FT - 1))
                            i.then_inc(summed, 1)

            @block.vector
            def _(dve):
                dve.sem_inc(laid, CT)
                dve.sem_inc(weighed, CT)
                with dve.Fori(0, NE // 2) as tt:
                    for b in range(2):
                        e = 2 * tt + b
                        for t in range(CT):
                            dve.wait_ge(turned, CT * e + t + 1)
                            if t == 0:
                                dve.wait_ge(hidden, FT * e + 1)
                            dve.tensor_copy(ext[:, :, t * P:(t + 1) * P], tb[t][:, :].rearrange("p (c t) -> p c t", c=KD)).then_inc(laid, 1)
                        for t in range(CT):
                            dve.wait_ge(summed, CT * e + t + 2)
                            dve.wait_ge(y_free, e + 1)
                            dve.tensor_scalar(y[:, b, t, :], ob[t][:, :], gate[:, bass.ds(e, 1), t:t + 1].rearrange("p a b -> p (a b)"), None, ALU.mult).then_inc(weighed, 1)

            @block.scalar
            def _(act):
                act.wait_ge(b_in, 16)
                act.sem_inc(act_done, R)
                with act.Fori(0, NE // 2) as tt:
                    for b in range(2):
                        e = 2 * tt + b
                        for f in range(FT):
                            act.wait_ge(hidden, FT * e + f + 2)
                            if f == 0:
                                act.wait_ge(summed, CT * e + 1)
                            act.activation(hid[:, f, :], hb[f % R][:, 0:CAP], ACT.Gelu,
                                           bias=b1[:, bass.ds(e, 1), f:f + 1].rearrange("p a b -> p (a b)")).then_inc(act_done, 1)


def store(nc, name, pairs):
    load(nc, name, pairs)


def layer0_ffn(nc, k, a, x1, xn, xt):
    with ExitStack() as ctx:
        m = Mem(nc, ctx, "ffn0")
        chosen_i = m.sb("chosen_i", [P, NE, CT], I32)
        gate = m.sb("gate", [P, NE, CT])
        rows = nc.dram_tensor("expert_rows", (N, D), F32).ap()
        total = nc.dram_tensor("expert_total", (N, D), F32).ap()
        scores_t = nc.dram_tensor("expert_scores", (NE, N), F32).ap()
        picks = nc.dram_tensor("expert_picks", (NE * N, 2), F32).ap()
        layernorm(nc, k, "ln1", x1, xn)
        store(nc, "ffn0_store", [(chunks(rows), xn[:, :, :]), (chunks(total), x1[:, :, :])])
        turn(nc, k, "turn1", xn, xt)
        expert_choice(nc, k, a, xt, scores_t, picks, chosen_i, gate)
        experts(nc, k, a, rows, total, chosen_i, gate)
        load(nc, "ffn0_load", [(x1[:, :, :], chunks(total))])


LOT = 4
LOTS = NB // LOT


def gat_gather(pool, tables, indices, idx, bufs, staged, got, free, per):
    def stage(n, b):
        for j, col in enumerate(indices):
            pool.tensor_copy(idx[:, b, j, :], col[:, bass.ds(LOT * n, LOT)]).then_inc(staged, 1)

    def fetch(b):
        for j, table in enumerate(tables):
            for u in range(LOT):
                pool.indirect_dma_start(out=bufs[j][:, b, u, :], out_offset=None, in_=table,
                                        in_offset=bass.IndirectOffsetOnAxis(ap=idx[:, b, j, u:u + 1], axis=0)).then_inc(got[b], 16)
    k = len(tables)
    stage(0, 0)
    pool.wait_ge(staged, k)
    stage(1, 1)
    fetch(0)
    with pool.Fori(0, LOTS // 2 - 1) as t:
        for b in range(2):
            n = 2 * t + b
            pool.wait_ge(staged, k * n + 2 * k)
            pool.wait_ge(got[b], 16 * k * LOT * (t + 1))
            pool.wait_ge(free, per * n + 2 * per)
            stage(n + 2, b)
            fetch(1 - b)
    pool.wait_ge(staged, k * LOTS)
    pool.wait_ge(free, per * LOTS)
    fetch(1)


def gat_scores(nc, k, a, xl_t, xr_t, alpha):
    with ExitStack() as ctx:
        m = Mem(nc, ctx, "score")
        left = m.sb("left", [P, 2, LOT, D])
        right = m.sb("right", [P, 2, LOT, D])
        att = m.sb("att", [P, D])
        idx = m.sb("idx", [P, 2, 2, LOT], I32)
        loaded, staged, free, steps = (m.sem(x) for x in ("loaded", "staged", "free", "steps"))
        got = [m.sem(f"got{i}") for i in range(2)]
        with nc.Block() as block:
            @block.sync
            def _(sp):
                sp.dma_start(att[:, :], a["L1_gnn_att"].rearrange("(a h) c -> a (h c)", a=1).broadcast_to([P, D])).then_inc(loaded, 16)

            @block.gpsimd
            def _(pool):
                gat_gather(pool, [xl_t, xr_t], [k.src_i, k.dst_i], idx, [left, right], staged, got, free, 1)

            @block.vector
            def _(dve):
                dve.sem_inc(free, 2)
                dve.wait_ge(loaded, 16)
                with dve.Fori(0, LOTS // 2) as t:
                    for b in range(2):
                        n = 2 * t + b
                        l = left[:, b, :, :].rearrange("p u d -> p (u d)")
                        r = right[:, b, :, :].rearrange("p u d -> p (u d)")
                        dve.wait_ge(got[b], 16 * 2 * LOT * (t + 1))
                        dve.tensor_tensor(l, l, r, ALU.add).then_inc(steps, 1)
                        dve.wait_ge(steps, 3 * n + 1)
                        dve.scalar_tensor_tensor(r, l, 0.2, l, ALU.mult, ALU.max).then_inc(steps, 1)
                        dve.wait_ge(steps, 3 * n + 2)
                        dve.tensor_tensor(left[:, b, :, :], right[:, b, :, :], att[:, :].unsqueeze(1).broadcast_to([P, LOT, D]),
                                          ALU.mult).then_inc(steps, 1)
                        dve.wait_ge(steps, 3 * n + 3)
                        dve.tensor_reduce(alpha[:, bass.ds(n * (LOT * H8), LOT * H8)],
                                          l.rearrange("p (q c) -> p q c", c=HC), AX.X, ALU.add).then_inc(free, 1)


def segment_softmax(nc, k, keys_t, alpha):
    with ExitStack() as ctx:
        m = Mem(nc, ctx, "seg")
        raw = m.sb("raw", [P, 3, SL])
        same_prev = m.sb("same_prev", [P, SL])
        same_next = m.sb("same_next", [P, SL])
        brk = m.sb("brk", [P, SL])
        last = m.sb("last", [P, SL])
        al = m.sb("al", [P, SL])
        run = m.sb("run", [P, SL])
        x = m.sb("x", [P, SL])
        fac = m.sb("fac", [P, 1])
        ends = m.sb("ends", [1, 2, P])
        st = m.sb("st", [1, P])
        carry_row = m.sb("carry_row", [1, P])
        carry = m.sb("carry", [P, 1])
        bank = [m.ps(f"bank{i}", [P, D]) for i in range(2)]
        rows = m.ps("rows", [1, D])
        col = m.ps("col", [P, D])
        loaded, steps, turned, brought, rowed, summed, colled, shifted, exped = (m.sem(x) for x in (
            "loaded", "steps", "turned", "brought", "rowed", "summed", "colled", "shifted", "exped"))
        lanes = alpha[:, :].rearrange("p (s i h) -> p i h s", s=SEG, i=BS)
        with nc.Block() as block:
            @block.sync
            def _(sp):
                for o in range(3):
                    v = keys_t[o:EP + o].rearrange("(s n) -> s n", s=SEG)
                    for h in range(H8):
                        sp.dma_start(raw[h * SEG:(h + 1) * SEG, o, :], v).then_inc(loaded, 16)

            @block.tensor
            def _(pe):
                pe.wait_ge(steps, 1)
                for i in range(BS):
                    if i >= 2:
                        pe.wait_ge(brought, i - 1)
                    pe.transpose(bank[i % 2][:, 0:P], x[:, i * P:(i + 1) * P], k.ident[:, :]).then_inc(turned, 1)
                for r in range(4):
                    pe.wait_ge(rowed, 3 * r + 1)
                    pe.transpose(rows[0:1, 0:P], run[:, SL - 1:SL] if r % 2 == 0 else run[:, 0:1], k.ident[:, :])
                    pe.transpose(rows[0:1, P:2 * P], fac[:, :], k.ident[:, :]).then_inc(summed, 1)
                    pe.wait_ge(rowed, 3 * r + 2)
                    pe.transpose(col[:, 0:1], carry_row[0:1, :], k.ident[0:1, 0:1]).then_inc(colled, 1)

            @block.scalar
            def _(act):
                act.wait_ge(shifted, 1)
                act.activation(al[:, :], al[:, :], ACT.Exp).then_inc(exped, 1)

            @block.vector
            def _(dve):
                c = Chain(dve, steps)
                c.mark(dve.tensor_copy(x[:, :].rearrange("p (i h s) -> p i h s", i=BS, h=H8), lanes))
                for i in range(BS):
                    dve.wait_ge(turned, i + 1)
                    dve.tensor_copy(al[:, i * P:(i + 1) * P], bank[i % 2][:, 0:P]).then_inc(brought, 1)
                dve.wait_ge(loaded, 16 * 3 * H8)
                v = [raw[:, o, :] for o in range(3)]
                c.mark(dve.tensor_tensor(same_prev[:, :], v[1], v[0], ALU.is_equal))
                c.then(dve.tensor_tensor(same_next[:, :], v[1], v[2], ALU.is_equal))
                c.mark(dve.tensor_scalar(brk[:, :], same_prev[:, :], -1.0, BIG, ALU.add, ALU.mult))
                c.then(dve.tensor_scalar(last[:, :], same_next[:, :], -1.0, 1.0, ALU.mult, ALU.add))
                dve.wait_ge(brought, BS)

                def recurrence(r, keepers, add, ops, start, back):
                    way = slice(None, None, -1) if back else slice(None)
                    c.then(dve.tensor_tensor_scan(run[:, way], keepers[:, way], add[:, way], start, *ops))
                    dve.tensor_reduce(fac[:, :], keepers[:, :], AX.X, ALU.min).then_inc(rowed, 1)
                    dve.wait_ge(summed, r + 1)
                    c.then(dve.tensor_copy(ends[:, :, :].rearrange("a b p -> a (b p)"), rows[0:1, 0:2 * P]))
                    first, over = (SEG - 1, slice(0, P - 1)) if back else (0, slice(1, P))
                    c.then(dve.memset(ends[0:1, 1, first::SEG], -BIG if ops[0] == ALU.add else 0.0))
                    c.then(dve.tensor_tensor_scan(st[0:1, way], ends[0:1, 1, way], ends[0:1, 0, way], start, *ops))
                    c.then(dve.tensor_copy(carry_row[0:1, over], st[0:1, 1:P] if back else st[0:1, 0:P - 1]))
                    dve.memset(carry_row[0:1, first::SEG], start).then_inc(rowed, 1)
                    dve.wait_ge(colled, r + 1)
                    dve.tensor_copy(carry[:, :], col[:, 0:1]).then_inc(rowed, 1)
                    dve.wait_ge(rowed, 3 * r + 3)
                    c.then(dve.tensor_tensor_scan(run[:, way], keepers[:, way], add[:, way], carry[:, :], *ops))

                linear = (ALU.mult, ALU.add)
                recurrence(0, brk, al, (ALU.add, ALU.max), -BIG, False)
                c.then(dve.tensor_tensor(x[:, :], last[:, :], run[:, :], ALU.mult))
                recurrence(1, same_next, x, linear, 0.0, True)
                dve.tensor_tensor(al[:, :], al[:, :], run[:, :], ALU.subtract).then_inc(shifted, 1)
                dve.wait_ge(exped, 1)
                recurrence(2, same_prev, al, linear, 0.0, False)
                c.then(dve.tensor_tensor(x[:, :], last[:, :], run[:, :], ALU.mult))
                recurrence(3, same_next, x, linear, 0.0, True)
                c.then(dve.tensor_scalar(run[:, :], run[:, :], 1e-16, None, ALU.max))
                c.then(dve.reciprocal(run[:, :], run[:, :]))
                c.then(dve.tensor_tensor(al[:, :], al[:, :], run[:, :], ALU.mult))
        turned, brought = m.sem("turned_b"), m.sem("brought_b")
        with nc.Block() as block:
            @block.tensor
            def _(pe):
                for i in range(BS):
                    if i >= 2:
                        pe.wait_ge(brought, i - 1)
                    pe.transpose(bank[i % 2][:, 0:P], al[:, i * P:(i + 1) * P], k.ident[:, :]).then_inc(turned, 1)

            @block.vector
            def _(dve):
                for i in range(BS):
                    dve.wait_ge(turned, i + 1)
                    dve.tensor_copy(lanes[:, i, :, :], bank[i % 2][:, 0:P].rearrange("p (h s) -> p h s", h=H8)).then_inc(brought, 1)


def gat_sum(nc, k, a, xl_t, alpha, xn, out):
    with ExitStack() as ctx:
        m = Mem(nc, ctx, "agg")
        left = m.sb("left", [P, 2, LOT, D])
        wx = m.sb("wx", [P, 2, LOT, D])
        to = m.sb("to", [P, 2, LOT, P])
        idx = m.sb("idx", [P, 2, 1, LOT], I32)
        zb = m.sb("zb", [P, D], BF16)
        bias = m.sb("bias", [P, D])
        neg = m.sb("neg", [P, 2, D])
        pos = m.sb("pos", [P, 2, D])
        acc = m.ps("acc", [P, NG * D])
        loaded, staged, free, ready, used, zeroed = (m.sem(x) for x in ("loaded", "staged", "free", "ready", "used", "zeroed"))
        steps, low, exped = (m.sem(x) for x in ("steps", "low", "exped"))
        got = [m.sem(f"got{i}") for i in range(2)]
        with nc.Block() as block:
            @block.sync
            def _(sp):
                sp.dma_start(bias[:, :], a["L1_gnn_bias"].rearrange("(a n) -> a n", a=1).broadcast_to([P, D])).then_inc(loaded, 16)

            @block.gpsimd
            def _(pool):
                gat_gather(pool, [xl_t], [k.src_i], idx, [left], staged, got, free, 1)

            @block.vector
            def _(dve):
                dve.memset(zb[:, :], 0.0).then_inc(zeroed, 1)
                dve.sem_inc(free, 2)
                with dve.Fori(0, LOTS // 2) as t:
                    for b in range(2):
                        n = 2 * t + b
                        dve.wait_ge(used, n + 1)
                        for u in range(LOT):
                            dve.tensor_scalar(to[:, b, u, :], k.iotaf[:, 0:P], k.local[:, bass.ds(LOT * n + u, 1)], None,
                                              ALU.is_equal).then_inc(ready, 1)
                        dve.wait_ge(got[b], 16 * LOT * (t + 1))
                        dve.tensor_tensor(wx[:, b, :, :].rearrange("p u (h c) -> p (u h) c", c=HC),
                                          left[:, b, :, :].rearrange("p u (h c) -> p (u h) c", c=HC),
                                          alpha[:, bass.ds(n * (LOT * H8), LOT * H8)].unsqueeze(2).broadcast_to([P, LOT * H8, HC]),
                                          ALU.mult).then_inc(free, 1)

            @block.tensor
            def _(pe):
                pe.wait_ge(zeroed, 1)
                pe.sem_inc(used, 2)
                for g in range(NG):
                    pe.matmul(acc[:, g * D:(g + 1) * D], k.ones_b[:, :], zb[:, :], start=True, stop=False, skip_group_check=True)
                with pe.Fori(0, LOTS // 2) as t:
                    for b in range(2):
                        n = 2 * t + b
                        groups = block_groups(nc, k, LOT * n, LOT)
                        for u in range(LOT):
                            g = groups[u]
                            if u == 0:
                                pe.wait_ge(ready, LOT * n + LOT)
                                pe.wait_ge(free, n + 3)
                            i = pe.matmul(acc[:, bass.ds(g, D)], to[:, b, u, :], wx[:, b, u, :], start=False, stop=False,
                                          skip_group_check=True)
                        i.then_inc(used, 1)
        with nc.Block() as block:
            @block.vector
            def _(dve):
                c = Chain(dve, steps)
                dve.wait_ge(loaded, 16)
                for g in range(NG):
                    b = g % 2
                    c.then(dve.tensor_tensor(pos[:, b, :], acc[:, g * D:(g + 1) * D], bias[:, :], ALU.add))
                    dve.tensor_scalar(neg[:, b, :], pos[:, b, :], 0.0, None, ALU.min).then_inc(low, 1)
                    c.then(dve.tensor_scalar(pos[:, b, :], pos[:, b, :], 0.0, -1.0, ALU.max, ALU.add))
                    c.then(dve.tensor_tensor(pos[:, b, :], pos[:, b, :], xn[:, g, :], ALU.add))
                    c.then(dve.tensor_tensor(pos[:, b, :], pos[:, b, :], out[:, g, :], ALU.add))
                    dve.wait_ge(exped, g + 1)
                    c.then(dve.tensor_tensor(out[:, g, :], pos[:, b, :], neg[:, b, :], ALU.add))

            @block.scalar
            def _(act):
                for g in range(NG):
                    act.wait_ge(low, g + 1)
                    act.activation(neg[:, g % 2, :], neg[:, g % 2, :], ACT.Exp).then_inc(exped, 1)


def layer1_gnn(nc, k, a, keys_t, xn, xt, x2):
    with ExitStack() as ctx:
        m = Mem(nc, ctx, "gat")
        alpha = m.sb("alpha", [P, NB * H8])
        xl_t = nc.dram_tensor("gat_left", (N, D), F32).ap()
        xr_t = nc.dram_tensor("gat_right", (N, D), F32).ap()
        with ExitStack() as inner:
            mi = Mem(nc, inner, "gatp")
            w = mi.sb("w", [P, 2, KD, D])
            y = mi.sb("y", [P, 2, NT, D])
            load(nc, "gat_load", [(w[:, 0, :, :], chunks(a["L1_gnn_W_l"])), (w[:, 1, :, :], chunks(a["L1_gnn_W_r"]))])
            products(nc, "gat_p", 2 * NT,
                     lambda pe, n, bank: accumulate(pe, bank[:, :], tile_terms(xt, w[:, n // NT, :, :], n % NT)),
                     lambda eng, n, bank: copy(eng, y[:, n // NT, n % NT, :], bank[:, :]))
            store(nc, "gat_store", [(chunks(xl_t), y[:, 0, :, :]), (chunks(xr_t), y[:, 1, :, :])])
        gat_scores(nc, k, a, xl_t, xr_t, alpha)
        segment_softmax(nc, k, keys_t, alpha)
        gat_sum(nc, k, a, xl_t, alpha, xn, x2)


NH = 16
HD = D // NH


def layer1_mix(nc, k, a, xn, xt, x2):
    with ExitStack() as ctx:
        m = Mem(nc, ctx, "mix1")
        w = m.sb("w", [P, 4, KD, D])
        bias = m.sb("bias", [1, D])
        qt = m.sb("qt", [P, KD, N])
        kk = m.sb("kk", [P, NT, D])
        v = m.sb("v", [P, NT, D + 1])
        kv = m.sb("kv", [P, KD, P + 4])
        blocks = m.sb("blocks", [P, P])
        pr = m.sb("pr", [P, NT, D])
        den = m.sb("den", [P, NT, NH])
        pt = qt
        load(nc, "mix1_load", [(w[:, i, :, :], chunks(a["L1_mix_qkv_weight"])[:, :, i * D:(i + 1) * D]) for i in range(3)] +
             [(w[:, 3, :, :], chunks(a["L1_mix_proj_weight"])), (bias[:, :], a["L1_mix_proj_bias"].rearrange("(a n) -> a n", a=1))])
        relu = lambda eng, out, in_: (eng.activation(out, in_, ACT.Relu) if isinstance(eng, bass.BassScalarEngine)
                                      else eng.tensor_scalar(out, in_, 0.0, None, ALU.max))
        made = m.sem("made")
        with nc.Block() as block:
            @block.gpsimd
            def _(pool):
                c = Chain(pool, made)
                c.then(pool.memset(v[:, :, D:D + 1], 1.0))
                c.then(pool.memset(blocks[:, :], 1.0))
                b3 = blocks[:, :].rearrange("p (a b) -> p a b", b=HD)
                c.then(pool.affine_select(out=b3, in_=b3, compare_op=ALU.is_ge, fill=0.0, base=0,
                                          pattern=[[-HD, P // HD], [0, HD]], channel_multiplier=1))
                c.then(pool.affine_select(out=b3, in_=b3, compare_op=ALU.is_gt, fill=0.0, base=HD,
                                          pattern=[[HD, P // HD], [0, HD]], channel_multiplier=-1))
        products(nc, "mix1_q", 2 * KD,
                 lambda pe, n, bank: accumulate(pe, bank[:, :], [
                     (w[:, 0, c, (n // 2) * P:(n // 2 + 1) * P], xt[:, c, (n % 2) * D:(n % 2 + 1) * D]) for c in range(KD)]),
                 lambda eng, n, bank: relu(eng, qt[:, n // 2, (n % 2) * D:(n % 2 + 1) * D], bank[:, :]))
        products(nc, "mix1_kv", 2 * NT,
                 lambda pe, n, bank: accumulate(pe, bank[:, :], tile_terms(xt, w[:, 1 + n % 2, :, :], n // 2)),
                 lambda eng, n, bank: relu(eng, kk[:, n // 2, :], bank[:, :]) if n % 2 == 0
                 else copy(eng, v[:, n // 2, 0:D], bank[:, :]))

        def kv_product(pe, n, bank):
            for i in range(NT):
                pe.matmul(bank[:, 0:P], kk[:, i, n * P:(n + 1) * P], v[:, i, n * P:(n + 1) * P], start=(i == 0),
                          stop=(i == NT - 1))
            for i in range(NT):
                t = pe.matmul(bank[:, P:P + 1], kk[:, i, n * P:(n + 1) * P], v[:, i, D:D + 1], start=(i == 0), stop=(i == NT - 1))
            return t

        def kv_keep(eng, n, bank):
            eng.tensor_tensor(kv[:, n, 0:P], bank[:, 0:P], blocks[:, :], ALU.mult)
            return eng.tensor_tensor(kv[:, n, P:P + 4], blocks[:, 0::HD], bank[:, P:P + 1].broadcast_to([P, 4]), ALU.mult)
        products(nc, "mix1_c", KD, kv_product, kv_keep, scalar=False)

        def attend(pe, n, bank):
            i, g = n // KD, n % KD
            return pe.matmul(bank[:, 0:P + 4], qt[:, g, i * P:(i + 1) * P], kv[:, g, :], start=True, stop=True)

        def attended(eng, n, bank):
            i, g = n // KD, n % KD
            copy(eng, den[:, i, 4 * g:4 * g + 4], bank[:, P:P + 4])
            return copy(eng, pr[:, i, g * P:(g + 1) * P], bank[:, 0:P])
        products(nc, "mix1_a", NT * KD, attend, attended)
        steps = m.sem("steps")
        with nc.Block() as block:
            @block.vector
            def _(dve):
                c = Chain(dve, steps)
                c.then(dve.tensor_scalar(den[:, :, :], den[:, :, :], 1e-15, None, ALU.add))
                c.then(dve.reciprocal(den[:, :, :], den[:, :, :]))
                for i in range(NT):
                    c.mark(dve.tensor_tensor(pr[:, i, :].rearrange("p (h c) -> p h c", c=HD), pr[:, i, :].rearrange("p (h c) -> p h c", c=HD),
                                             den[:, i, :].unsqueeze(2).broadcast_to([P, NH, HD]), ALU.mult))
        turn(nc, k, "mix1_t", pr, pt)
        products(nc, "mix1_o", NT,
                 lambda pe, n, bank: accumulate(pe, bank[:, :], tile_terms(pt, w[:, 3, :, :], n) + [(k.ones[0:1, :], bias[:, :])]),
                 lambda eng, n, bank: eng.tensor_tensor(x2[:, n, :], bank[:, :], x2[:, n, :], ALU.add), scalar=False)


T = 64
DH = P
GRID = 16
CL = 8
BT = 32
LB = P // BT
NL = (T * BT + N) // P
NBK = NL * LB
W_UP, W_BASE, W_SLOPE, W_SCALE = D, 2 * D, 2 * D + GRID, 2 * D + 2 * GRID
ROW = W_SCALE + 4


def sign(c, dve, x, scratch, out):
    c.then(dve.tensor_scalar(scratch, x, 0.0, None, ALU.is_lt))
    c.then(dve.scalar_tensor_tensor(out, x, 0.0, scratch, ALU.is_gt, ALU.subtract))


def tile_signatures(nc, k, table, sig):
    with ExitStack() as ctx:
        m = Mem(nc, ctx, "sig")
        G = 4
        w = m.sb("w", [P, 2, G, D])
        sums = m.sb("sums", [P, T * KD])
        scratch = m.sb("scratch", [P, T * KD])
        csum = m.sb("csum", [P, CL, KD])
        cneg = m.sb("cneg", [P, CL, KD])
        got = [m.sem(f"got{i}") for i in range(2)]
        read, steps = m.sem("read"), m.sem("steps")
        v = table.rearrange("(t p) r -> p t r", p=P)
        with nc.Block() as block:
            @block.sync
            def _(sp):
                for b in range(2):
                    sp.dma_start(w[:, b, :, :], v[:, G * b:G * b + G, 0:D]).then_inc(got[b], 16)
                with sp.Fori(1, T // G // 2) as t:
                    for b in range(2):
                        sp.wait_ge(read, 2 * t + b - 1)
                        sp.dma_start(w[:, b, :, :], v[:, bass.ds((2 * t + b) * G, G), 0:D]).then_inc(got[b], 16)

            @block.vector
            def _(dve):
                c = Chain(dve, steps)
                with dve.Fori(0, T // G // 2) as t:
                    for b in range(2):
                        dve.wait_ge(got[b], 16 * t + 16)
                        dve.tensor_reduce(sums[:, bass.ds((2 * t + b) * (G * KD), G * KD)],
                                          w[:, b, :, :].rearrange("p g (c h) -> p (g c) h", h=DH), AX.X, ALU.add).then_inc(read, 1)
                dve.wait_ge(read, T // G)
                sign(c, dve, sums[:, :], scratch[:, :], sums[:, :])
                c.mark(dve.tensor_copy(sig[:, :, 0:T], sums[:, :].rearrange("p (t c) -> p c t", c=KD)))
                c.then(dve.tensor_reduce(csum[:, :, :], sums[:, :].rearrange("p (g u c) -> p g c u", g=CL, c=KD), AX.X, ALU.add))
                sign(c, dve, csum[:, :, :], cneg[:, :, :], csum[:, :, :])
                c.mark(dve.tensor_copy(sig[:, :, T:T + CL], csum[:, :, :].rearrange("p g c -> p c g")))


def route(nc, k, xt, sig, token_t, slot_i, weight_i, token_i):
    with ExitStack() as ctx:
        m = Mem(nc, ctx, "route")
        st = m.sb("st", [P, KD, N], BF16)
        neg = m.sb("neg", [P, KD, N], BF16)
        sc = m.sb("sc", [P, NT, T + CL])
        top = m.sb("top", [P, NT])
        best = m.sb("best", [P, NT])
        one = m.sb("one", [P, NT, T])
        w = m.sb("w", [P, NT, T])
        oneb = m.sb("oneb", [P, NT, T], BF16)
        cnt = m.sb("cnt", [P, T], I32)
        nblk = m.sb("nblk", [P, T])
        end = m.sb("end", [P, T])
        start = m.sb("start", [P, T])
        past = m.sb("past", [P, NBK, T])
        tile_of = m.sb("tile_of", [P, NBK])
        rows = m.sb("rows", [P, NT, 2], I32)
        zero = m.sb("zero", [P, 2 * NL], I32)
        lot = m.sb("lot", [P, NL, 2], I32)
        sb_ = [m.ps(f"s{i}", [P, D]) for i in range(2)]
        rank = m.ps("rank", [P, D])
        tot = m.ps("tot", [P, D])
        steps, signed, scored, hot, ranked, zeroed, filled, slotted, sent, back = (m.sem(x) for x in (
            "steps", "signed", "scored", "hot", "ranked", "zeroed", "filled", "slotted", "sent", "back"))
        wide, cwide = [P, NT, T], [P, NT, CL]
        with nc.Block() as block:
            @block.sync
            def _(sp):
                sp.wait_ge(zeroed, 1)
                sp.dma_start(token_t.rearrange("(p l) c -> p (l c)", p=P), zero[:, :]).then_inc(filled, 16)
                sp.wait_ge(sent, 16 * NT)
                sp.dma_start(lot[:, :, :], token_t.rearrange("(l p) c -> p l c", p=P)).then_inc(back, 16)

            @block.gpsimd
            def _(pool):
                pool.wait_ge(filled, 16)
                pool.wait_ge(slotted, 1)
                for i in range(NT):
                    pool.indirect_dma_start(out=token_t, out_offset=bass.IndirectOffsetOnAxis(ap=slot_i[:, i:i + 1], axis=0),
                                            in_=rows[:, i, :], in_offset=None).then_inc(sent, 16)
                pool.wait_ge(sent, 16 * NT)

            @block.tensor
            def _(pe):
                pe.wait_ge(signed, 1)
                for i in range(NT):
                    o = (i % 4) * (T + CL)
                    t = accumulate(pe, sb_[i // 4][:, o:o + T + CL], [(st[:, c, i * P:(i + 1) * P], sig[:, c, :]) for c in range(KD)])
                t.then_inc(scored, 1)
                pe.wait_ge(hot, 1)
                for i in range(NT):
                    t = accumulate(pe, rank[:, i * T:(i + 1) * T],
                                   [(k.ones_b[:, :], oneb[:, j, :]) for j in range(i)] + [(k.before_b[:, :], oneb[:, i, :])])
                t = accumulate(pe, tot[:, 0:T], [(k.ones_b[:, :], oneb[:, j, :]) for j in range(NT)])
                t.then_inc(ranked, 1)

            @block.vector
            def _(dve):
                c = Chain(dve, steps)
                dve.memset(zero[:, :], 0).then_inc(zeroed, 1)
                c.then(dve.tensor_scalar(neg[:, :, :], xt, 0.0, None, ALU.is_lt))
                c.then(dve.tensor_scalar(st[:, :, :], xt, 0.0, None, ALU.is_gt))
                dve.tensor_tensor(st[:, :, :], st[:, :, :], neg[:, :, :], ALU.subtract).then_inc(signed, 1)
                dve.wait_ge(scored, 1)
                for h in range(2):
                    c.mark(dve.tensor_copy(sc[:, 4 * h:4 * h + 4, :].rearrange("p i s -> p (i s)"), sb_[h][:, 0:4 * (T + CL)]))
                dve.wait_ge(steps, c.n)

                def first_best(x, width, shape, out):
                    c.then(dve.tensor_reduce(top[:, :], x, AX.X, ALU.max))
                    c.then(dve.tensor_tensor(w[:, :, 0:width], x, top[:, :].unsqueeze(2).broadcast_to(shape), ALU.is_equal))
                    c.then(dve.tensor_scalar(w[:, :, 0:width], w[:, :, 0:width], -1000.0, 1000.0, ALU.mult, ALU.add))
                    c.then(dve.tensor_tensor(w[:, :, 0:width], w[:, :, 0:width],
                                             k.iotaf[:, 0:width].unsqueeze(1).broadcast_to(shape), ALU.add))
                    c.then(dve.tensor_reduce(out, w[:, :, 0:width], AX.X, ALU.min))
                first_best(sc[:, :, T:T + CL], CL, cwide, best[:, :])
                c.then(dve.tensor_tensor(w[:, :, 0:CL], k.iotaf[:, 0:CL].unsqueeze(1).broadcast_to(cwide),
                                         best[:, :].unsqueeze(2).broadcast_to(cwide), ALU.is_equal))
                c.then(dve.tensor_scalar(w[:, :, 0:CL], w[:, :, 0:CL], -1.0, 10000.0, ALU.add, ALU.mult))
                for i in range(NT):
                    c.mark(dve.tensor_tensor(one[:, i, :].rearrange("p (g u) -> p g u", g=CL), sc[:, i, 0:T].rearrange("p (g u) -> p g u", g=CL),
                                             w[:, i, 0:CL].unsqueeze(2).broadcast_to([P, CL, T // CL]), ALU.add))
                dve.wait_ge(steps, c.n)
                first_best(one[:, :, :], T, wide, best[:, :])
                c.then(dve.tensor_tensor(one[:, :, :], k.iotaf[:, 0:T].unsqueeze(1).broadcast_to(wide),
                                         best[:, :].unsqueeze(2).broadcast_to(wide), ALU.is_equal))
                dve.tensor_copy(oneb[:, :, :], one[:, :, :]).then_inc(hot, 1)
                dve.wait_ge(ranked, 1)
                c.then(dve.tensor_scalar(cnt[:, :], tot[:, 0:T], float(BT - 1), None, ALU.add))
                c.then(dve.tensor_scalar(cnt[:, :], cnt[:, :], BT.bit_length() - 1, None, ALU.arith_shift_right))
                c.then(dve.tensor_copy(nblk[:, :], cnt[:, :]))
                c.then(dve.tensor_tensor_scan(end[:, :], nblk[:, :], k.ones[:, 0:T], 0.0, ALU.add, ALU.mult))
                c.then(dve.tensor_tensor(start[:, :], end[:, :], nblk[:, :], ALU.subtract))
                c.then(dve.tensor_scalar(start[:, :], start[:, :], float(BT), None, ALU.mult))
                c.then(dve.tensor_tensor(w[:, :, :], rank[:, 0:NT * T].rearrange("p (i t) -> p i t", t=T),
                                         start[:, :].unsqueeze(1).broadcast_to(wide), ALU.add))
                c.then(dve.tensor_tensor(w[:, :, :], w[:, :, :], one[:, :, :], ALU.mult))
                c.then(dve.tensor_reduce(top[:, :], w[:, :, :], AX.X, ALU.add))
                c.mark(dve.tensor_copy(slot_i[:, :], top[:, :]))
                c.mark(dve.memset(rows[:, :, 1], 0))
                for i in range(NT):
                    c.mark(dve.tensor_scalar(rows[:, i, 0:1], k.lane[:, :], float(i * P), None, ALU.add))
                dve.wait_ge(steps, c.n)
                dve.sem_inc(slotted, 1)
                c.then(dve.tensor_tensor(past[:, :, :], k.iotaf[:, 0:NBK].unsqueeze(2).broadcast_to([P, NBK, T]),
                                         end[:, :].unsqueeze(1).broadcast_to([P, NBK, T]), ALU.is_ge))
                c.then(dve.tensor_reduce(tile_of[:, :], past[:, :, :], AX.X, ALU.add))
                c.then(dve.tensor_scalar(tile_of[:, :], tile_of[:, :], float(T - 1), float(P), ALU.min, ALU.mult))
                c.then(dve.tensor_scalar(weight_i[:, :], tile_of[:, :], k.lane[:, :], None, ALU.add))
                dve.wait_ge(back, 16)
                c.then(dve.tensor_copy(token_i[:, :], lot[:, :, 0]))


def tile_ffn(nc, k, table, rows_t, y_t, weight_i, token_i):
    with ExitStack() as ctx:
        m = Mem(nc, ctx, "tile")
        w = m.sb("w", [P, 2, LB, ROW])
        x = m.sb("x", [P, 2, D])
        xt = m.sb("xt", [P, 2, KD, P])
        hn = m.sb("hn", [P, 2, P])
        s = m.sb("s", [P, P])
        r = m.sb("r", [P, P])
        cell = m.sb("cell", [P, P])
        one = m.sb("one", [P, P, GRID])
        pick = m.sb("pick", [P, P, GRID])
        base = m.sb("base", [P, P])
        slope = m.sb("slope", [P, P])
        hs = m.sb("hs", [P, 2, P])
        y = m.sb("y", [P, 2, D])
        idx = m.sb("idx", [P, 2, LB + 1], I32)
        tb = [m.ps(f"tb{i}", [P, D]) for i in range(2)]
        hb = [m.ps(f"hb{i}", [P, D]) for i in range(2)]
        yb = [m.ps(f"yb{i}", [P, D]) for i in range(2)]
        got = [m.sem(f"got{i}") for i in range(2)]
        stored = [m.sem(f"stored{i}") for i in range(2)]
        staged, turned, laid, hidden, squashed, splined, summed, brought, y_free, steps = (m.sem(x) for x in (
            "staged", "turned", "laid", "hidden", "squashed", "splined", "summed", "brought", "y_free", "steps"))
        with nc.Block() as block:
            @block.gpsimd
            def _(pool):
                def stage(n, b):
                    pool.tensor_copy(idx[:, b, 0:LB], weight_i[:, bass.ds(LB * n, LB)]).then_inc(staged, 1)
                    pool.tensor_copy(idx[:, b, LB:LB + 1], token_i[:, bass.ds(n, 1)]).then_inc(staged, 1)

                def fetch(b):
                    pool.indirect_dma_start(out=x[:, b, :], out_offset=None, in_=rows_t,
                                            in_offset=bass.IndirectOffsetOnAxis(ap=idx[:, b, LB:LB + 1], axis=0)).then_inc(got[b], 16)
                    for u in range(LB):
                        pool.indirect_dma_start(out=w[:, b, u, :], out_offset=None, in_=table,
                                                in_offset=bass.IndirectOffsetOnAxis(ap=idx[:, b, u:u + 1], axis=0)).then_inc(got[b], 16)
                stage(0, 0)
                pool.wait_ge(staged, 2)
                stage(1, 1)
                fetch(0)
                with pool.Fori(0, NL // 2 - 1) as t:
                    for b in range(2):
                        n = 2 * t + b
                        pool.wait_ge(staged, 2 * n + 4)
                        pool.wait_ge(got[b], 16 * (LB + 1) * (t + 1))
                        pool.wait_ge(summed, n + 2)
                        stage(n + 2, b)
                        fetch(1 - b)
                pool.wait_ge(staged, 2 * NL)
                pool.wait_ge(summed, NL)
                fetch(1)

            @block.tensor
            def _(pe):
                pe.sem_inc(hidden, 2)
                pe.sem_inc(summed, 2)

                def down(n, b, t):
                    pe.wait_ge(got[b], 16 * (LB + 1) * (t + 1))
                    pe.wait_ge(laid, n + 1)
                    for c in range(KD):
                        i = pe.transpose(tb[b][:, c * P:(c + 1) * P], x[:, b, c * P:(c + 1) * P], k.ident[:, :])
                    i.then_inc(turned, 1)
                    pe.wait_ge(laid, n + 3)
                    pe.wait_ge(squashed, n + 1)
                    for u in range(LB):
                        i = accumulate(pe, hb[b][:, u * BT:(u + 1) * BT], [
                            (w[:, b, u, c * P:(c + 1) * P], xt[:, b, c, u * BT:(u + 1) * BT]) for c in range(KD)])
                    i.then_inc(hidden, 1)

                def up(n, b):
                    pe.wait_ge(splined, n + 3)
                    pe.wait_ge(brought, n + 1)
                    for u in range(LB):
                        i = pe.matmul(yb[b][u * BT:(u + 1) * BT, :], hs[:, b, u * BT:(u + 1) * BT], w[:, b, u, W_UP:W_UP + D],
                                      start=True, stop=True, tile_position=(0, u * BT))
                    i.then_inc(summed, 1)
                down(0, 0, 0)
                with pe.Fori(0, NL // 2 - 1) as t:
                    down(2 * t + 1, 1, t)
                    up(2 * t, 0)
                    down(2 * t + 2, 0, t + 1)
                    up(2 * t + 1, 1)
                down(NL - 1, 1, NL // 2 - 1)
                up(NL - 2, 0)
                up(NL - 1, 1)

            @block.scalar
            def _(act):
                for q in (laid, squashed, brought):
                    act.sem_inc(q, 2)

                def into(n, b):
                    act.wait_ge(turned, n + 1)
                    act.wait_ge(hidden, n + 1)
                    act.activation(xt[:, b, :, :].rearrange("p c t -> p (c t)"), tb[b][:, :], ACT.Copy).then_inc(laid, 1)
                    act.wait_ge(hidden, n + 3)
                    act.wait_ge(splined, n + 1)
                    act.activation(hn[:, b, :], hb[b][:, 0:P], ACT.Sigmoid).then_inc(squashed, 1)

                def out(n, b):
                    act.wait_ge(summed, n + 3)
                    act.wait_ge(y_free, n + 1)
                    act.activation(y[:, b, :], yb[b][:, :], ACT.Copy).then_inc(brought, 1)
                into(0, 0)
                with act.Fori(0, NL // 2 - 1) as t:
                    into(2 * t + 1, 1)
                    out(2 * t, 0)
                    into(2 * t + 2, 0)
                    out(2 * t + 1, 1)
                into(NL - 1, 1)
                out(NL - 2, 0)
                out(NL - 1, 1)

            @block.vector
            def _(dve):
                dve.sem_inc(splined, 2)
                grid = k.iotaf[:, 0:GRID].unsqueeze(1).broadcast_to([P, P, GRID])
                spread = lambda z: z.unsqueeze(2).broadcast_to([P, P, GRID])
                with dve.Fori(0, NL // 2) as t:
                    for b in range(2):
                        n = 2 * t + b
                        STEPS = 12 + 2 * LB
                        c = Chain(dve, steps, STEPS * n)
                        weights = lambda u, o: w[:, b, u, o:o + GRID].unsqueeze(1).broadcast_to([P, BT, GRID])
                        blk = lambda z, u: z[:, u * BT:(u + 1) * BT]
                        dve.wait_ge(squashed, n + 3)
                        c.then(dve.tensor_scalar(s[:, :], hn[:, b, :], float(GRID), None, ALU.mult))
                        c.then(dve.tensor_scalar(r[:, :], s[:, :], 8388608.0, None, ALU.add))
                        c.then(dve.tensor_scalar(r[:, :], r[:, :], 8388608.0, None, ALU.subtract))
                        c.then(dve.tensor_tensor(cell[:, :], r[:, :], s[:, :], ALU.is_gt))
                        c.then(dve.tensor_tensor(cell[:, :], r[:, :], cell[:, :], ALU.subtract))
                        c.then(dve.tensor_scalar(cell[:, :], cell[:, :], float(GRID - 1), None, ALU.min))
                        c.mark(dve.tensor_tensor(s[:, :], s[:, :], cell[:, :], ALU.subtract))
                        c.then(dve.tensor_tensor(one[:, :, :], grid, spread(cell[:, :]), ALU.is_equal))
                        for z, o in ((base, W_BASE), (slope, W_SLOPE)):
                            for u in range(LB):
                                i = dve.tensor_tensor(blk(pick, u), blk(one, u), weights(u, o), ALU.mult)
                                if u == LB - 1:
                                    c.then(i)
                                else:
                                    c.mark(i)
                            c.then(dve.tensor_reduce(z[:, :], pick[:, :, :], AX.X, ALU.add))
                        c.then(dve.tensor_tensor(slope[:, :], slope[:, :], s[:, :], ALU.mult))
                        dve.tensor_tensor(base[:, :], base[:, :], slope[:, :], ALU.add).then_inc(steps, 1)
                        c.n += 1
                        dve.wait_ge(steps, c.base + c.n)
                        assert c.n == STEPS, c.n
                        dve.wait_ge(summed, n + 1)
                        for u in range(LB):
                            i = dve.tensor_scalar(blk(hs[:, b, :], u), blk(base, u), w[:, b, u, W_SCALE:W_SCALE + 1], None, ALU.mult)
                        i.then_inc(splined, 1)

            @block.sync
            def _(sp):
                sp.sem_inc(y_free, 2)
                v = y_t.rearrange("(l p) d -> p l d", p=P)

                def put(n, b):
                    sp.wait_ge(brought, n + 3)
                    sp.dma_start(v[:, bass.ds(n, 1), :].rearrange("p a d -> p (a d)"), y[:, b, :]).then_inc(stored[b], 16)
                put(0, 0)
                with sp.Fori(0, NL // 2 - 1) as t:
                    put(2 * t + 1, 1)
                    sp.wait_ge(stored[0], 16 * t + 16)
                    sp.sem_inc(y_free, 1)
                    put(2 * t + 2, 0)
                    sp.wait_ge(stored[1], 16 * t + 16)
                    sp.sem_inc(y_free, 1)
                put(NL - 1, 1)
                for b in range(2):
                    sp.wait_ge(stored[b], 16 * (NL // 2))


def layer1_ffn(nc, k, a, x3, xn, xt, out):
    with ExitStack() as ctx:
        m = Mem(nc, ctx, "ffn1")
        xa = m.sb("xa", [P, NT, D])
        sig = m.sb("sig", [P, KD, T + CL], BF16)
        slot_i = m.sb("slot_i", [P, NT], I32)
        weight_i = m.sb("weight_i", [P, NBK], I32)
        token_i = m.sb("token_i", [P, NL], I32)
        gamma = m.sb("gamma", [P, D])
        beta = m.sb("beta", [P, D])
        rows_t = nc.dram_tensor("tile_rows", (N, D), F32).ap()
        token_t = nc.dram_tensor("tile_tokens", (NL * P, 2), I32).ap()
        y_t = nc.dram_tensor("tile_out", (NL * P, D), F32).ap()
        table = a["tile_table"]
        tile_signatures(nc, k, table, sig)
        load(nc, "ffn1_load", [(gamma[:, :], a["L1_ffn_gamma"].rearrange("(a n) -> a n", a=1).broadcast_to([P, D])),
                               (beta[:, :], a["L1_ffn_beta"].rearrange("(a n) -> a n", a=1).broadcast_to([P, D]))])
        layernorm(nc, k, "ln3", x3, xa)
        layernorm(nc, k, "ln4", xa, xn, extra=(gamma, beta))
        store(nc, "ffn1_store", [(chunks(rows_t), xn[:, :, :])])
        turn(nc, k, "turn3", xn, xt)
        route(nc, k, xt, sig, token_t, slot_i, weight_i, token_i)
        tile_ffn(nc, k, table, rows_t, y_t, weight_i, token_i)
        got, summed, stored = m.sem("got"), m.sem("summed"), m.sem("stored")
        y = xn
        with nc.Block() as block:
            @block.gpsimd
            def _(pool):
                for i in range(NT):
                    pool.indirect_dma_start(out=y[:, i, :], out_offset=None, in_=y_t,
                                            in_offset=bass.IndirectOffsetOnAxis(ap=slot_i[:, i:i + 1], axis=0)).then_inc(got, 16)

            @block.vector
            def _(dve):
                dve.tensor_tensor(xa[:, :, :], xa[:, :, :], x3[:, :, :], ALU.add).then_inc(summed, 1)
                dve.wait_ge(got, 16 * NT)
                dve.wait_ge(summed, 1)
                dve.tensor_tensor(xa[:, :, :], xa[:, :, :], y[:, :, :], ALU.add).then_inc(summed, 1)

            @block.sync
            def _(sp):
                sp.wait_ge(summed, 2)
                sp.dma_start(chunks(out), xa[:, :, :]).then_inc(stored, 16)
                sp.wait_ge(stored, 16)


USED = ("x", "src", "dst", "L0_gnn_W", "L0_gnn_b", "L0_gnn_diffusion_weights",
        "L0_mix_Wq", "L0_mix_Wk", "L0_mix_Wv", "L0_mix_W1", "L0_mix_W2",
        "L0_ffn_Wg", "L0_ffn_W1", "L0_ffn_b1", "L0_ffn_W2", "L0_ffn_b2",
        "L1_gnn_W_l", "L1_gnn_W_r", "L1_gnn_att", "L1_gnn_bias",
        "L1_mix_qkv_weight", "L1_mix_proj_weight", "L1_mix_proj_bias",
        "L1_ffn_gamma", "L1_ffn_beta", "tile_table")


def program(nc, a, out):
    with ExitStack() as ctx:
        k = keep(nc, ctx)
        m = Mem(nc, ctx, "x")
        x, xn, xt, x1 = (m.sb(s, [P, NT, D]) for s in ("x", "xn", "xt", "x1"))
        xt = xt[:, :, :].rearrange("p a b -> p (a b)").rearrange("p (c n) -> p c n", c=KD)
        keys_t = nc.dram_tensor("edge_keys", (EP + 2,), F32).ap()
        with part(nc):
            constants(nc, k)
            sort_edges(nc, k, a["src"], a["dst"], keys_t)
            load(nc, "loadx", [(x[:, :, :], chunks(a["x"]))])
            layernorm(nc, k, "ln0", x, xn)
            turn(nc, k, "turn0", xn, xt)
            layer0_gnn(nc, k, a, x, xn, xt, x1)
            layer0_mix(nc, k, a, xn, xt, x1)
        with part(nc):
            layer0_ffn(nc, k, a, x1, xn, xt)
            layernorm(nc, k, "ln2", x1, xn)
            turn(nc, k, "turn2", xn, xt)
            layer1_gnn(nc, k, a, keys_t, xn, xt, x1)
        with part(nc):
            layer1_mix(nc, k, a, xn, xt, x1)
            layer1_ffn(nc, k, a, x1, xn, xt, out)


def lay_out(name, v):
    if name in ("L0_mix_Wq", "L0_mix_Wk", "L0_mix_Wv", "L0_mix_W1", "L0_mix_W2", "L1_mix_qkv_weight", "L1_mix_proj_weight"):
        return v.T
    if name == "L0_ffn_b1":
        return v.reshape(NE, FF // P, P).transpose(2, 0, 1)
    return v


def kernel(**inputs):
    import numpy as np
    import concourse.bacc as bacc
    from concourse.bass_utils import run_bass_kernel_spmd as run

    nc = bacc.Bacc("TRN2", target_bir_lowering=False, num_devices=1)
    arrays, a = {}, {}
    for n in USED:
        if n == "tile_table":
            v = np.concatenate([
                inputs["L1_ffn_Wd"].reshape(T, DH, KD, P).transpose(0, 3, 2, 1).reshape(T, P, D),
                inputs["L1_ffn_Wu"].transpose(0, 2, 1), inputs["L1_ffn_spline_bases"], inputs["L1_ffn_spline_slopes"],
                np.broadcast_to(inputs["L1_ffn_scale"][:, None, None], (T, P, ROW - W_SCALE))], axis=2).reshape(T * P, ROW)
        else:
            v = lay_out(n, inputs[n])
        v = np.ascontiguousarray(v)
        arrays[f"in_{n}"] = v
        a[n] = nc.dram_tensor(f"in_{n}", v.shape, mybir.dt.from_np(v.dtype), kind="ExternalInput").ap()
    out = nc.dram_tensor("result", (N, D), F32, kind="ExternalOutput").ap()
    program(nc, a, out)
    r = run(nc, [arrays], core_ids=[0])
    return r.results[0]["result"]
```

```python
from contextlib import ExitStack, contextmanager

import concourse.bass as bass
from concourse import mybir

P = 128
N = 1024
D = 512
NT = N // P
KD = D // P
E = 32768
EC = E // P
CH = EC + NT
NG = N // P
NB = CH + NG
EP = NB * P
SEG = 16
BS = NB // SEG
SL = BS * P
H8 = 8
HC = D // H8
BIG = 1.0e30

F32 = mybir.dt.float32
F16 = mybir.dt.float16
BF16 = mybir.dt.bfloat16
I32 = mybir.dt.int32
ALU = mybir.AluOpType
ACT = mybir.ActivationFunctionType
AX = mybir.AxisListType


class Chain:

    def __init__(self, eng, sem, base=0):
        self.eng, self.sem, self.base, self.n = eng, sem, base, 0

    def mark(self, ins):
        ins.then_inc(self.sem, 1)
        self.n += 1
        return self.n

    def then(self, ins):
        self.mark(ins)
        self.eng.wait_ge(self.sem, self.base + self.n)


class Mem:

    def __init__(self, nc, ctx, stage):
        self.nc, self.ctx, self.stage = nc, ctx, stage

    def sb(self, name, shape, dt=F32):
        return self.ctx.enter_context(self.nc.sbuf_tensor(f"{self.stage}_{name}", shape, dt))

    def ps(self, name, shape, dt=F32):
        return self.ctx.enter_context(self.nc.psum_tensor(f"{self.stage}_{name}", shape, dt))

    def sem(self, name):
        return self.nc.alloc_semaphore(name=f"{self.stage}_{name}")


@contextmanager
def part(nc):
    with nc.cleanup_on_exit():
        yield
    nc.all_engine_barrier()


def scatter(pool, table, slot, rows, count, idx, buf, staged, sent, filled):
    G = 8
    lots = count // G

    def stage(n, b):
        pool.tensor_copy(idx[:, b, :], slot[:, bass.ds(G * n, G)]).then_inc(staged, 1)
        pool.tensor_copy(buf[:, b, :, :], rows[:, bass.ds(G * n, G), :]).then_inc(staged, 1)

    def send(b):
        for j in range(G):
            pool.indirect_dma_start(out=table, out_offset=bass.IndirectOffsetOnAxis(ap=idx[:, b, j:j + 1], axis=0),
                                    in_=buf[:, b, j, :], in_offset=None).then_inc(sent[b], 16)
    stage(0, 0)
    pool.wait_ge(staged, 2)
    stage(1, 1)
    send(0)
    with pool.Fori(0, lots // 2 - 1) as t:
        for b in range(2):
            pool.wait_ge(staged, 4 * t + 2 * b + 4)
            pool.wait_ge(sent[b], 16 * G * (t + 1))
            stage(2 * t + b + 2, b)
            send(1 - b)
    pool.wait_ge(staged, 4 * (lots // 2))
    if lots % 2:
        pool.wait_ge(sent[0], 16 * G * (lots // 2))
        stage(lots - 1, 0)
    send(1)
    if lots % 2:
        pool.wait_ge(staged, 2 * lots)
        send(0)
    pool.wait_ge(sent[0], 16 * G * (lots - lots // 2))
    pool.wait_ge(sent[1], 16 * G * (lots // 2))


def constants(nc, k):
    with ExitStack() as ctx:
        m = Mem(nc, ctx, "const")
        made, laid = m.sem("made"), m.sem("laid")
        row = m.sb("row", [P, N], I32)
        with nc.Block() as block:
            @block.gpsimd
            def _(pool):
                c = Chain(pool, made)
                c.then(pool.iota(row[:, :], [[1, N]], base=0, channel_multiplier=0))
                c.then(pool.iota(k.lane_i[:, :], [[0, 1]], base=0, channel_multiplier=1))
                c.then(pool.memset(k.ident[:, :], 0.0))
                c.then(pool.memset(k.ones[:, :], 1.0))
                c.then(pool.affine_select(out=k.ident[:, :], in_=k.ident[:, :], compare_op=ALU.not_equal, fill=1.0,
                                          base=0, pattern=[[-1, P]], channel_multiplier=1))
                c.then(pool.affine_select(out=k.before[:, :], in_=k.ones[:, :], compare_op=ALU.is_gt, fill=0.0,
                                          base=0, pattern=[[1, P]], channel_multiplier=-1))

            @block.vector
            def _(dve):
                dve.wait_ge(made, 6)
                c = Chain(dve, laid)
                c.mark(dve.tensor_copy(k.iota16[:, :], row[:, :]))
                c.mark(dve.tensor_copy(k.iotaf[:, :], row[:, :]))
                c.mark(dve.tensor_copy(k.lane[:, :], k.lane_i[:, :]))
                c.mark(dve.tensor_copy(k.ones_b[:, :], k.ones[:, :]))
                c.mark(dve.tensor_copy(k.ident_b[:, :], k.ident[:, :]))
                c.mark(dve.tensor_copy(k.before_b[:, :], k.before[:, :]))
                c.mark(dve.tensor_scalar(k.later[:, :], k.before[:, :], -1.0, 1.0, ALU.mult, ALU.add))
                dve.wait_ge(laid, c.n)
                c.mark(dve.tensor_tensor(k.later[:, :], k.later[:, :], k.ident[:, :], ALU.subtract))
                c.mark(dve.tensor_scalar(k.notbefore_b[:, :], k.before[:, :], 1.0, None, ALU.subtract))


R = 32
TW = R * CH
SLICES = [slice(o, min(o + D, TW)) for o in range(0, TW, D)]


def radix_slots(nc, k, name, digit, slot, groups=None):
    with ExitStack() as ctx:
        m = Mem(nc, ctx, name)
        hot = m.sb("hot", [P, R, CH], BF16)
        run = m.sb("run", [P, TW])
        prod = m.sb("prod", [P, R, CH])
        bank = [m.ps(f"bank{i}", [P, D]) for i in range(4)]
        made, full, free, based, full2, free2, steps = (m.sem(x) for x in (
            "made", "full", "free", "based", "full2", "free2", "steps"))
        flat = lambda x: x[:, :, :].rearrange("p q n -> p (q n)")
        QS = 8
        if groups is not None:
            last, before, total, nblk, shift = (m.sb(x, [P, NG]) for x in ("last", "before", "total", "nblk", "shift"))
            total_i = m.sb("total_i", [P, NG], I32)
        with nc.Block() as block:
            @block.vector
            def _(dve):
                c = Chain(dve, steps)
                for q in range(0, R, QS):
                    shape = [P, QS, CH]
                    dve.tensor_tensor(hot[:, q:q + QS, :], digit[:, :].unsqueeze(1).broadcast_to(shape),
                                      k.iotaf[:, q:q + QS].unsqueeze(2).broadcast_to(shape), ALU.is_equal).then_inc(made, 1)
                dve.wait_ge(free, len(SLICES))
                c.then(dve.tensor_tensor_scan(run[:, :], run[:, :], k.ones[:, 0:1].broadcast_to([P, TW]), 0.0, ALU.add, ALU.mult))
                if groups is not None:
                    W = TW // NG
                    c.mark(dve.tensor_copy(last[:, :], run[:, W - 1::W]))
                    c.mark(dve.memset(before[:, 0:1], 0.0))
                    c.then(dve.tensor_copy(before[:, 1:NG], run[:, W - 1:TW - 1:W]))
                    c.then(dve.tensor_tensor(total[:, :], last[:, :], before[:, :], ALU.subtract))
                    c.then(dve.tensor_scalar(total_i[:, :], total[:, :], float(P - 1), None, ALU.add))
                    c.then(dve.tensor_scalar(total_i[:, :], total_i[:, :], P.bit_length() - 1, None, ALU.arith_shift_right))
                    c.then(dve.tensor_copy(nblk[:, :], total_i[:, :]))
                    c.then(dve.tensor_tensor_scan(groups[:, :], nblk[:, :], k.ones[:, 0:NG], 0.0, ALU.add, ALU.mult))
                    c.then(dve.tensor_tensor(shift[:, :], groups[:, :], nblk[:, :], ALU.subtract))
                    c.then(dve.tensor_scalar(shift[:, :], shift[:, :], float(P), None, ALU.mult))
                    c.then(dve.tensor_tensor(shift[:, :], shift[:, :], before[:, :], ALU.subtract))
                    for g in range(NG):
                        c.mark(dve.tensor_scalar(run[0:1, g * W:(g + 1) * W], run[0:1, g * W:(g + 1) * W], shift[0:1, g:g + 1],
                                                 None, ALU.add))
                    dve.wait_ge(steps, c.n)
                dve.sem_inc(based, 1)
                for j, here in enumerate(SLICES):
                    dve.wait_ge(full2, j + 1)
                    dve.tensor_tensor(flat(prod)[:, here], bank[j % 4][:, 0:here.stop - here.start], flat(hot)[:, here],
                                      ALU.mult).then_inc(free2, 1)
                dve.wait_ge(free2, len(SLICES))
                c.then(dve.tensor_reduce(slot[:, :], prod[:, :, :].rearrange("p q n -> p n q"), AX.X, ALU.add))

            @block.tensor
            def _(pe):
                for j, here in enumerate(SLICES):
                    pe.wait_ge(made, (here.stop - 1) // (QS * CH) + 1)
                    if j >= 4:
                        pe.wait_ge(free, j - 3)
                    pe.matmul(bank[j % 4][:, 0:here.stop - here.start], k.ones_b[:, :], flat(hot)[:, here],
                              start=True, stop=True).then_inc(full, 1)
                pe.wait_ge(based, 1)
                for j, here in enumerate(SLICES):
                    b = bank[j % 4][:, 0:here.stop - here.start]
                    if j >= 4:
                        pe.wait_ge(free2, j - 3)
                    pe.matmul(b, k.notbefore_b[:, :], flat(hot)[:, here], start=True, stop=False)
                    pe.matmul(b, k.ones[0:1, :], run[0:1, here], start=False, stop=True).then_inc(full2, 1)

            @block.scalar
            def _(act):
                for j, here in enumerate(SLICES):
                    act.wait_ge(full, j + 1)
                    act.activation(run[:, here], bank[j % 4][:, 0:here.stop - here.start], ACT.Copy).then_inc(free, 1)


def place(nc, k, name, slot, values, outs, width):
    with ExitStack() as ctx:
        m = Mem(nc, ctx, name)
        U = 4
        slot_i = m.sb("slot_i", [P, CH], I32)
        part_i = m.sb("part_i", [P, 2, CH], I32)
        at_lane = m.sb("at_lane", [P, CH])
        at_block = m.sb("at_block", [P, CH])
        lanes = m.sb("lanes", [P, U, 2, P], F16)
        blocks = m.sb("blocks", [P, U, NB], F16)
        zb = m.sb("zb", [P, D], BF16)
        placed = [m.ps(f"placed{i}", [P, D]) for i in range(2)]
        zeroed, laid, used, steps = (m.sem(x) for x in ("zeroed", "laid", "used", "steps"))
        with nc.Block() as block:
            @block.vector
            def _(dve):
                c = Chain(dve, steps)
                dve.memset(zb[:, :], 0.0).then_inc(zeroed, 1)
                c.then(dve.tensor_copy(slot_i[:, :], slot[:, :]))
                c.mark(dve.tensor_scalar(part_i[:, 0, :], slot_i[:, :], P - 1, None, ALU.bitwise_and))
                c.then(dve.tensor_scalar(part_i[:, 1, :], slot_i[:, :], P.bit_length() - 1, None, ALU.arith_shift_right))
                c.mark(dve.tensor_copy(at_lane[:, :], part_i[:, 0, :]))
                c.then(dve.tensor_copy(at_block[:, :], part_i[:, 1, :]))

                def lay(n, u):
                    for f, v in enumerate(values):
                        dve.tensor_scalar(lanes[:, u, f, :], k.iota16[:, 0:P], at_lane[:, bass.ds(n, 1)], v[:, bass.ds(n, 1)],
                                          ALU.is_equal, ALU.mult)
                    dve.tensor_scalar(blocks[:, u, 0:width], k.iota16[:, 0:width], at_block[:, bass.ds(n, 1)], None,
                                      ALU.is_equal).then_inc(laid, 1)
                for u in range(U):
                    lay(u, u)
                with dve.Fori(1, CH // U) as t:
                    for u in range(U):
                        dve.wait_ge(used, U * t + u - U + 1)
                        lay(U * t + u, u)
                dve.wait_ge(used, CH)
                for f, out in enumerate(outs):
                    c.mark(dve.tensor_copy(out[:, 0:width], placed[f][:, 0:width]))

            @block.tensor
            def _(pe):
                pe.wait_ge(zeroed, 1)
                for x in placed:
                    pe.matmul(x[:, :], k.ones_b[:, :], zb[:, :], start=True, stop=False, skip_group_check=True)
                with pe.Fori(0, CH // U) as t:
                    for u in range(U):
                        pe.wait_ge(laid, U * t + u + 1)
                        for f in range(2):
                            i = pe.matmul(placed[f][:, 0:width], lanes[:, u, f, :], blocks[:, u, 0:width], start=False, stop=False,
                                          skip_group_check=True)
                        i.then_inc(used, 1)


def sort_edges(nc, k, src, dst, keys_t):
    with ExitStack() as ctx:
        m = Mem(nc, ctx, "sort")
        dst_i = m.sb("dst_i", [P, CH], I32)
        src_i = m.sb("src_i", [P, EC], I32)
        srcf = m.sb("srcf", [P, CH])
        dstf = m.sb("dstf", [P, CH])
        key = m.sb("key", [P, CH])
        digit = m.sb("digit", [P, CH])
        slot = m.sb("slot", [P, CH])
        src2 = m.sb("src2", [P, CH])
        key2 = m.sb("key2", [P, CH])
        gend = m.sb("gend", [P, NG])
        ging = m.sb("ging", [P, NB, NG])
        keyrow = m.sb("keyrow", [SEG, SL])
        guard = m.sb("guard", [1, 2])
        loaded, first, second, third = (m.sem(x) for x in ("loaded", "first", "second", "third"))
        SHIFT = R.bit_length() - 1
        with nc.Block() as block:
            @block.sync
            def _(sp):
                sp.dma_start(dst_i[:, 0:EC], dst.rearrange("(p c) -> p c", p=P)).then_inc(loaded, 16)
                sp.dma_start(src_i[:, :], src.rearrange("(p c) -> p c", p=P)).then_inc(loaded, 16)

            @block.vector
            def _(dve):
                c = Chain(dve, first)
                for i in range(NT):
                    c.mark(dve.tensor_scalar(dstf[:, EC + i:EC + i + 1], k.lane[:, :], float(P * i), None, ALU.add))
                    c.mark(dve.tensor_scalar(srcf[:, EC + i:EC + i + 1], k.lane[:, :], float(P * i), None, ALU.add))
                dve.wait_ge(loaded, 32)
                c.mark(dve.tensor_copy(dstf[:, 0:EC], dst_i[:, 0:EC]))
                c.then(dve.tensor_copy(srcf[:, 0:EC], src_i[:, :]))
                c.mark(dve.tensor_scalar(key[:, :], dstf[:, :], 1.0, None, ALU.add))
                c.then(dve.tensor_copy(dst_i[:, EC:CH], dstf[:, EC:CH]))
                c.then(dve.tensor_scalar(dst_i[:, :], dst_i[:, :], R - 1, None, ALU.bitwise_and))
                c.then(dve.tensor_copy(digit[:, :], dst_i[:, :]))
        radix_slots(nc, k, "low", digit, slot)
        place(nc, k, "placel", slot, (srcf, key), (src2, key2), CH)
        with nc.Block() as block:
            @block.vector
            def _(dve):
                c = Chain(dve, second)
                c.then(dve.tensor_scalar(dst_i[:, :], key2[:, :], -1.0, None, ALU.add))
                c.then(dve.tensor_scalar(dst_i[:, :], dst_i[:, :], SHIFT, None, ALU.arith_shift_right))
                c.then(dve.tensor_copy(digit[:, :], dst_i[:, :]))
        radix_slots(nc, k, "high", digit, slot, groups=gend)
        place(nc, k, "placeh", slot, (src2, key2), (k.srcf, k.key), NB)
        keyp = m.ps("keyp", [SEG, 5 * D])
        turned, copied, stored, guarded = (m.sem(x) for x in ("turned", "copied", "stored", "guarded"))
        with nc.Block() as block:
            @block.tensor
            def _(pe):
                for i in range(BS):
                    t = pe.transpose(keyp[:, i * P:(i + 1) * P], k.key[:, i::BS], k.ident[:, :])
                t.then_inc(turned, 1)

            @block.vector
            def _(dve):
                c = Chain(dve, third)
                dve.memset(guard[:, 0:1], 0.0).then_inc(guarded, 1)
                dve.memset(guard[:, 1:2], -1.0).then_inc(guarded, 1)
                c.mark(dve.tensor_copy(k.src_i[:, :], k.srcf[:, :]))
                c.mark(dve.tensor_scalar(k.dst_i[:, :], k.key[:, :], -1.0, 0.0, ALU.add, ALU.max))
                dve.wait_ge(turned, 1)
                dve.tensor_copy(keyrow[:, :], keyp[:, 0:SL]).then_inc(copied, 1)
                c.then(dve.tensor_tensor(ging[:, :, :], k.iotaf[:, 0:NB].unsqueeze(2).broadcast_to([P, NB, NG]),
                                         gend[:, :].unsqueeze(1).broadcast_to([P, NB, NG]), ALU.is_ge))
                c.then(dve.tensor_reduce(k.group[:, :], ging[:, :, :], AX.X, ALU.add))
                c.then(dve.tensor_scalar(k.group[:, :], k.group[:, :], float(NG - 1), None, ALU.min))
                c.mark(dve.tensor_scalar(k.group_i[:, :], k.group[:, :], float(D), None, ALU.mult))
                c.then(dve.tensor_scalar(k.local[:, :], k.group[:, :], float(-P), -1.0, ALU.mult, ALU.add))
                c.then(dve.tensor_tensor(k.local[:, :], k.local[:, :], k.key[:, :], ALU.add))

            @block.sync
            def _(sp):
                row = keys_t.rearrange("(a n) -> a n", a=1)
                sp.wait_ge(guarded, 2)
                sp.dma_start(row[:, 0:1], guard[:, 0:1]).then_inc(stored, 16)
                sp.dma_start(row[:, EP + 1:EP + 2], guard[:, 1:2]).then_inc(stored, 16)
                sp.wait_ge(copied, 1)
                sp.dma_start(keys_t[1:EP + 1].rearrange("(s n) -> s n", s=SEG), keyrow[:, :]).then_inc(stored, 16)
                sp.wait_ge(stored, 48)


class Keep:
    pass


def keep(nc, ctx):
    k = Keep()
    m = Mem(nc, ctx, "k")
    k.ident = m.sb("ident", [P, P])
    k.ident_b = m.sb("ident_b", [P, P], BF16)
    k.ones = m.sb("ones", [P, P])
    k.ones_b = m.sb("ones_b", [P, P], BF16)
    k.before = m.sb("before", [P, P])
    k.before_b = m.sb("before_b", [P, P], BF16)
    k.notbefore_b = m.sb("notbefore_b", [P, P], BF16)
    k.later = m.sb("later", [P, P])
    k.iota16 = m.sb("iota16", [P, N], F16)
    k.iotaf = m.sb("iotaf", [P, N])
    k.lane_i = m.sb("lane_i", [P, 1], I32)
    k.lane = m.sb("lane", [P, 1])
    k.group = m.sb("group", [P, NB])
    k.group_i = m.sb("group_i", [P, NB], I32)
    k.srcf = m.sb("srcf", [P, NB])
    k.src_i = m.sb("src_i", [P, NB], I32)
    k.dst_i = m.sb("dst_i", [P, NB], I32)
    k.local = m.sb("local", [P, NB])
    k.key = m.sb("key", [P, NB])
    return k


def block_groups(nc, k, first, count):
    _, values = nc.values_load_multi_w_load_instructions(
        k.group_i[0:1, bass.ds(first, count)], engines=[mybir.EngineType.PE], min_val=0, max_val=(NG - 1) * D,
        skip_runtime_bounds_check_because="k.group_i is clamped to the last group where it is made")
    return values


def adjacency(nc, k, adj, rs):
    with ExitStack() as ctx:
        m = Mem(nc, ctx, "adj")
        U = 8
        zb = m.sb("zb", [P, D], BF16)
        to = m.sb("to", [P, U, P], BF16)
        frm = m.sb("frm", [P, U, D], BF16)
        cnt = m.sb("cnt", [P, NG, N], BF16)
        both = m.sb("both", [P, 2, N], BF16)
        two = m.sb("two", [P, P], BF16)
        zeroed, made, used, counted, capped = (m.sem(x) for x in ("zeroed", "made", "used", "counted", "capped"))
        turned, summed, steps = (m.sem(x) for x in ("turned", "summed", "steps"))
        with ExitStack() as inner:
            mi = Mem(nc, inner, "adjc")
            acc = mi.ps("acc", [P, NG * D])
            with nc.Block() as block:
                @block.vector
                def _(dve):
                    dve.memset(zb[:, :], 0.0).then_inc(zeroed, 1)

                    def onehots(n, u, h):
                        dve.tensor_scalar(to[:, u, :], k.iota16[:, 0:P], k.local[:, bass.ds(n, 1)], None,
                                          ALU.is_equal).then_inc(made, 1)
                        dve.tensor_scalar(frm[:, u, :], k.iota16[:, h * D:(h + 1) * D], k.srcf[:, bass.ds(n, 1)], None,
                                          ALU.is_equal).then_inc(made, 1)
                    for h in range(2):
                        for u in range(U):
                            if h:
                                dve.wait_ge(used, NB * h)
                            onehots(u, u, h)
                        with dve.Fori(1, NB // U) as t:
                            for u in range(U):
                                dve.wait_ge(used, U * t + (u + 1 - U + NB * h))
                                onehots(U * t + u, u, h)
                        dve.wait_ge(used, NB * (h + 1))
                        for g in range(NG):
                            dve.tensor_scalar(cnt[:, g, h * D:(h + 1) * D], acc[:, g * D:(g + 1) * D], 3.0, None,
                                              ALU.min).then_inc(capped, 1)

                @block.tensor
                def _(pe):
                    pe.wait_ge(zeroed, 1)
                    for h in range(2):
                        if h:
                            pe.wait_ge(capped, NG)
                        for g in range(NG):
                            pe.matmul(acc[:, g * D:(g + 1) * D], k.ones_b[:, :], zb[:, :], start=True, stop=False,
                                      skip_group_check=True)
                        with pe.Fori(0, NB // U) as t:
                            groups = block_groups(nc, k, U * t, U)
                            for u in range(U):
                                g = groups[u]
                                pe.wait_ge(made, 2 * (U * t + u) + (2 + 2 * NB * h))
                                pe.matmul(acc[:, bass.ds(g, D)], to[:, u, :], frm[:, u, :], start=False, stop=False,
                                          skip_group_check=True).then_inc(used, 1)
        tp = m.ps("tp", [P, 2, N], BF16)
        with nc.Block() as block:
            @block.tensor
            def _(pe):
                for i in range(NT):
                    if i >= 2:
                        pe.wait_ge(summed, i - 1)
                    for j in range(NT):
                        t = pe.transpose(tp[:, i % 2, j * P:(j + 1) * P], cnt[:, j, i * P:(i + 1) * P], k.ident_b[:, :])
                    t.then_inc(turned, 1)

            @block.vector
            def _(dve):
                c = Chain(dve, steps)
                c.then(dve.tensor_scalar(two[:, :], k.ident[:, :], 2.0, None, ALU.mult))
                for i in range(NT):
                    here = slice(i * P, (i + 1) * P)
                    dve.wait_ge(turned, i + 1)
                    dve.tensor_tensor(both[:, i % 2, :], cnt[:, i, :], tp[:, i % 2, :], ALU.add).then_inc(summed, 1)
                    dve.wait_ge(summed, i + 1)
                    c.then(dve.tensor_tensor(both[:, i % 2, here], both[:, i % 2, here], two[:, :], ALU.subtract))
                    c.then(dve.tensor_scalar(adj[:, i, :], both[:, i % 2, :], 0.0, None, ALU.is_gt))
                    c.then(dve.tensor_tensor(adj[:, i, here], adj[:, i, here], k.ident[:, :], ALU.add))
                c.then(dve.tensor_reduce(rs[:, :], adj[:, :, :], AX.X, ALU.add))
                c.then(dve.tensor_scalar(rs[:, :], rs[:, :], 1.0, None, ALU.max))
                c.then(dve.reciprocal(rs[:, :], rs[:, :]))


def products(nc, name, count, produce, evacuate, width=D, dt=F32, ring=4, vector=True, scalar=True, before=None):
    with ExitStack() as ctx:
        m = Mem(nc, ctx, name)
        bank = [m.ps(f"bank{i}", [P, D if dt == F32 else 2 * D], dt) for i in range(ring)]
        full = m.sem("full")
        free = [m.sem("free_even"), m.sem("free_odd")]
        both = vector and scalar
        with nc.Block() as block:
            @block.tensor
            def _(pe):
                for n in range(count):
                    if n >= ring:
                        done = n - ring + 1
                        pe.wait_ge(free[(n - ring) % 2] if both else free[0], (done + 1) // 2 if both and (n - ring) % 2 == 0
                                   else done // 2 if both else done)
                    produce(pe, n, bank[n % ring]).then_inc(full, 1)

            def drain(eng, which):
                for n in range(count):
                    if not both or n % 2 == which:
                        eng.wait_ge(full, n + 1)
                        evacuate(eng, n, bank[n % ring]).then_inc(free[which if both else 0], 1)

            if vector:
                @block.vector
                def _(dve):
                    drain(dve, 0)
            if scalar:
                @block.scalar
                def _(act):
                    drain(act, 1)


def copy(eng, out, in_):
    return eng.activation(out, in_, ACT.Copy) if isinstance(eng, bass.BassScalarEngine) else eng.tensor_copy(out, in_)


def accumulate(pe, bank, terms):
    for i, (lhsT, rhs) in enumerate(terms):
        last = pe.matmul(bank, lhsT, rhs, start=(i == 0), stop=(i == len(terms) - 1))
    return last


def turn(nc, k, name, src, dst):
    def produce(pe, n, bank):
        for c in range(KD):
            t = pe.transpose(bank[:, c * P:(c + 1) * P], src[:, n, c * P:(c + 1) * P], k.ident[:, :])
        return t
    products(nc, name, NT, produce, lambda eng, n, bank: copy(
        eng, dst[:, :, n * P:(n + 1) * P], bank[:, :].rearrange("p (c t) -> p c t", c=KD)))


def unturn(nc, k, name, src, dst):
    def produce(pe, n, bank):
        for c in range(KD):
            t = pe.transpose(bank[:, c * P:(c + 1) * P], src[:, c, n * P:(n + 1) * P], k.ident[:, :])
        return t
    products(nc, name, NT, produce, lambda eng, n, bank: copy(eng, dst[:, n, :], bank[:, :]))


def load(nc, name, pairs):
    with ExitStack() as ctx:
        landed = Mem(nc, ctx, name).sem("landed")
        with nc.Block() as block:
            @block.sync
            def _(sp):
                for out, in_ in pairs:
                    sp.dma_start(out, in_).then_inc(landed, 16)
                sp.wait_ge(landed, 16 * len(pairs))


def layernorm(nc, k, name, x, out, extra=None):
    with ExitStack() as ctx:
        m = Mem(nc, ctx, name)
        stats = m.sb("stats", [P, NT, 6])
        mv = m.sb("mv", [P, NT, 2])
        v = m.sb("v", [P, NT])
        r = m.sb("r", [P, NT])
        w = m.sb("w", [P, NT])
        steps, var, root = m.sem("steps"), m.sem("var"), m.sem("root")
        with nc.Block() as block:
            @block.vector
            def _(dve):
                c = Chain(dve, steps)
                for i in range(NT):
                    c.mark(dve.bn_stats(stats[:, i, :], x[:, i, :]))
                dve.wait_ge(steps, c.n)
                for i in range(NT):
                    c.mark(dve.bn_aggr(mv[:, i, :], stats[:, i, :]))
                dve.wait_ge(steps, c.n)
                dve.tensor_scalar(v[:, :], mv[:, :, 1], 1e-5, None, ALU.add).then_inc(var, 1)
                dve.wait_ge(root, 1)
                c.then(dve.reciprocal(r[:, :], r[:, :]))
                dve.wait_ge(var, 1)
                c.then(dve.tensor_tensor(w[:, :], r[:, :], r[:, :], ALU.mult))
                c.then(dve.tensor_tensor(w[:, :], w[:, :], v[:, :], ALU.mult))
                c.then(dve.tensor_scalar(w[:, :], w[:, :], -0.5, 1.5, ALU.mult, ALU.add))
                c.then(dve.tensor_tensor(r[:, :], r[:, :], w[:, :], ALU.mult))
                for i in range(NT):
                    c.mark(dve.tensor_scalar(out[:, i, :], x[:, i, :], mv[:, i, 0:1], r[:, i:i + 1], ALU.subtract, ALU.mult))
                if extra is not None:
                    dve.wait_ge(steps, c.n)
                    for n, (row, op) in enumerate(zip(extra, (ALU.mult, ALU.add))):
                        for i in range(NT):
                            c.mark(dve.tensor_tensor(out[:, i, :], out[:, i, :], row[:, :], op))
                        dve.wait_ge(steps, c.n)

            @block.scalar
            def _(act):
                act.wait_ge(var, 1)
                act.activation(r[:, :], v[:, :], ACT.Sqrt).then_inc(root, 1)


def softmax_rows(nc, name, x, rows, width, scale):
    with ExitStack() as ctx:
        m = Mem(nc, ctx, name)
        top = m.sb("top", [P, rows])
        total = m.sb("total", [P, rows])
        steps, raised, summed = m.sem("steps"), m.sem("raised"), m.sem("summed")
        with nc.Block() as block:
            @block.vector
            def _(dve):
                c = Chain(dve, steps)
                c.then(dve.tensor_reduce(top[:, :], x[:, :, :], AX.X, ALU.max))
                dve.tensor_scalar(top[:, :], top[:, :], -1.0, None, ALU.mult).then_inc(raised, 1)
                for i in range(rows):
                    dve.wait_ge(summed, i + 1)
                    c.then(dve.reciprocal(total[:, i:i + 1], total[:, i:i + 1]))
                    c.mark(dve.tensor_scalar(x[:, i, :], x[:, i, :], total[:, i:i + 1], scale, ALU.mult, ALU.mult))

            @block.scalar
            def _(act):
                act.wait_ge(raised, 1)
                for i in range(rows):
                    act.activation(x[:, i, :], x[:, i, :], ACT.Exp, bias=top[:, i:i + 1],
                                   accum_out=total[:, i:i + 1]).then_inc(summed, 1)


def chunks(w):
    return w.rearrange("(c p) n -> p c n", p=P)


def tile_terms(lhsT, rhs, n, kd=KD):
    return [(lhsT[:, c, n * P:(n + 1) * P], rhs[:, c, :]) for c in range(kd)]


def layer0_gnn(nc, k, a, x, xn, xt, sum_out):
    with ExitStack() as ctx:
        m = Mem(nc, ctx, "gnn0")
        adj = m.sb("adj", [P, NT, N])
        rs = m.sb("rs", [P, NT])
        adjacency(nc, k, adj, rs)
        w = m.sb("w", [P, KD, D])
        b = m.sb("b", [1, D])
        dw = m.sb("dw", [P, 4])
        cur = [m.sb(f"cur{i}", [P, NT, D]) for i in range(2)]
        acc = m.sb("acc", [P, NT, D])
        load(nc, "gnn0_load", [(w[:, :, :], chunks(a["L0_gnn_W"])), (b[:, :], a["L0_gnn_b"].rearrange("(a n) -> a n", a=1)),
                               (dw[:, :], a["L0_gnn_diffusion_weights"].rearrange("(a n) -> a n", a=1).broadcast_to([P, 4]))])
        products(nc, "gnn0_h", NT,
                 lambda pe, n, bank: accumulate(pe, bank[:, :], tile_terms(xt, w, n) + [(k.ones[0:1, :], b[:, :])]),
                 lambda eng, n, bank: copy(eng, cur[0][:, n, :], bank[:, :]))
        mixed, summed = m.sem("mixed"), m.sem("summed")
        for step in range(3):
            src, dst = cur[step % 2], cur[(step + 1) % 2]
            products(nc, f"gnn0_s{step}", NT,
                     lambda pe, n, bank: accumulate(pe, bank[:, :], tile_terms(adj, src, n, NT)),
                     lambda eng, n, bank: eng.activation(dst[:, n, :], bank[:, :], ACT.Copy, scale=rs[:, n:n + 1])
                     if isinstance(eng, bass.BassScalarEngine)
                     else eng.tensor_scalar(dst[:, n, :], bank[:, :], rs[:, n:n + 1], None, ALU.mult))
            with nc.Block() as block:
                @block.vector
                def _(dve):
                    flat = lambda z: z[:, :, :].rearrange("p t d -> p (t d)")
                    if step == 0:
                        dve.tensor_scalar(flat(acc), flat(src), dw[:, 0:1], None, ALU.mult).then_inc(summed, 1)
                        dve.wait_ge(summed, 1)
                    dve.scalar_tensor_tensor(flat(acc), flat(dst), dw[:, step + 1:step + 2], flat(acc), ALU.mult,
                                             ALU.add).then_inc(summed, 1)
                    if step == 2:
                        dve.wait_ge(summed, 4)
                        dve.scalar_tensor_tensor(flat(sum_out), flat(acc), 0.0, flat(x), ALU.max, ALU.add).then_inc(summed, 1)


def layer0_mix(nc, k, a, xn, xt, x1):
    with ExitStack() as ctx:
        m = Mem(nc, ctx, "mix0")
        w = m.sb("w", [P, 5, KD, D])
        q = m.sb("q", [P, NT, D])
        qt = m.sb("qt", [P, KD, N])
        kt = m.sb("kt", [P, KD, N])
        kk = m.sb("kk", [P, NT, D])
        v = m.sb("v", [P, NT, D])
        context = q[:, 0:KD, :]
        names = ("Wq", "Wk", "Wv", "W1", "W2")
        load(nc, "mix0_load", [(w[:, i, :, :], chunks(a[f"L0_mix_{s}"])) for i, s in enumerate(names)])
        wk = w[:, 1, :, :]
        products(nc, "mix0_q", NT, lambda pe, n, bank: accumulate(pe, bank[:, :], tile_terms(xt, w[:, 0, :, :], n)),
                 lambda eng, n, bank: copy(eng, q[:, n, :], bank[:, :]))

        def halves(out, lhs, rhs, name, extra=None):
            products(nc, name, 2 * KD,
                     lambda pe, n, bank: accumulate(pe, bank[:, :], [
                         (lhs[:, c, (n // 2) * P:(n // 2 + 1) * P], rhs[:, c, (n % 2) * D:(n % 2 + 1) * D]) for c in range(KD)]),
                     lambda eng, n, bank: copy(eng, out[:, n // 2, (n % 2) * D:(n % 2 + 1) * D], bank[:, :])
                     if extra is None else eng.tensor_tensor(
                         out[:, n // 2, (n % 2) * D:(n % 2 + 1) * D], bank[:, :],
                         extra[:, n // 2, (n % 2) * D:(n % 2 + 1) * D], ALU.add), scalar=extra is None)
        halves(kt, wk, xt, "mix0_k")
        products(nc, "mix0_v", NT, lambda pe, n, bank: accumulate(pe, bank[:, :], tile_terms(xt, w[:, 2, :, :], n)),
                 lambda eng, n, bank: copy(eng, v[:, n, :], bank[:, :]))
        softmax_rows(nc, "mix0_sq", q, NT, D, float(D) ** -0.5)
        softmax_rows(nc, "mix0_sk", kt, KD, N, 1.0)
        unturn(nc, k, "mix0_kk", kt, kk)
        turn(nc, k, "mix0_qt", q, qt)
        products(nc, "mix0_c", KD, lambda pe, n, bank: accumulate(pe, bank[:, :], [
            (kk[:, i, n * P:(n + 1) * P], v[:, i, :]) for i in range(NT)]),
                 lambda eng, n, bank: copy(eng, context[:, n, :], bank[:, :]))
        yt, zt = kt, qt
        halves(yt, context, qt, "mix0_a", extra=xt)
        halves(zt, w[:, 3, :, :], yt, "mix0_1")
        products(nc, "mix0_2", NT,
                 lambda pe, n, bank: (accumulate(pe, bank[:, :], tile_terms(zt, w[:, 4, :, :], n)), [
                     pe.matmul(bank[:, c * P:(c + 1) * P], yt[:, c, n * P:(n + 1) * P], k.ident[:, :], start=False,
                               stop=(c == KD - 1), skip_group_check=True) for c in range(KD)][-1])[1],
                 lambda eng, n, bank: eng.tensor_tensor(x1[:, n, :], bank[:, :], x1[:, n, :], ALU.add), scalar=False)


NE = 8
CAP = 256
FF = 1024
CT = CAP // P


def expert_choice(nc, k, a, xt, scores_t, picks, chosen_i, gate):
    with ExitStack() as ctx:
        m = Mem(nc, ctx, "pick")
        wg = m.sb("wg", [P, KD, NE])
        s = m.sb("s", [P, NT, NE])
        w = m.sb("w", [P, NT, NE])
        top = m.sb("top", [P, NT])
        st = m.sb("st", [NE, N])
        sb = m.sb("sb", [P, NE, N])
        junk = m.sb("junk", [P, N], BF16)
        spare = m.sb("spare", [P, 1])
        gt = m.sb("gt", [P, NT, NE])
        ge = m.sb("ge", [P, NT, NE])
        tie = m.sb("tie", [P, NT, NE])
        token = m.sb("token", [P, NT])
        slot_i = m.sb("slot_i", [P, NT * NE], I32)
        recs = m.sb("recs", [P, NT * NE, 2])
        idx = m.sb("idx", [P, 2, 8], I32)
        buf = m.sb("buf", [P, 2, 8, 2])
        back = m.sb("back", [P, NE, CT, 2])
        lg = m.ps("lg", [P, D])
        tp = m.ps("tp", [NE, N])
        loaded, logits, steps, exped, shifted, norm, turned = (m.sem(x) for x in (
            "loaded", "logits", "steps", "exped", "shifted", "norm", "turned"))
        copied, stored, spread, ranked, ready, staged, fetched, out = (m.sem(x) for x in (
            "copied", "stored", "spread", "ranked", "ready", "staged", "fetched", "out"))
        sent = [m.sem(f"sent{i}") for i in range(2)]
        with nc.Block() as block:
            @block.sync
            def _(sp):
                sp.dma_start(wg[:, :, :], chunks(a["L0_ffn_Wg"])).then_inc(loaded, 16)
                sp.wait_ge(copied, 2)
                sp.dma_start(scores_t, st[:, :]).then_inc(stored, 16)
                sp.wait_ge(stored, 16)
                for e in range(NE):
                    sp.dma_start(sb[:, e, :], scores_t[e:e + 1, :].broadcast_to([P, N])).then_inc(spread, 16)

            @block.tensor
            def _(pe):
                pe.wait_ge(loaded, 16)
                for i in range(NT):
                    t = accumulate(pe, lg[:, i * NE:(i + 1) * NE], [(xt[:, c, i * P:(i + 1) * P], wg[:, c, :]) for c in range(KD)])
                t.then_inc(logits, 1)
                pe.wait_ge(norm, 1)
                for i in range(NT):
                    t = pe.transpose(tp[:, i * P:(i + 1) * P], s[:, i, :], k.ident[:, :])
                t.then_inc(turned, 1)

            @block.scalar
            def _(act):
                act.wait_ge(shifted, 1)
                act.activation(w[:, :, :], s[:, :, :], ACT.Exp).then_inc(exped, 1)

            @block.vector
            def _(dve):
                c = Chain(dve, steps)
                wide = [P, NT, NE]
                dve.wait_ge(logits, 1)
                c.then(dve.tensor_copy(s[:, :, :].rearrange("p t e -> p (t e)"), lg[:, 0:NT * NE]))
                c.then(dve.tensor_reduce(top[:, :], s[:, :, :], AX.X, ALU.max))
                dve.tensor_tensor(s[:, :, :], s[:, :, :], top[:, :].unsqueeze(2).broadcast_to(wide), ALU.subtract).then_inc(shifted, 1)
                dve.wait_ge(exped, 1)
                c.then(dve.tensor_reduce(top[:, :], w[:, :, :], AX.X, ALU.add))
                c.then(dve.reciprocal(top[:, :], top[:, :]))
                dve.tensor_tensor(s[:, :, :], w[:, :, :], top[:, :].unsqueeze(2).broadcast_to(wide), ALU.mult).then_inc(norm, 1)
                dve.wait_ge(turned, 1)
                for h in range(2):
                    dve.tensor_copy(st[:, h * D:(h + 1) * D], tp[:, h * D:(h + 1) * D]).then_inc(copied, 1)
                c.mark(dve.memset(ge[:, 0, :], 0.0))
                c.mark(dve.memset(junk[:, :], 0.0))
                dve.wait_ge(norm, 1)
                for i in range(NT):
                    c.mark(dve.tensor_scalar(token[:, i:i + 1], k.lane[:, :], float(i * P), None, ALU.add))
                dve.wait_ge(steps, c.n)
                dve.wait_ge(spread, 16 * NE)
                with dve.Fori(0, NE) as e:
                    for i in range(NT):
                        mine = s[:, i, bass.ds(e, 1)]
                        lo, hi = i * P, (i + 1) * P
                        row = lambda x, n: sb[:, :, :].rearrange("p e n -> p (e n)")[:, bass.ds(e * N + x, n)]
                        if i:
                            dve.tensor_scalar(junk[:, 0:lo], row(0, lo), mine, 0.0, ALU.is_ge, ALU.add,
                                              accum_out=ge[:, i, bass.ds(e, 1)]).then_inc(ranked, 1)
                        else:
                            dve.tensor_copy(spare[:, :], k.lane[:, :]).then_inc(ranked, 1)
                        dve.tensor_scalar(junk[:, lo:N], row(lo, N - lo), mine, 0.0, ALU.is_gt, ALU.add,
                                          accum_out=gt[:, i, bass.ds(e, 1)]).then_inc(ranked, 1)
                        dve.wait_ge(ranked, 3 * NT * e + (3 * i + 2))
                        dve.scalar_tensor_tensor(junk[:, lo:hi], row(lo, P), mine, k.later[:, :], ALU.is_equal, ALU.mult,
                                                 accum_out=tie[:, i, bass.ds(e, 1)]).then_inc(ranked, 1)
                        dve.wait_ge(ranked, 3 * NT * e + (3 * i + 3))
                c.then(dve.tensor_tensor(gt[:, :, :], gt[:, :, :], ge[:, :, :], ALU.add))
                c.then(dve.tensor_tensor(gt[:, :, :], gt[:, :, :], tie[:, :, :], ALU.add))
                c.then(dve.tensor_scalar(w[:, 0, :], k.iotaf[:, 0:NE], float(N), None, ALU.mult))
                c.then(dve.tensor_tensor(gt[:, :, :], gt[:, :, :], w[:, 0:1, :].broadcast_to(wide), ALU.add))
                c.mark(dve.tensor_copy(slot_i[:, :], gt[:, :, :].rearrange("p t e -> p (t e)")))
                c.mark(dve.tensor_copy(recs[:, :, 0].rearrange("p (t e) -> p t e", t=NT), token[:, :].unsqueeze(2).broadcast_to(wide)))
                c.mark(dve.tensor_copy(recs[:, :, 1], s[:, :, :].rearrange("p t e -> p (t e)")))
                dve.wait_ge(steps, c.n)
                dve.sem_inc(ready, 1)

            @block.gpsimd
            def _(pool):
                pool.wait_ge(ready, 1)
                scatter(pool, picks, slot_i, recs, NT * NE, idx, buf, staged, sent, ready)
        with nc.Block() as block:
            @block.sync
            def _(sp):
                for t in range(CT):
                    sp.dma_start(back[:, :, t, :], picks.rearrange("(e t p) c -> p e t c", e=NE, p=P)[:, :, t, :]).then_inc(fetched, 16)

            @block.vector
            def _(dve):
                dve.wait_ge(fetched, 16 * CT)
                dve.tensor_copy(chosen_i[:, :, :], back[:, :, :, 0]).then_inc(out, 1)
                dve.tensor_copy(gate[:, :, :], back[:, :, :, 1]).then_inc(out, 1)


def experts(nc, k, a, rows, total, chosen_i, gate):
    with ExitStack() as ctx:
        m = Mem(nc, ctx, "moe")
        w1 = m.sb("w1", [P, 2, KD, FF])
        w2 = m.sb("w2", [P, 2, FF // P, D])
        b1 = m.sb("b1", [P, NE, FF // P])
        b2 = m.sb("b2", [1, 2, D])
        ex = m.sb("ex", [P, 2, CT, D])
        ext = m.sb("ext", [P, KD, CAP])
        hid = m.sb("hid", [P, FF // P, CAP])
        y = m.sb("y", [P, 2, CT, D])
        R = 4
        tb = [m.ps(f"tb{i}", [P, D]) for i in range(CT)]
        hb = [m.ps(f"hb{i}", [P, D]) for i in range(R)]
        ob = [m.ps(f"ob{i}", [P, D]) for i in range(CT)]
        w_in = [m.sem(f"w_in{i}") for i in range(2)]
        got = [m.sem(f"got{i}") for i in range(2)]
        added = [m.sem(f"added{i}") for i in range(CT)]
        b_in, y_free, turned, laid, hidden, act_done, summed, weighed = (m.sem(x) for x in (
            "b_in", "y_free", "turned", "laid", "hidden", "act_done", "summed", "weighed"))
        FT = FF // P
        with nc.Block() as block:
            @block.sync
            def _(sp):
                def weights(e, b):
                    sp.dma_start(w1[:, b, :, :], a["L0_ffn_W1"][bass.ds(e, 1), :, :].rearrange("a (c p) f -> p (a c) f", p=P)).then_inc(w_in[b], 16)
                    sp.dma_start(w2[:, b, :, :], a["L0_ffn_W2"][bass.ds(e, 1), :, :].rearrange("a (c p) f -> p (a c) f", p=P)).then_inc(w_in[b], 16)
                    sp.dma_start(b2[:, b, :], a["L0_ffn_b2"][bass.ds(e, 1), :]).then_inc(w_in[b], 16)
                sp.dma_start(b1[:, :, :], a["L0_ffn_b1"]).then_inc(b_in, 16)
                for b in range(2):
                    weights(b, b)
                with sp.Fori(1, NE // 2) as t:
                    for b in range(2):
                        sp.wait_ge(summed, CT * (2 * t) + (CT * (b - 1) + 1))
                        weights(2 * t + b, b)

            @block.gpsimd
            def _(pool):
                def gather(e):
                    if e >= 2:
                        pool.wait_ge(turned, CT * (e - 1))
                    for t in range(CT):
                        pool.indirect_dma_start(out=ex[:, e % 2, t, :], out_offset=None, in_=rows,
                                                in_offset=bass.IndirectOffsetOnAxis(ap=chosen_i[:, e, t:t + 1], axis=0)).then_inc(got[e % 2], 16)
                pool.sem_inc(y_free, 2)
                gather(0)
                for e in range(NE):
                    if e + 1 < NE:
                        gather(e + 1)
                    for t in range(CT):
                        pool.wait_ge(weighed, CT * e + t + 1 + CT)
                        if e and t == 0:
                            for o in range(CT):
                                pool.wait_ge(added[o], 16 * e)
                            pool.sem_inc(y_free, 1)
                        pool.indirect_dma_start(out=total, out_offset=bass.IndirectOffsetOnAxis(ap=chosen_i[:, e, t:t + 1], axis=0),
                                                in_=y[:, e % 2, t, :], in_offset=None, compute_op=ALU.add).then_inc(added[t], 16)
                for o in range(CT):
                    pool.wait_ge(added[o], 16 * NE)

            @block.tensor
            def _(pe):
                pe.sem_inc(hidden, 1)
                pe.sem_inc(summed, 1)
                with pe.Fori(0, NE // 2) as tt:
                    for b in range(2):
                        e = 2 * tt + b
                        pe.wait_ge(got[b], 16 * CT * (tt + 1))
                        pe.wait_ge(laid, CT * e + CT)
                        for t in range(CT):
                            for c in range(KD):
                                i = pe.transpose(tb[t][:, c * P:(c + 1) * P], ex[:, b, t, c * P:(c + 1) * P], k.ident[:, :])
                            i.then_inc(turned, 1)
                        pe.wait_ge(w_in[b], 48 * (tt + 1))
                        pe.wait_ge(laid, CT * e + 2 * CT)
                        for f in range(FT):
                            pe.wait_ge(act_done, FT * e + (f + 1))
                            accumulate(pe, hb[f % R][:, 0:CAP],
                                       [(w1[:, b, c, f * P:(f + 1) * P], ext[:, c, :]) for c in range(KD)]).then_inc(hidden, 1)
                        pe.wait_ge(act_done, FT * e + (FT + R))
                        for t in range(CT):
                            pe.wait_ge(weighed, CT * e + t + 1)
                            pe.matmul(ob[t][:, :], k.ones[0:1, :], b2[0:1, b, :], start=True, stop=False)
                            for f in range(FT):
                                i = pe.matmul(ob[t][:, :], hid[:, f, t * P:(t + 1) * P], w2[:, b, f, :], start=False, stop=(f == FT - 1))
                            i.then_inc(summed, 1)

            @block.vector
            def _(dve):
                dve.sem_inc(laid, CT)
                dve.sem_inc(weighed, CT)
                with dve.Fori(0, NE // 2) as tt:
                    for b in range(2):
                        e = 2 * tt + b
                        for t in range(CT):
                            dve.wait_ge(turned, CT * e + t + 1)
                            if t == 0:
                                dve.wait_ge(hidden, FT * e + 1)
                            dve.tensor_copy(ext[:, :, t * P:(t + 1) * P], tb[t][:, :].rearrange("p (c t) -> p c t", c=KD)).then_inc(laid, 1)
                        for t in range(CT):
                            dve.wait_ge(summed, CT * e + t + 2)
                            dve.wait_ge(y_free, e + 1)
                            dve.tensor_scalar(y[:, b, t, :], ob[t][:, :], gate[:, bass.ds(e, 1), t:t + 1].rearrange("p a b -> p (a b)"), None, ALU.mult).then_inc(weighed, 1)

            @block.scalar
            def _(act):
                act.wait_ge(b_in, 16)
                act.sem_inc(act_done, R)
                with act.Fori(0, NE // 2) as tt:
                    for b in range(2):
                        e = 2 * tt + b
                        for f in range(FT):
                            act.wait_ge(hidden, FT * e + f + 2)
                            if f == 0:
                                act.wait_ge(summed, CT * e + 1)
                            act.activation(hid[:, f, :], hb[f % R][:, 0:CAP], ACT.Gelu,
                                           bias=b1[:, bass.ds(e, 1), f:f + 1].rearrange("p a b -> p (a b)")).then_inc(act_done, 1)


def store(nc, name, pairs):
    load(nc, name, pairs)


def layer0_ffn(nc, k, a, x1, xn, xt):
    with ExitStack() as ctx:
        m = Mem(nc, ctx, "ffn0")
        chosen_i = m.sb("chosen_i", [P, NE, CT], I32)
        gate = m.sb("gate", [P, NE, CT])
        rows = nc.dram_tensor("expert_rows", (N, D), F32).ap()
        total = nc.dram_tensor("expert_total", (N, D), F32).ap()
        scores_t = nc.dram_tensor("expert_scores", (NE, N), F32).ap()
        picks = nc.dram_tensor("expert_picks", (NE * N, 2), F32).ap()
        layernorm(nc, k, "ln1", x1, xn)
        store(nc, "ffn0_store", [(chunks(rows), xn[:, :, :]), (chunks(total), x1[:, :, :])])
        turn(nc, k, "turn1", xn, xt)
        expert_choice(nc, k, a, xt, scores_t, picks, chosen_i, gate)
        experts(nc, k, a, rows, total, chosen_i, gate)
        load(nc, "ffn0_load", [(x1[:, :, :], chunks(total))])


LOT = 2
LOTS = NB // LOT
RING = 4


def gat_gather(pool, tables, indices, idx, bufs, staged, got, free):
    k, I = len(tables), 2 * RING

    def stage(n, i):
        for j, col in enumerate(indices):
            pool.tensor_copy(idx[:, i, j, :], col[:, bass.ds(LOT * n, LOT)]).then_inc(staged, 1)

    def fetch(i):
        for j, table in enumerate(tables):
            for u in range(LOT):
                pool.indirect_dma_start(out=bufs[j][:, i % RING, u, :], out_offset=None, in_=table,
                                        in_offset=bass.IndirectOffsetOnAxis(ap=idx[:, i, j, u:u + 1], axis=0)).then_inc(got[i % RING], 16)

    def step(n, i, more=True):
        pool.wait_ge(staged, k * n + k)
        pool.wait_ge(free, n + 1)
        if more:
            stage(n + 1, (i + 1) % I)
        fetch(i)
    stage(0, 0)
    with pool.Fori(0, LOTS // I - 1) as t:
        for i in range(I):
            step(I * t + i, i)
    for i in range(I):
        step(LOTS - I + i, i, i + 1 < I)


def gat_scores(nc, k, a, xl_t, xr_t, alpha, xt, x2):
    with ExitStack() as ctx:
        m = Mem(nc, ctx, "score")
        left = m.sb("left", [P, RING, LOT, D])
        right = m.sb("right", [P, RING, LOT, D])
        att = m.sb("att", [P, D])
        idx = m.sb("idx", [P, 2 * RING, 2, LOT], I32)
        loaded, staged, free, steps = (m.sem(x) for x in ("loaded", "staged", "free", "steps"))
        got = [m.sem(f"got{i}") for i in range(RING)]
        mix = Layer1Mix(nc, ctx, k, a, xt, x2)
        with nc.Block() as block:
            @block.sync
            def _(sp):
                sp.dma_start(att[:, :], a["L1_gnn_att"].rearrange("(a h) c -> a (h c)", a=1).broadcast_to([P, D])).then_inc(loaded, 16)
                mix.load(sp)

            @block.gpsimd
            def _(pool):
                mix.constants(pool)
                gat_gather(pool, [xl_t, xr_t], [k.src_i, k.dst_i], idx, [left, right], staged, got, free)

            @block.tensor
            def _(pe):
                mix.multiply(pe)

            @block.scalar
            def _(act):
                mix.evacuate(act)

            @block.vector
            def _(dve):
                dve.sem_inc(free, RING)
                dve.wait_ge(loaded, 16)

                flat = lambda x, b: x[:, b, :, :].rearrange("p u d -> p (u d)")

                def add(b, full):
                    dve.wait_ge(got[b], 16 * 2 * LOT * full)
                    dve.tensor_tensor(flat(left, b), flat(left, b), flat(right, b), ALU.add).then_inc(steps, 1)

                def rectify(b, added):
                    dve.wait_ge(steps, added)
                    dve.scalar_tensor_tensor(flat(right, b), flat(left, b), 0.2, flat(left, b), ALU.mult, ALU.max).then_inc(steps, 1)

                def weigh(b, rectified):
                    dve.wait_ge(steps, rectified)
                    dve.tensor_tensor(left[:, b, :, :], right[:, b, :, :], att[:, :].unsqueeze(1).broadcast_to([P, LOT, D]),
                                      ALU.mult).then_inc(steps, 1)

                def total(n, b, weighed):
                    dve.wait_ge(steps, weighed)
                    dve.tensor_reduce(alpha[:, bass.ds(n * (LOT * H8), LOT * H8)],
                                      flat(left, b).rearrange("p (q c) -> p q c", c=HC), AX.X, ALU.add).then_inc(free, 1)

                def lots(t, count):
                    for i in range(count):
                        n, b, last = RING * t + (i + 1), (i + 1) % RING, i
                        add(b, t + (1 + (i + 1) // RING))
                        weigh(last, 3 * n - 1)
                        rectify(b, 3 * n)
                        total(n - 1, last, 3 * n + 1)
                add(0, 1)
                rectify(0, 1)
                rings = LOTS // RING - 1
                with dve.Fori(0, rings // 2) as t:
                    lots(t, RING)
                mix.divide(dve)
                with dve.Fori(rings // 2, rings) as t:
                    lots(t, RING)
                lots(rings, RING - 1)
                weigh(RING - 1, 3 * LOTS - 1)
                total(LOTS - 1, RING - 1, 3 * LOTS)


def segment_softmax(nc, k, keys_t, alpha):
    with ExitStack() as ctx:
        m = Mem(nc, ctx, "seg")
        raw = m.sb("raw", [P, 3, SL])
        same_prev = m.sb("same_prev", [P, SL])
        same_next = m.sb("same_next", [P, SL])
        brk = m.sb("brk", [P, SL])
        last = m.sb("last", [P, SL])
        al = m.sb("al", [P, SL])
        run = m.sb("run", [P, SL])
        x = m.sb("x", [P, SL])
        fac = m.sb("fac", [P, 1])
        ends = m.sb("ends", [1, 2, P])
        st = m.sb("st", [1, P])
        carry_row = m.sb("carry_row", [1, P])
        carry = m.sb("carry", [P, 1])
        bank = [m.ps(f"bank{i}", [P, D]) for i in range(2)]
        rows = m.ps("rows", [1, D])
        col = m.ps("col", [P, D])
        loaded, steps, turned, brought, rowed, summed, colled, shifted, exped = (m.sem(x) for x in (
            "loaded", "steps", "turned", "brought", "rowed", "summed", "colled", "shifted", "exped"))
        lanes = alpha[:, :].rearrange("p (s i h) -> p i h s", s=SEG, i=BS)
        with nc.Block() as block:
            @block.sync
            def _(sp):
                for o in range(3):
                    v = keys_t[o:EP + o].rearrange("(s n) -> s n", s=SEG)
                    for h in range(H8):
                        sp.dma_start(raw[h * SEG:(h + 1) * SEG, o, :], v).then_inc(loaded, 16)

            @block.tensor
            def _(pe):
                pe.wait_ge(steps, 1)
                for i in range(BS):
                    if i >= 2:
                        pe.wait_ge(brought, i - 1)
                    pe.transpose(bank[i % 2][:, 0:P], x[:, i * P:(i + 1) * P], k.ident[:, :]).then_inc(turned, 1)
                for r in range(4):
                    pe.wait_ge(rowed, 3 * r + 1)
                    pe.transpose(rows[0:1, 0:P], run[:, SL - 1:SL] if r % 2 == 0 else run[:, 0:1], k.ident[:, :])
                    pe.transpose(rows[0:1, P:2 * P], fac[:, :], k.ident[:, :]).then_inc(summed, 1)
                    pe.wait_ge(rowed, 3 * r + 2)
                    pe.transpose(col[:, 0:1], carry_row[0:1, :], k.ident[0:1, 0:1]).then_inc(colled, 1)

            @block.scalar
            def _(act):
                act.wait_ge(shifted, 1)
                act.activation(al[:, :], al[:, :], ACT.Exp).then_inc(exped, 1)

            @block.vector
            def _(dve):
                c = Chain(dve, steps)
                c.mark(dve.tensor_copy(x[:, :].rearrange("p (i h s) -> p i h s", i=BS, h=H8), lanes))
                for i in range(BS):
                    dve.wait_ge(turned, i + 1)
                    dve.tensor_copy(al[:, i * P:(i + 1) * P], bank[i % 2][:, 0:P]).then_inc(brought, 1)
                dve.wait_ge(loaded, 16 * 3 * H8)
                v = [raw[:, o, :] for o in range(3)]
                c.mark(dve.tensor_tensor(same_prev[:, :], v[1], v[0], ALU.is_equal))
                c.then(dve.tensor_tensor(same_next[:, :], v[1], v[2], ALU.is_equal))
                c.mark(dve.tensor_scalar(brk[:, :], same_prev[:, :], -1.0, BIG, ALU.add, ALU.mult))
                c.then(dve.tensor_scalar(last[:, :], same_next[:, :], -1.0, 1.0, ALU.mult, ALU.add))
                dve.wait_ge(brought, BS)

                def recurrence(r, keepers, add, ops, start, back):
                    way = slice(None, None, -1) if back else slice(None)
                    c.then(dve.tensor_tensor_scan(run[:, way], keepers[:, way], add[:, way], start, *ops))
                    dve.tensor_reduce(fac[:, :], keepers[:, :], AX.X, ALU.min).then_inc(rowed, 1)
                    dve.wait_ge(summed, r + 1)
                    c.then(dve.tensor_copy(ends[:, :, :].rearrange("a b p -> a (b p)"), rows[0:1, 0:2 * P]))
                    first, over = (SEG - 1, slice(0, P - 1)) if back else (0, slice(1, P))
                    c.then(dve.memset(ends[0:1, 1, first::SEG], -BIG if ops[0] == ALU.add else 0.0))
                    c.then(dve.tensor_tensor_scan(st[0:1, way], ends[0:1, 1, way], ends[0:1, 0, way], start, *ops))
                    c.then(dve.tensor_copy(carry_row[0:1, over], st[0:1, 1:P] if back else st[0:1, 0:P - 1]))
                    dve.memset(carry_row[0:1, first::SEG], start).then_inc(rowed, 1)
                    dve.wait_ge(colled, r + 1)
                    dve.tensor_copy(carry[:, :], col[:, 0:1]).then_inc(rowed, 1)
                    dve.wait_ge(rowed, 3 * r + 3)
                    c.then(dve.tensor_tensor_scan(run[:, way], keepers[:, way], add[:, way], carry[:, :], *ops))

                linear = (ALU.mult, ALU.add)
                recurrence(0, brk, al, (ALU.add, ALU.max), -BIG, False)
                c.then(dve.tensor_tensor(x[:, :], last[:, :], run[:, :], ALU.mult))
                recurrence(1, same_next, x, linear, 0.0, True)
                dve.tensor_tensor(al[:, :], al[:, :], run[:, :], ALU.subtract).then_inc(shifted, 1)
                dve.wait_ge(exped, 1)
                recurrence(2, same_prev, al, linear, 0.0, False)
                c.then(dve.tensor_tensor(x[:, :], last[:, :], run[:, :], ALU.mult))
                recurrence(3, same_next, x, linear, 0.0, True)
                c.then(dve.tensor_scalar(run[:, :], run[:, :], 1e-16, None, ALU.max))
                c.then(dve.reciprocal(run[:, :], run[:, :]))
                c.then(dve.tensor_tensor(al[:, :], al[:, :], run[:, :], ALU.mult))
        turned, brought = m.sem("turned_b"), m.sem("brought_b")
        with nc.Block() as block:
            @block.tensor
            def _(pe):
                for i in range(BS):
                    if i >= 2:
                        pe.wait_ge(brought, i - 1)
                    pe.transpose(bank[i % 2][:, 0:P], al[:, i * P:(i + 1) * P], k.ident[:, :]).then_inc(turned, 1)

            @block.vector
            def _(dve):
                for i in range(BS):
                    dve.wait_ge(turned, i + 1)
                    dve.tensor_copy(lanes[:, i, :, :], bank[i % 2][:, 0:P].rearrange("p (h s) -> p h s", h=H8)).then_inc(brought, 1)


def gat_sum(nc, k, a, xl_t, alpha, xn, out):
    with ExitStack() as ctx:
        m = Mem(nc, ctx, "agg")
        left = m.sb("left", [P, RING, LOT, D])
        wx = m.sb("wx", [P, RING, LOT, D])
        to = m.sb("to", [P, RING, LOT, P])
        idx = m.sb("idx", [P, 2 * RING, 1, LOT], I32)
        zb = m.sb("zb", [P, D], BF16)
        bias = m.sb("bias", [P, D])
        neg = m.sb("neg", [P, 2, D])
        pos = m.sb("pos", [P, 2, D])
        acc = m.ps("acc", [P, NG * D])
        loaded, staged, free, ready, used, zeroed = (m.sem(x) for x in ("loaded", "staged", "free", "ready", "used", "zeroed"))
        steps, low, exped = (m.sem(x) for x in ("steps", "low", "exped"))
        got = [m.sem(f"got{i}") for i in range(RING)]
        with nc.Block() as block:
            @block.sync
            def _(sp):
                sp.dma_start(bias[:, :], a["L1_gnn_bias"].rearrange("(a n) -> a n", a=1).broadcast_to([P, D])).then_inc(loaded, 16)

            @block.gpsimd
            def _(pool):
                gat_gather(pool, [xl_t], [k.src_i], idx, [left], staged, got, free)

            @block.vector
            def _(dve):
                dve.memset(zb[:, :], 0.0).then_inc(zeroed, 1)
                dve.sem_inc(free, RING)
                with dve.Fori(0, LOTS // RING) as t:
                    for b in range(RING):
                        n = RING * t + b
                        dve.wait_ge(used, n + 1)
                        for u in range(LOT):
                            dve.tensor_scalar(to[:, b, u, :], k.iotaf[:, 0:P], k.local[:, bass.ds(LOT * n + u, 1)], None,
                                              ALU.is_equal).then_inc(ready, 1)
                        dve.wait_ge(got[b], 16 * LOT * (t + 1))
                        dve.tensor_tensor(wx[:, b, :, :].rearrange("p u (h c) -> p (u h) c", c=HC),
                                          left[:, b, :, :].rearrange("p u (h c) -> p (u h) c", c=HC),
                                          alpha[:, bass.ds(n * (LOT * H8), LOT * H8)].unsqueeze(2).broadcast_to([P, LOT * H8, HC]),
                                          ALU.mult).then_inc(free, 1)

            @block.tensor
            def _(pe):
                pe.wait_ge(zeroed, 1)
                pe.sem_inc(used, RING)
                for g in range(NG):
                    pe.matmul(acc[:, g * D:(g + 1) * D], k.ones_b[:, :], zb[:, :], start=True, stop=False, skip_group_check=True)
                with pe.Fori(0, LOTS // RING) as t:
                    groups = block_groups(nc, k, RING * LOT * t, RING * LOT)
                    for b in range(RING):
                        n = RING * t + b
                        for u in range(LOT):
                            g = groups[LOT * b + u]
                            if u == 0:
                                pe.wait_ge(ready, LOT * n + LOT)
                                pe.wait_ge(free, n + (RING + 1))
                            i = pe.matmul(acc[:, bass.ds(g, D)], to[:, b, u, :], wx[:, b, u, :], start=False, stop=False,
                                          skip_group_check=True)
                        i.then_inc(used, 1)
        with nc.Block() as block:
            @block.vector
            def _(dve):
                c = Chain(dve, steps)
                dve.wait_ge(loaded, 16)
                for g in range(NG):
                    b = g % 2
                    c.then(dve.tensor_tensor(pos[:, b, :], acc[:, g * D:(g + 1) * D], bias[:, :], ALU.add))
                    dve.tensor_scalar(neg[:, b, :], pos[:, b, :], 0.0, None, ALU.min).then_inc(low, 1)
                    c.then(dve.tensor_scalar(pos[:, b, :], pos[:, b, :], 0.0, -1.0, ALU.max, ALU.add))
                    c.then(dve.tensor_tensor(pos[:, b, :], pos[:, b, :], xn[:, g, :], ALU.add))
                    c.then(dve.tensor_tensor(pos[:, b, :], pos[:, b, :], out[:, g, :], ALU.add))
                    dve.wait_ge(exped, g + 1)
                    c.then(dve.tensor_tensor(out[:, g, :], pos[:, b, :], neg[:, b, :], ALU.add))

            @block.scalar
            def _(act):
                for g in range(NG):
                    act.wait_ge(low, g + 1)
                    act.activation(neg[:, g % 2, :], neg[:, g % 2, :], ACT.Exp).then_inc(exped, 1)


def layer1_gnn(nc, k, a, keys_t, xn, xt, x2):
    with ExitStack() as ctx:
        m = Mem(nc, ctx, "gat")
        alpha = m.sb("alpha", [P, NB * H8])
        xl_t = nc.dram_tensor("gat_left", (N, D), F32).ap()
        xr_t = nc.dram_tensor("gat_right", (N, D), F32).ap()
        with ExitStack() as inner:
            mi = Mem(nc, inner, "gatp")
            w = mi.sb("w", [P, 2, KD, D])
            y = mi.sb("y", [P, 2, NT, D])
            load(nc, "gat_load", [(w[:, 0, :, :], chunks(a["L1_gnn_W_l"])), (w[:, 1, :, :], chunks(a["L1_gnn_W_r"]))])
            products(nc, "gat_p", 2 * NT,
                     lambda pe, n, bank: accumulate(pe, bank[:, :], tile_terms(xt, w[:, n // NT, :, :], n % NT)),
                     lambda eng, n, bank: copy(eng, y[:, n // NT, n % NT, :], bank[:, :]))
            store(nc, "gat_store", [(chunks(xl_t), y[:, 0, :, :]), (chunks(xr_t), y[:, 1, :, :])])
        gat_scores(nc, k, a, xl_t, xr_t, alpha, xt, x2)
        segment_softmax(nc, k, keys_t, alpha)
        gat_sum(nc, k, a, xl_t, alpha, xn, x2)


NH = 16
HD = D // NH


class Ring:

    def __init__(self, m, ring):
        self.bank = [m.ps(f"bank{i}", [P, D]) for i in range(ring)]
        self.full, self.free, self.made, self.brought = m.sem("full"), m.sem("free"), 0, 0

    def make(self, pe, count, product):
        for n in range(count):
            if self.made >= len(self.bank):
                pe.wait_ge(self.free, self.made - len(self.bank) + 1)
            product(pe, n, self.bank[self.made % len(self.bank)]).then_inc(self.full, 1)
            self.made += 1

    def settle(self, pe):
        pe.wait_ge(self.free, self.made)

    def bring(self, act, count, out):
        for n in range(count):
            act.wait_ge(self.full, self.brought + 1)
            out(act, n, self.bank[self.brought % len(self.bank)]).then_inc(self.free, 1)
            self.brought += 1


class Layer1Mix:
    EVACUATED = 2 * KD + 2 * NT + KD + NT * KD

    def __init__(self, nc, ctx, k, a, xt, x2):
        m = Mem(nc, ctx, "mix1")
        self.k, self.a, self.xt, self.x2 = k, a, xt, x2
        self.w = m.sb("w", [P, 4, KD, D])
        self.bias = m.sb("bias", [1, D])
        self.qt = m.sb("qt", [P, KD, N])
        self.kk = m.sb("kk", [P, NT, D])
        self.v = m.sb("v", [P, NT, D + 1])
        self.kv = m.sb("kv", [P, KD, P + 4])
        self.den = m.sb("den", [P, NT, NH])
        self.pr, self.pt = self.kk, self.qt
        self.ring = Ring(m, 4)
        self.landed, self.laid, self.steps, self.divided = (m.sem(x) for x in ("landed", "laid", "steps", "divided"))

    def load(self, sp):
        w, a = self.w, self.a
        for i in range(3):
            sp.dma_start(w[:, i, :, :], chunks(a["L1_mix_qkv_weight"])[:, :, i * D:(i + 1) * D]).then_inc(self.landed, 16)
        sp.dma_start(w[:, 3, :, :], chunks(a["L1_mix_proj_weight"])).then_inc(self.landed, 16)
        sp.dma_start(self.bias[:, :], a["L1_mix_proj_bias"].rearrange("(a n) -> a n", a=1)).then_inc(self.landed, 16)

    def constants(self, pool):
        pool.memset(self.v[:, :, D:D + 1], 1.0).then_inc(self.laid, 1)
        pool.memset(self.kv[:, :, :], 0.0).then_inc(self.laid, 1)

    def multiply(self, pe):
        w, xt, qt, kk, v, kv, k, ring = self.w, self.xt, self.qt, self.kk, self.v, self.kv, self.k, self.ring

        def sums(pe, n, bank):
            here = slice(n * P, (n + 1) * P)
            for i in range(NT):
                pe.matmul(bank[:, 0:P], kk[:, i, here], v[:, i, here], start=(i == 0), stop=(i == NT - 1))
            for i in range(NT):
                t = pe.matmul(bank[:, P:P + 1], kk[:, i, here], v[:, i, D:D + 1], start=(i == 0), stop=(i == NT - 1))
            return t

        def turned(pe, n, bank):
            for c in range(KD):
                t = pe.transpose(bank[:, c * P:(c + 1) * P], self.pr[:, n, c * P:(c + 1) * P], k.ident[:, :])
            return t
        pe.wait_ge(self.landed, 16 * 5)
        ring.make(pe, 2 * KD, lambda pe, n, bank: accumulate(pe, bank[:, :], [
            (w[:, 0, c, (n // 2) * P:(n // 2 + 1) * P], xt[:, c, (n % 2) * D:(n % 2 + 1) * D]) for c in range(KD)]))
        ring.make(pe, 2 * NT, lambda pe, n, bank: accumulate(pe, bank[:, :], tile_terms(xt, w[:, 1 + n % 2, :, :], n // 2)))
        ring.settle(pe)
        pe.wait_ge(self.laid, 1)
        ring.make(pe, KD, sums)
        ring.settle(pe)
        ring.make(pe, NT * KD, lambda pe, n, bank: pe.matmul(
            bank[:, 0:P + 4], qt[:, n % KD, (n // KD) * P:(n // KD + 1) * P], kv[:, n % KD, :], start=True, stop=True))
        pe.wait_ge(self.divided, NT)
        ring.make(pe, NT, turned)
        ring.settle(pe)
        ring.make(pe, NT, lambda pe, n, bank: accumulate(pe, bank[:, :], tile_terms(self.pt, w[:, 3, :, :], n) + [
            (k.ones[0:1, :], self.bias[:, :]), (k.ident[:, :], self.x2[:, n, :])]))

    def evacuate(self, act):
        ring, kv, den, pr = self.ring, self.kv, self.den, self.pr

        def heads(act, n, bank):
            for h in range(P // HD):
                here = slice(h * HD, (h + 1) * HD)
                act.activation(kv[here, n, here], bank[here, here], ACT.Copy)
                i = act.activation(kv[here, n, P + h:P + h + 1], bank[here, P:P + 1], ACT.Copy)
            return i

        def attended(act, n, bank):
            i, g = n // KD, n % KD
            act.activation(den[:, i, 4 * g:4 * g + 4], bank[:, P:P + 4], ACT.Copy)
            return act.activation(pr[:, i, g * P:(g + 1) * P], bank[:, 0:P], ACT.Copy)
        ring.bring(act, 2 * KD, lambda act, n, bank: act.activation(
            self.qt[:, n // 2, (n % 2) * D:(n % 2 + 1) * D], bank[:, :], ACT.Relu))
        ring.bring(act, 2 * NT, lambda act, n, bank: act.activation(self.kk[:, n // 2, :], bank[:, :], ACT.Relu) if n % 2 == 0
                   else act.activation(self.v[:, n // 2, 0:D], bank[:, :], ACT.Copy))
        act.wait_ge(self.laid, 2)
        ring.bring(act, KD, heads)
        ring.bring(act, NT * KD, attended)
        ring.bring(act, NT, lambda act, n, bank: act.activation(
            self.pt[:, :, n * P:(n + 1) * P], bank[:, :].rearrange("p (c t) -> p c t", c=KD), ACT.Copy))
        ring.bring(act, NT, lambda act, n, bank: act.activation(self.x2[:, n, :], bank[:, :], ACT.Copy))

    def divide(self, dve):
        den = self.den
        c = Chain(dve, self.steps)
        dve.wait_ge(self.ring.free, self.EVACUATED)
        c.then(dve.tensor_scalar(den[:, :, :], den[:, :, :], 1e-15, None, ALU.add))
        c.then(dve.reciprocal(den[:, :, :], den[:, :, :]))
        for i in range(NT):
            heads = self.pr[:, i, :].rearrange("p (h c) -> p h c", c=HD)
            dve.tensor_tensor(heads, heads, den[:, i, :].unsqueeze(2).broadcast_to([P, NH, HD]), ALU.mult).then_inc(self.divided, 1)


T = 64
DH = P
GRID = 16
CL = 8
BT = 32
LB = P // BT
NL = (T * BT + N) // P
NBK = NL * LB
W_UP, W_BASE, W_SLOPE, W_SCALE = D, 2 * D, 2 * D + GRID, 2 * D + 2 * GRID
ROW = W_SCALE + 4


def sign(c, dve, x, scratch, out):
    c.then(dve.tensor_scalar(scratch, x, 0.0, None, ALU.is_lt))
    c.then(dve.scalar_tensor_tensor(out, x, 0.0, scratch, ALU.is_gt, ALU.subtract))


def tile_signatures(nc, k, table, sig):
    with ExitStack() as ctx:
        m = Mem(nc, ctx, "sig")
        G = 4
        w = m.sb("w", [P, 2, G, D])
        sums = m.sb("sums", [P, T * KD])
        scratch = m.sb("scratch", [P, T * KD])
        csum = m.sb("csum", [P, CL, KD])
        cneg = m.sb("cneg", [P, CL, KD])
        got = [m.sem(f"got{i}") for i in range(2)]
        read, steps = m.sem("read"), m.sem("steps")
        v = table.rearrange("(t p) r -> p t r", p=P)
        with nc.Block() as block:
            @block.sync
            def _(sp):
                for b in range(2):
                    sp.dma_start(w[:, b, :, :], v[:, G * b:G * b + G, 0:D]).then_inc(got[b], 16)
                with sp.Fori(1, T // G // 2) as t:
                    for b in range(2):
                        sp.wait_ge(read, 2 * t + b - 1)
                        sp.dma_start(w[:, b, :, :], v[:, bass.ds((2 * t + b) * G, G), 0:D]).then_inc(got[b], 16)

            @block.vector
            def _(dve):
                c = Chain(dve, steps)
                with dve.Fori(0, T // G // 2) as t:
                    for b in range(2):
                        dve.wait_ge(got[b], 16 * t + 16)
                        dve.tensor_reduce(sums[:, bass.ds((2 * t + b) * (G * KD), G * KD)],
                                          w[:, b, :, :].rearrange("p g (c h) -> p (g c) h", h=DH), AX.X, ALU.add).then_inc(read, 1)
                dve.wait_ge(read, T // G)
                sign(c, dve, sums[:, :], scratch[:, :], sums[:, :])
                c.mark(dve.tensor_copy(sig[:, :, 0:T], sums[:, :].rearrange("p (t c) -> p c t", c=KD)))
                c.then(dve.tensor_reduce(csum[:, :, :], sums[:, :].rearrange("p (g u c) -> p g c u", g=CL, c=KD), AX.X, ALU.add))
                sign(c, dve, csum[:, :, :], cneg[:, :, :], csum[:, :, :])
                c.mark(dve.tensor_copy(sig[:, :, T:T + CL], csum[:, :, :].rearrange("p g c -> p c g")))


def route(nc, k, xt, sig, token_t, slot_i, weight_i, token_i):
    with ExitStack() as ctx:
        m = Mem(nc, ctx, "route")
        st = m.sb("st", [P, KD, N], BF16)
        neg = m.sb("neg", [P, KD, N], BF16)
        sc = m.sb("sc", [P, NT, T + CL])
        top = m.sb("top", [P, NT])
        best = m.sb("best", [P, NT])
        one = m.sb("one", [P, NT, T])
        w = m.sb("w", [P, NT, T])
        oneb = m.sb("oneb", [P, NT, T], BF16)
        cnt = m.sb("cnt", [P, T], I32)
        nblk = m.sb("nblk", [P, T])
        end = m.sb("end", [P, T])
        start = m.sb("start", [P, T])
        past = m.sb("past", [P, NBK, T])
        tile_of = m.sb("tile_of", [P, NBK])
        rows = m.sb("rows", [P, NT, 2], I32)
        zero = m.sb("zero", [P, 2 * NL], I32)
        lot = m.sb("lot", [P, NL, 2], I32)
        sb_ = [m.ps(f"s{i}", [P, D]) for i in range(2)]
        rank = m.ps("rank", [P, D])
        tot = m.ps("tot", [P, D])
        steps, signed, scored, hot, ranked, zeroed, filled, slotted, sent, back = (m.sem(x) for x in (
            "steps", "signed", "scored", "hot", "ranked", "zeroed", "filled", "slotted", "sent", "back"))
        wide, cwide = [P, NT, T], [P, NT, CL]
        with nc.Block() as block:
            @block.sync
            def _(sp):
                sp.wait_ge(zeroed, 1)
                sp.dma_start(token_t.rearrange("(p l) c -> p (l c)", p=P), zero[:, :]).then_inc(filled, 16)
                sp.wait_ge(sent, 16 * NT)
                sp.dma_start(lot[:, :, :], token_t.rearrange("(l p) c -> p l c", p=P)).then_inc(back, 16)

            @block.gpsimd
            def _(pool):
                pool.wait_ge(filled, 16)
                pool.wait_ge(slotted, 1)
                for i in range(NT):
                    pool.indirect_dma_start(out=token_t, out_offset=bass.IndirectOffsetOnAxis(ap=slot_i[:, i:i + 1], axis=0),
                                            in_=rows[:, i, :], in_offset=None).then_inc(sent, 16)
                pool.wait_ge(sent, 16 * NT)

            @block.tensor
            def _(pe):
                pe.wait_ge(signed, 1)
                for i in range(NT):
                    o = (i % 4) * (T + CL)
                    t = accumulate(pe, sb_[i // 4][:, o:o + T + CL], [(st[:, c, i * P:(i + 1) * P], sig[:, c, :]) for c in range(KD)])
                t.then_inc(scored, 1)
                pe.wait_ge(hot, 1)
                for i in range(NT):
                    t = accumulate(pe, rank[:, i * T:(i + 1) * T],
                                   [(k.ones_b[:, :], oneb[:, j, :]) for j in range(i)] + [(k.before_b[:, :], oneb[:, i, :])])
                t = accumulate(pe, tot[:, 0:T], [(k.ones_b[:, :], oneb[:, j, :]) for j in range(NT)])
                t.then_inc(ranked, 1)

            @block.vector
            def _(dve):
                c = Chain(dve, steps)
                dve.memset(zero[:, :], 0).then_inc(zeroed, 1)
                c.then(dve.tensor_scalar(neg[:, :, :], xt, 0.0, None, ALU.is_lt))
                c.then(dve.tensor_scalar(st[:, :, :], xt, 0.0, None, ALU.is_gt))
                dve.tensor_tensor(st[:, :, :], st[:, :, :], neg[:, :, :], ALU.subtract).then_inc(signed, 1)
                dve.wait_ge(scored, 1)
                for h in range(2):
                    c.mark(dve.tensor_copy(sc[:, 4 * h:4 * h + 4, :].rearrange("p i s -> p (i s)"), sb_[h][:, 0:4 * (T + CL)]))
                dve.wait_ge(steps, c.n)

                def first_best(x, width, shape, out):
                    c.then(dve.tensor_reduce(top[:, :], x, AX.X, ALU.max))
                    c.then(dve.tensor_tensor(w[:, :, 0:width], x, top[:, :].unsqueeze(2).broadcast_to(shape), ALU.is_equal))
                    c.then(dve.tensor_scalar(w[:, :, 0:width], w[:, :, 0:width], -1000.0, 1000.0, ALU.mult, ALU.add))
                    c.then(dve.tensor_tensor(w[:, :, 0:width], w[:, :, 0:width],
                                             k.iotaf[:, 0:width].unsqueeze(1).broadcast_to(shape), ALU.add))
                    c.then(dve.tensor_reduce(out, w[:, :, 0:width], AX.X, ALU.min))
                first_best(sc[:, :, T:T + CL], CL, cwide, best[:, :])
                c.then(dve.tensor_tensor(w[:, :, 0:CL], k.iotaf[:, 0:CL].unsqueeze(1).broadcast_to(cwide),
                                         best[:, :].unsqueeze(2).broadcast_to(cwide), ALU.is_equal))
                c.then(dve.tensor_scalar(w[:, :, 0:CL], w[:, :, 0:CL], -1.0, 10000.0, ALU.add, ALU.mult))
                for i in range(NT):
                    c.mark(dve.tensor_tensor(one[:, i, :].rearrange("p (g u) -> p g u", g=CL), sc[:, i, 0:T].rearrange("p (g u) -> p g u", g=CL),
                                             w[:, i, 0:CL].unsqueeze(2).broadcast_to([P, CL, T // CL]), ALU.add))
                dve.wait_ge(steps, c.n)
                first_best(one[:, :, :], T, wide, best[:, :])
                c.then(dve.tensor_tensor(one[:, :, :], k.iotaf[:, 0:T].unsqueeze(1).broadcast_to(wide),
                                         best[:, :].unsqueeze(2).broadcast_to(wide), ALU.is_equal))
                dve.tensor_copy(oneb[:, :, :], one[:, :, :]).then_inc(hot, 1)
                dve.wait_ge(ranked, 1)
                c.then(dve.tensor_scalar(cnt[:, :], tot[:, 0:T], float(BT - 1), None, ALU.add))
                c.then(dve.tensor_scalar(cnt[:, :], cnt[:, :], BT.bit_length() - 1, None, ALU.arith_shift_right))
                c.then(dve.tensor_copy(nblk[:, :], cnt[:, :]))
                c.then(dve.tensor_tensor_scan(end[:, :], nblk[:, :], k.ones[:, 0:T], 0.0, ALU.add, ALU.mult))
                c.then(dve.tensor_tensor(start[:, :], end[:, :], nblk[:, :], ALU.subtract))
                c.then(dve.tensor_scalar(start[:, :], start[:, :], float(BT), None, ALU.mult))
                c.then(dve.tensor_tensor(w[:, :, :], rank[:, 0:NT * T].rearrange("p (i t) -> p i t", t=T),
                                         start[:, :].unsqueeze(1).broadcast_to(wide), ALU.add))
                c.then(dve.tensor_tensor(w[:, :, :], w[:, :, :], one[:, :, :], ALU.mult))
                c.then(dve.tensor_reduce(top[:, :], w[:, :, :], AX.X, ALU.add))
                c.mark(dve.tensor_copy(slot_i[:, :], top[:, :]))
                c.mark(dve.memset(rows[:, :, 1], 0))
                for i in range(NT):
                    c.mark(dve.tensor_scalar(rows[:, i, 0:1], k.lane[:, :], float(i * P), None, ALU.add))
                dve.wait_ge(steps, c.n)
                dve.sem_inc(slotted, 1)
                c.then(dve.tensor_tensor(past[:, :, :], k.iotaf[:, 0:NBK].unsqueeze(2).broadcast_to([P, NBK, T]),
                                         end[:, :].unsqueeze(1).broadcast_to([P, NBK, T]), ALU.is_ge))
                c.then(dve.tensor_reduce(tile_of[:, :], past[:, :, :], AX.X, ALU.add))
                c.then(dve.tensor_scalar(tile_of[:, :], tile_of[:, :], float(T - 1), float(P), ALU.min, ALU.mult))
                c.then(dve.tensor_scalar(weight_i[:, :], tile_of[:, :], k.lane[:, :], None, ALU.add))
                dve.wait_ge(back, 16)
                c.then(dve.tensor_copy(token_i[:, :], lot[:, :, 0]))


def tile_ffn(nc, k, table, rows_t, y_t, weight_i, token_i):
    with ExitStack() as ctx:
        m = Mem(nc, ctx, "tile")
        w = m.sb("w", [P, 2, LB, ROW])
        x = m.sb("x", [P, 2, D])
        xt = m.sb("xt", [P, 2, KD, P])
        hn = m.sb("hn", [P, 2, P])
        s = m.sb("s", [P, P])
        r = m.sb("r", [P, P])
        cell = m.sb("cell", [P, P])
        one = m.sb("one", [P, P, GRID])
        pick = m.sb("pick", [P, P, GRID])
        base = m.sb("base", [P, P])
        slope = m.sb("slope", [P, P])
        hs = m.sb("hs", [P, 2, P])
        y = m.sb("y", [P, 2, D])
        idx = m.sb("idx", [P, 2, LB + 1], I32)
        tb = [m.ps(f"tb{i}", [P, D]) for i in range(2)]
        hb = [m.ps(f"hb{i}", [P, D]) for i in range(2)]
        yb = [m.ps(f"yb{i}", [P, D]) for i in range(2)]
        got = [m.sem(f"got{i}") for i in range(2)]
        stored = [m.sem(f"stored{i}") for i in range(2)]
        staged, turned, laid, hidden, squashed, splined, summed, brought, y_free, steps = (m.sem(x) for x in (
            "staged", "turned", "laid", "hidden", "squashed", "splined", "summed", "brought", "y_free", "steps"))
        with nc.Block() as block:
            @block.gpsimd
            def _(pool):
                def stage(n, b):
                    pool.tensor_copy(idx[:, b, 0:LB], weight_i[:, bass.ds(LB * n, LB)]).then_inc(staged, 1)
                    pool.tensor_copy(idx[:, b, LB:LB + 1], token_i[:, bass.ds(n, 1)]).then_inc(staged, 1)

                def fetch(b):
                    pool.indirect_dma_start(out=x[:, b, :], out_offset=None, in_=rows_t,
                                            in_offset=bass.IndirectOffsetOnAxis(ap=idx[:, b, LB:LB + 1], axis=0)).then_inc(got[b], 16)
                    for u in range(LB):
                        pool.indirect_dma_start(out=w[:, b, u, :], out_offset=None, in_=table,
                                                in_offset=bass.IndirectOffsetOnAxis(ap=idx[:, b, u:u + 1], axis=0)).then_inc(got[b], 16)
                stage(0, 0)
                pool.wait_ge(staged, 2)
                stage(1, 1)
                fetch(0)
                with pool.Fori(0, NL // 2 - 1) as t:
                    for b in range(2):
                        n = 2 * t + b
                        pool.wait_ge(staged, 2 * n + 4)
                        pool.wait_ge(got[b], 16 * (LB + 1) * (t + 1))
                        pool.wait_ge(summed, n + 2)
                        stage(n + 2, b)
                        fetch(1 - b)
                pool.wait_ge(staged, 2 * NL)
                pool.wait_ge(summed, NL)
                fetch(1)

            @block.tensor
            def _(pe):
                pe.sem_inc(hidden, 2)
                pe.sem_inc(summed, 2)

                def down(n, b, t):
                    pe.wait_ge(got[b], 16 * (LB + 1) * (t + 1))
                    pe.wait_ge(laid, n + 1)
                    for c in range(KD):
                        i = pe.transpose(tb[b][:, c * P:(c + 1) * P], x[:, b, c * P:(c + 1) * P], k.ident[:, :])
                    i.then_inc(turned, 1)
                    pe.wait_ge(laid, n + 3)
                    pe.wait_ge(squashed, n + 1)
                    for u in range(LB):
                        i = accumulate(pe, hb[b][:, u * BT:(u + 1) * BT], [
                            (w[:, b, u, c * P:(c + 1) * P], xt[:, b, c, u * BT:(u + 1) * BT]) for c in range(KD)])
                    i.then_inc(hidden, 1)

                def up(n, b):
                    pe.wait_ge(splined, n + 3)
                    pe.wait_ge(brought, n + 1)
                    for u in range(LB):
                        i = pe.matmul(yb[b][u * BT:(u + 1) * BT, :], hs[:, b, u * BT:(u + 1) * BT], w[:, b, u, W_UP:W_UP + D],
                                      start=True, stop=True, tile_position=(0, u * BT))
                    i.then_inc(summed, 1)
                down(0, 0, 0)
                with pe.Fori(0, NL // 2 - 1) as t:
                    down(2 * t + 1, 1, t)
                    up(2 * t, 0)
                    down(2 * t + 2, 0, t + 1)
                    up(2 * t + 1, 1)
                down(NL - 1, 1, NL // 2 - 1)
                up(NL - 2, 0)
                up(NL - 1, 1)

            @block.scalar
            def _(act):
                for q in (laid, squashed, brought):
                    act.sem_inc(q, 2)

                def into(n, b):
                    act.wait_ge(turned, n + 1)
                    act.wait_ge(hidden, n + 1)
                    act.activation(xt[:, b, :, :].rearrange("p c t -> p (c t)"), tb[b][:, :], ACT.Copy).then_inc(laid, 1)
                    act.wait_ge(hidden, n + 3)
                    act.wait_ge(splined, n + 1)
                    act.activation(hn[:, b, :], hb[b][:, 0:P], ACT.Sigmoid).then_inc(squashed, 1)

                def out(n, b):
                    act.wait_ge(summed, n + 3)
                    act.wait_ge(y_free, n + 1)
                    act.activation(y[:, b, :], yb[b][:, :], ACT.Copy).then_inc(brought, 1)
                into(0, 0)
                with act.Fori(0, NL // 2 - 1) as t:
                    into(2 * t + 1, 1)
                    out(2 * t, 0)
                    into(2 * t + 2, 0)
                    out(2 * t + 1, 1)
                into(NL - 1, 1)
                out(NL - 2, 0)
                out(NL - 1, 1)

            @block.vector
            def _(dve):
                dve.sem_inc(splined, 2)
                grid = k.iotaf[:, 0:GRID].unsqueeze(1).broadcast_to([P, P, GRID])
                spread = lambda z: z.unsqueeze(2).broadcast_to([P, P, GRID])
                with dve.Fori(0, NL // 2) as t:
                    for b in range(2):
                        n = 2 * t + b
                        STEPS = 12 + 2 * LB
                        c = Chain(dve, steps, STEPS * n)
                        weights = lambda u, o: w[:, b, u, o:o + GRID].unsqueeze(1).broadcast_to([P, BT, GRID])
                        blk = lambda z, u: z[:, u * BT:(u + 1) * BT]
                        dve.wait_ge(squashed, n + 3)
                        c.then(dve.tensor_scalar(s[:, :], hn[:, b, :], float(GRID), None, ALU.mult))
                        c.then(dve.tensor_scalar(r[:, :], s[:, :], 8388608.0, None, ALU.add))
                        c.then(dve.tensor_scalar(r[:, :], r[:, :], 8388608.0, None, ALU.subtract))
                        c.then(dve.tensor_tensor(cell[:, :], r[:, :], s[:, :], ALU.is_gt))
                        c.then(dve.tensor_tensor(cell[:, :], r[:, :], cell[:, :], ALU.subtract))
                        c.then(dve.tensor_scalar(cell[:, :], cell[:, :], float(GRID - 1), None, ALU.min))
                        c.mark(dve.tensor_tensor(s[:, :], s[:, :], cell[:, :], ALU.subtract))
                        c.then(dve.tensor_tensor(one[:, :, :], grid, spread(cell[:, :]), ALU.is_equal))
                        for z, o in ((base, W_BASE), (slope, W_SLOPE)):
                            for u in range(LB):
                                i = dve.tensor_tensor(blk(pick, u), blk(one, u), weights(u, o), ALU.mult)
                                if u == LB - 1:
                                    c.then(i)
                                else:
                                    c.mark(i)
                            c.then(dve.tensor_reduce(z[:, :], pick[:, :, :], AX.X, ALU.add))
                        c.then(dve.tensor_tensor(slope[:, :], slope[:, :], s[:, :], ALU.mult))
                        dve.tensor_tensor(base[:, :], base[:, :], slope[:, :], ALU.add).then_inc(steps, 1)
                        c.n += 1
                        dve.wait_ge(steps, c.base + c.n)
                        assert c.n == STEPS, c.n
                        dve.wait_ge(summed, n + 1)
                        for u in range(LB):
                            i = dve.tensor_scalar(blk(hs[:, b, :], u), blk(base, u), w[:, b, u, W_SCALE:W_SCALE + 1], None, ALU.mult)
                        i.then_inc(splined, 1)

            @block.sync
            def _(sp):
                sp.sem_inc(y_free, 2)
                v = y_t.rearrange("(l p) d -> p l d", p=P)

                def put(n, b):
                    sp.wait_ge(brought, n + 3)
                    sp.dma_start(v[:, bass.ds(n, 1), :].rearrange("p a d -> p (a d)"), y[:, b, :]).then_inc(stored[b], 16)
                put(0, 0)
                with sp.Fori(0, NL // 2 - 1) as t:
                    put(2 * t + 1, 1)
                    sp.wait_ge(stored[0], 16 * t + 16)
                    sp.sem_inc(y_free, 1)
                    put(2 * t + 2, 0)
                    sp.wait_ge(stored[1], 16 * t + 16)
                    sp.sem_inc(y_free, 1)
                put(NL - 1, 1)
                for b in range(2):
                    sp.wait_ge(stored[b], 16 * (NL // 2))


def layer1_ffn(nc, k, a, x3, xn, xt, out):
    with ExitStack() as ctx:
        m = Mem(nc, ctx, "ffn1")
        xa = m.sb("xa", [P, NT, D])
        sig = m.sb("sig", [P, KD, T + CL], BF16)
        slot_i = m.sb("slot_i", [P, NT], I32)
        weight_i = m.sb("weight_i", [P, NBK], I32)
        token_i = m.sb("token_i", [P, NL], I32)
        gamma = m.sb("gamma", [P, D])
        beta = m.sb("beta", [P, D])
        rows_t = nc.dram_tensor("tile_rows", (N, D), F32).ap()
        token_t = nc.dram_tensor("tile_tokens", (NL * P, 2), I32).ap()
        y_t = nc.dram_tensor("tile_out", (NL * P, D), F32).ap()
        table = a["tile_table"]
        tile_signatures(nc, k, table, sig)
        load(nc, "ffn1_load", [(gamma[:, :], a["L1_ffn_gamma"].rearrange("(a n) -> a n", a=1).broadcast_to([P, D])),
                               (beta[:, :], a["L1_ffn_beta"].rearrange("(a n) -> a n", a=1).broadcast_to([P, D]))])
        layernorm(nc, k, "ln3", x3, xa)
        layernorm(nc, k, "ln4", xa, xn, extra=(gamma, beta))
        store(nc, "ffn1_store", [(chunks(rows_t), xn[:, :, :])])
        turn(nc, k, "turn3", xn, xt)
        route(nc, k, xt, sig, token_t, slot_i, weight_i, token_i)
        tile_ffn(nc, k, table, rows_t, y_t, weight_i, token_i)
        got, summed, stored = m.sem("got"), m.sem("summed"), m.sem("stored")
        y = xn
        with nc.Block() as block:
            @block.gpsimd
            def _(pool):
                for i in range(NT):
                    pool.indirect_dma_start(out=y[:, i, :], out_offset=None, in_=y_t,
                                            in_offset=bass.IndirectOffsetOnAxis(ap=slot_i[:, i:i + 1], axis=0)).then_inc(got, 16)

            @block.vector
            def _(dve):
                dve.tensor_tensor(xa[:, :, :], xa[:, :, :], x3[:, :, :], ALU.add).then_inc(summed, 1)
                dve.wait_ge(got, 16 * NT)
                dve.wait_ge(summed, 1)
                dve.tensor_tensor(xa[:, :, :], xa[:, :, :], y[:, :, :], ALU.add).then_inc(summed, 1)

            @block.sync
            def _(sp):
                sp.wait_ge(summed, 2)
                sp.dma_start(chunks(out), xa[:, :, :]).then_inc(stored, 16)
                sp.wait_ge(stored, 16)


USED = ("x", "src", "dst", "L0_gnn_W", "L0_gnn_b", "L0_gnn_diffusion_weights",
        "L0_mix_Wq", "L0_mix_Wk", "L0_mix_Wv", "L0_mix_W1", "L0_mix_W2",
        "L0_ffn_Wg", "L0_ffn_W1", "L0_ffn_b1", "L0_ffn_W2", "L0_ffn_b2",
        "L1_gnn_W_l", "L1_gnn_W_r", "L1_gnn_att", "L1_gnn_bias",
        "L1_mix_qkv_weight", "L1_mix_proj_weight", "L1_mix_proj_bias",
        "L1_ffn_gamma", "L1_ffn_beta", "tile_table")


def program(nc, a, out):
    with ExitStack() as ctx:
        k = keep(nc, ctx)
        m = Mem(nc, ctx, "x")
        x, xn, xt, x1 = (m.sb(s, [P, NT, D]) for s in ("x", "xn", "xt", "x1"))
        xt = xt[:, :, :].rearrange("p a b -> p (a b)").rearrange("p (c n) -> p c n", c=KD)
        keys_t = nc.dram_tensor("edge_keys", (EP + 2,), F32).ap()
        with part(nc):
            constants(nc, k)
            sort_edges(nc, k, a["src"], a["dst"], keys_t)
            load(nc, "loadx", [(x[:, :, :], chunks(a["x"]))])
            layernorm(nc, k, "ln0", x, xn)
            turn(nc, k, "turn0", xn, xt)
            layer0_gnn(nc, k, a, x, xn, xt, x1)
            layer0_mix(nc, k, a, xn, xt, x1)
        with part(nc):
            layer0_ffn(nc, k, a, x1, xn, xt)
            layernorm(nc, k, "ln2", x1, xn)
            turn(nc, k, "turn2", xn, xt)
            layer1_gnn(nc, k, a, keys_t, xn, xt, x1)
        with part(nc):
            layer1_ffn(nc, k, a, x1, xn, xt, out)


def lay_out(name, v):
    if name in ("L0_mix_Wq", "L0_mix_Wk", "L0_mix_Wv", "L0_mix_W1", "L0_mix_W2", "L1_mix_qkv_weight", "L1_mix_proj_weight"):
        return v.T
    if name == "L0_ffn_b1":
        return v.reshape(NE, FF // P, P).transpose(2, 0, 1)
    return v


def kernel(**inputs):
    import numpy as np
    import concourse.bacc as bacc
    from concourse.bass_utils import run_bass_kernel_spmd as run

    nc = bacc.Bacc("TRN2", target_bir_lowering=False, num_devices=1)
    arrays, a = {}, {}
    for n in USED:
        if n == "tile_table":
            v = np.concatenate([
                inputs["L1_ffn_Wd"].reshape(T, DH, KD, P).transpose(0, 3, 2, 1).reshape(T, P, D),
                inputs["L1_ffn_Wu"].transpose(0, 2, 1), inputs["L1_ffn_spline_bases"], inputs["L1_ffn_spline_slopes"],
                np.broadcast_to(inputs["L1_ffn_scale"][:, None, None], (T, P, ROW - W_SCALE))], axis=2).reshape(T * P, ROW)
        else:
            v = lay_out(n, inputs[n])
        v = np.ascontiguousarray(v)
        arrays[f"in_{n}"] = v
        a[n] = nc.dram_tensor(f"in_{n}", v.shape, mybir.dt.from_np(v.dtype), kind="ExternalInput").ap()
    out = nc.dram_tensor("result", (N, D), F32, kind="ExternalOutput").ap()
    program(nc, a, out)
    r = run(nc, [arrays], core_ids=[0])
    return r.results[0]["result"]
```

```python
from contextlib import ExitStack, contextmanager

import concourse.bass as bass
from concourse import mybir

P = 128
N = 1024
D = 512
NT = N // P
KD = D // P
E = 32768
EC = E // P
CH = EC + NT
NG = N // P
NB = CH + NG
EP = NB * P
SEG = 16
BS = NB // SEG
SL = BS * P
H8 = 8
HC = D // H8
BIG = 1.0e30

F32 = mybir.dt.float32
F16 = mybir.dt.float16
BF16 = mybir.dt.bfloat16
I32 = mybir.dt.int32
ALU = mybir.AluOpType
ACT = mybir.ActivationFunctionType
AX = mybir.AxisListType


class Chain:

    def __init__(self, eng, sem, base=0):
        self.eng, self.sem, self.base, self.n = eng, sem, base, 0

    def mark(self, ins):
        ins.then_inc(self.sem, 1)
        self.n += 1
        return self.n

    def then(self, ins):
        self.mark(ins)
        self.eng.wait_ge(self.sem, self.base + self.n)


class Mem:

    def __init__(self, nc, ctx, stage):
        self.nc, self.ctx, self.stage = nc, ctx, stage

    def sb(self, name, shape, dt=F32):
        return self.ctx.enter_context(self.nc.sbuf_tensor(f"{self.stage}_{name}", shape, dt))

    def ps(self, name, shape, dt=F32):
        return self.ctx.enter_context(self.nc.psum_tensor(f"{self.stage}_{name}", shape, dt))

    def sem(self, name):
        return self.nc.alloc_semaphore(name=f"{self.stage}_{name}")


@contextmanager
def part(nc):
    with nc.cleanup_on_exit():
        yield
    nc.all_engine_barrier()


def constants(nc, k):
    with ExitStack() as ctx:
        m = Mem(nc, ctx, "const")
        made, laid = m.sem("made"), m.sem("laid")
        row = m.sb("row", [P, N], I32)
        with nc.Block() as block:
            @block.gpsimd
            def _(pool):
                c = Chain(pool, made)
                c.then(pool.iota(row[:, :], [[1, N]], base=0, channel_multiplier=0))
                c.then(pool.iota(k.lane_i[:, :], [[0, 1]], base=0, channel_multiplier=1))
                c.then(pool.memset(k.ident[:, :], 0.0))
                c.then(pool.memset(k.ones[:, :], 1.0))
                c.then(pool.affine_select(out=k.ident[:, :], in_=k.ident[:, :], compare_op=ALU.not_equal, fill=1.0,
                                          base=0, pattern=[[-1, P]], channel_multiplier=1))
                c.then(pool.affine_select(out=k.before[:, :], in_=k.ones[:, :], compare_op=ALU.is_gt, fill=0.0,
                                          base=0, pattern=[[1, P]], channel_multiplier=-1))

            @block.vector
            def _(dve):
                dve.wait_ge(made, 6)
                c = Chain(dve, laid)
                c.mark(dve.tensor_copy(k.iota16[:, :], row[:, :]))
                c.mark(dve.tensor_copy(k.iotaf[:, :], row[:, :]))
                c.mark(dve.tensor_copy(k.lane[:, :], k.lane_i[:, :]))
                c.mark(dve.tensor_copy(k.ones_b[:, :], k.ones[:, :]))
                c.mark(dve.tensor_copy(k.ident_b[:, :], k.ident[:, :]))
                c.mark(dve.tensor_copy(k.before_b[:, :], k.before[:, :]))
                c.mark(dve.tensor_scalar(k.later[:, :], k.before[:, :], -1.0, 1.0, ALU.mult, ALU.add))
                dve.wait_ge(laid, c.n)
                c.mark(dve.tensor_tensor(k.later[:, :], k.later[:, :], k.ident[:, :], ALU.subtract))
                c.mark(dve.tensor_scalar(k.notbefore_b[:, :], k.before[:, :], 1.0, None, ALU.subtract))


R = 32
TW = R * CH
SLICES = [slice(o, min(o + D, TW)) for o in range(0, TW, D)]


def radix_slots(nc, k, name, digit, slot, groups=None):
    with ExitStack() as ctx:
        m = Mem(nc, ctx, name)
        hot = m.sb("hot", [P, R, CH], BF16)
        run = m.sb("run", [P, TW])
        bank = [m.ps(f"bank{i}", [P, D]) for i in range(4)]
        made, full, free, full2, free2, steps = (m.sem(x) for x in ("made", "full", "free", "full2", "free2", "steps"))
        flat = lambda x: x[:, :, :].rearrange("p q n -> p (q n)")
        if groups is not None:
            last, before, total, nblk, shift = (m.sb(x, [P, NG]) for x in ("last", "before", "total", "nblk", "shift"))
            total_i = m.sb("total_i", [P, NG], I32)
        with nc.Block() as block:
            @block.vector
            def _(dve):
                c = Chain(dve, steps)
                for q in range(R):
                    dve.tensor_scalar(hot[:, q, :], digit[:, :], float(q), None, ALU.is_equal).then_inc(made, 1)
                dve.wait_ge(free, len(SLICES))
                c.then(dve.tensor_tensor_scan(run[:, :], run[:, :], k.ones[:, 0:1].broadcast_to([P, TW]), 0.0, ALU.add, ALU.mult))
                if groups is not None:
                    W = TW // NG
                    c.mark(dve.tensor_copy(last[:, :], run[:, W - 1::W]))
                    c.mark(dve.memset(before[:, 0:1], 0.0))
                    c.then(dve.tensor_copy(before[:, 1:NG], run[:, W - 1:TW - 1:W]))
                    c.then(dve.tensor_tensor(total[:, :], last[:, :], before[:, :], ALU.subtract))
                    c.then(dve.tensor_scalar(total_i[:, :], total[:, :], float(P - 1), None, ALU.add))
                    c.then(dve.tensor_scalar(total_i[:, :], total_i[:, :], P.bit_length() - 1, None, ALU.arith_shift_right))
                    c.then(dve.tensor_copy(nblk[:, :], total_i[:, :]))
                    c.then(dve.tensor_tensor_scan(groups[:, :], nblk[:, :], k.ones[:, 0:NG], 0.0, ALU.add, ALU.mult))
                    c.then(dve.tensor_tensor(shift[:, :], groups[:, :], nblk[:, :], ALU.subtract))
                    c.then(dve.tensor_scalar(shift[:, :], shift[:, :], float(P), None, ALU.mult))
                    c.then(dve.tensor_tensor(shift[:, :], shift[:, :], before[:, :], ALU.subtract))
                    for g in range(NG):
                        c.mark(dve.tensor_scalar(run[:, g * W:(g + 1) * W], run[:, g * W:(g + 1) * W], shift[:, g:g + 1],
                                                 None, ALU.add))
                    dve.wait_ge(steps, c.n)
                def masked(j):
                    here = SLICES[j]
                    dve.wait_ge(free2, j + 1)
                    c.mark(dve.tensor_tensor(run[:, here], run[:, here], flat(hot)[:, here], ALU.mult))
                for j, here in enumerate(SLICES):
                    dve.wait_ge(full2, j + 1)
                    dve.tensor_tensor(run[:, here], bank[j % 4][:, 0:here.stop - here.start], run[:, here],
                                      ALU.add).then_inc(free2, 1)
                    if j:
                        masked(j - 1)
                masked(len(SLICES) - 1)
                dve.wait_ge(steps, c.n)
                c.then(dve.tensor_reduce(slot[:, :], run[:, :].rearrange("p (q n) -> p n q", n=CH), AX.X, ALU.add))

            @block.tensor
            def _(pe):
                for j, here in enumerate(SLICES):
                    pe.wait_ge(made, (here.stop - 1) // CH + 1)
                    if j >= 4:
                        pe.wait_ge(free, j - 3)
                    pe.matmul(bank[j % 4][:, 0:here.stop - here.start], k.ones_b[:, :], flat(hot)[:, here],
                              start=True, stop=True).then_inc(full, 1)
                pe.wait_ge(free, len(SLICES))
                for j, here in enumerate(SLICES):
                    if j >= 4:
                        pe.wait_ge(free2, j - 3)
                    pe.matmul(bank[j % 4][:, 0:here.stop - here.start], k.notbefore_b[:, :], flat(hot)[:, here],
                              start=True, stop=True).then_inc(full2, 1)

            @block.scalar
            def _(act):
                for j, here in enumerate(SLICES):
                    act.wait_ge(full, j + 1)
                    act.activation(run[:, here], bank[j % 4][:, 0:here.stop - here.start], ACT.Copy).then_inc(free, 1)


def place(nc, k, name, slot, values, outs, width):
    with ExitStack() as ctx:
        m = Mem(nc, ctx, name)
        U = 6
        minus = m.sb("minus", [P, 2, CH])
        away = m.sb("away", [P, U // 2, P])
        slot_i = m.sb("slot_i", [P, CH], I32)
        part_i = m.sb("part_i", [P, 2, CH], I32)
        at_lane = m.sb("at_lane", [P, CH])
        at_block = m.sb("at_block", [P, CH])
        lanes = m.sb("lanes", [P, U, 2, P], F16)
        blocks = m.sb("blocks", [P, U, NB], F16)
        zb = m.sb("zb", [P, D], BF16)
        placed = [m.ps(f"placed{i}", [P, D]) for i in range(2)]
        zeroed, parted, laid, laid2, far, used, steps = (m.sem(x) for x in (
            "zeroed", "parted", "laid", "laid2", "far", "used", "steps"))
        with nc.Block() as block:
            @block.vector
            def _(dve):
                c = Chain(dve, steps)
                dve.memset(zb[:, :], 0.0).then_inc(zeroed, 1)
                c.then(dve.tensor_copy(slot_i[:, :], slot[:, :]))
                c.mark(dve.tensor_scalar(part_i[:, 0, :], slot_i[:, :], P - 1, None, ALU.bitwise_and))
                c.then(dve.tensor_scalar(part_i[:, 1, :], slot_i[:, :], P.bit_length() - 1, None, ALU.arith_shift_right))
                c.mark(dve.tensor_copy(at_lane[:, :], part_i[:, 0, :]))
                c.then(dve.tensor_copy(at_block[:, :], part_i[:, 1, :]))

                def lay(n, u):
                    for f, v in enumerate(values):
                        if f == 0 or u % 2 == 0:
                            dve.tensor_scalar(lanes[:, u, f, :], k.iota16[:, 0:P], at_lane[:, bass.ds(n, 1)], v[:, bass.ds(n, 1)],
                                              ALU.is_equal, ALU.mult)
                    dve.tensor_scalar(blocks[:, u, 0:width], k.iota16[:, 0:width], at_block[:, bass.ds(n, 1)], None,
                                      ALU.is_equal).then_inc(laid, 1)
                c.mark(dve.tensor_scalar(minus[:, 0, :], at_lane[:, :], -1.0, None, ALU.mult))
                c.then(dve.tensor_scalar(minus[:, 1, :], values[1][:, 0:CH], -1.0, None, ALU.mult))
                dve.sem_inc(parted, 1)
                for u in range(U):
                    lay(u, u)
                with dve.Fori(1, CH // U) as t:
                    for u in range(U):
                        dve.wait_ge(used, U * t + u - U + 1)
                        lay(U * t + u, u)
                dve.wait_ge(used, CH)
                for f, out in enumerate(outs):
                    c.mark(dve.tensor_copy(out[:, 0:width], placed[f][:, 0:width]))

            @block.scalar
            def _(act):
                def lay(n, u, count):
                    act.activation(away[:, u // 2, :], k.iota16[:, 0:P], ACT.Abs, bias=minus[:, 0, bass.ds(n, 1)]).then_inc(far, 1)
                    act.wait_ge(far, count)
                    act.activation(lanes[:, u, 1, :], away[:, u // 2, :], ACT.Relu, scale=minus[:, 1, bass.ds(n, 1)],
                                   bias=values[1][:, bass.ds(n, 1)]).then_inc(laid2, 1)
                act.wait_ge(parted, 1)
                for u in range(1, U, 2):
                    lay(u, u, u // 2 + 1)
                with act.Fori(1, CH // U) as t:
                    for u in range(1, U, 2):
                        act.wait_ge(used, U * t + u - U + 1)
                        lay(U * t + u, u, U // 2 * t + (u // 2 + 1))

            @block.tensor
            def _(pe):
                pe.wait_ge(zeroed, 1)
                for x in placed:
                    pe.matmul(x[:, :], k.ones_b[:, :], zb[:, :], start=True, stop=False, skip_group_check=True)
                with pe.Fori(0, CH // U) as t:
                    for u in range(U):
                        pe.wait_ge(laid, U * t + u + 1)
                        if u % 2:
                            pe.wait_ge(laid2, U // 2 * t + (u // 2 + 1))
                        for f in range(2):
                            i = pe.matmul(placed[f][:, 0:width], lanes[:, u, f, :], blocks[:, u, 0:width], start=False, stop=False,
                                          skip_group_check=True)
                        i.then_inc(used, 1)


def sort_edges(nc, k, src, dst, keys_t, ahead):
    with ExitStack() as ctx:
        m = Mem(nc, ctx, "sort")
        dst_i = m.sb("dst_i", [P, CH], I32)
        src_i = m.sb("src_i", [P, EC], I32)
        srcf = m.sb("srcf", [P, CH])
        dstf = m.sb("dstf", [P, CH])
        key = m.sb("key", [P, CH])
        digit = m.sb("digit", [P, CH], F16)
        slot = m.sb("slot", [P, CH])
        src2 = m.sb("src2", [P, CH])
        key2 = m.sb("key2", [P, CH])
        gend = m.sb("gend", [P, NG])
        guard = m.sb("guard", [1, 2])
        loaded, first, second, third = (m.sem(x) for x in ("loaded", "first", "second", "third"))
        SHIFT = R.bit_length() - 1
        with nc.Block() as block:
            @block.sync
            def _(sp):
                sp.dma_start(dst_i[:, 0:EC], dst.rearrange("(p c) -> p c", p=P)).then_inc(loaded, 16)
                sp.dma_start(src_i[:, :], src.rearrange("(p c) -> p c", p=P)).then_inc(loaded, 16)
                for x in ahead:
                    x.start(sp)

            @block.vector
            def _(dve):
                c = Chain(dve, first)
                for i in range(NT):
                    c.mark(dve.tensor_scalar(dstf[:, EC + i:EC + i + 1], k.lane[:, :], float(P * i), None, ALU.add))
                    c.mark(dve.tensor_scalar(srcf[:, EC + i:EC + i + 1], k.lane[:, :], float(P * i), None, ALU.add))
                dve.wait_ge(loaded, 32)
                c.mark(dve.tensor_copy(dstf[:, 0:EC], dst_i[:, 0:EC]))
                c.then(dve.tensor_copy(srcf[:, 0:EC], src_i[:, :]))
                c.mark(dve.tensor_scalar(key[:, :], dstf[:, :], 1.0, None, ALU.add))
                c.then(dve.tensor_copy(dst_i[:, EC:CH], dstf[:, EC:CH]))
                c.then(dve.tensor_scalar(dst_i[:, :], dst_i[:, :], R - 1, None, ALU.bitwise_and))
                c.then(dve.tensor_copy(digit[:, :], dst_i[:, :]))
        radix_slots(nc, k, "low", digit, slot)
        place(nc, k, "placel", slot, (srcf, key), (src2, key2), CH)
        with nc.Block() as block:
            @block.vector
            def _(dve):
                c = Chain(dve, second)
                c.then(dve.tensor_scalar(dst_i[:, :], key2[:, :], -1.0, None, ALU.add))
                c.then(dve.tensor_scalar(dst_i[:, :], dst_i[:, :], SHIFT, None, ALU.arith_shift_right))
                c.then(dve.tensor_copy(digit[:, :], dst_i[:, :]))
        radix_slots(nc, k, "high", digit, slot, groups=gend)
        place(nc, k, "placeh", slot, (src2, key2), (k.srcf, k.key), NB)
        ging = m.sb("ging", [P, NB, NG])
        keyrow = m.sb("keyrow", [SEG, SL])
        keyp = m.ps("keyp", [SEG, 5 * D])
        turned, copied, stored, guarded = (m.sem(x) for x in ("turned", "copied", "stored", "guarded"))
        with nc.Block() as block:
            @block.tensor
            def _(pe):
                for i in range(BS):
                    t = pe.transpose(keyp[:, i * P:(i + 1) * P], k.key[:, i::BS], k.ident[:, :])
                t.then_inc(turned, 1)

            @block.vector
            def _(dve):
                c = Chain(dve, third)
                dve.memset(guard[:, 0:1], 0.0).then_inc(guarded, 1)
                dve.memset(guard[:, 1:2], -1.0).then_inc(guarded, 1)
                c.mark(dve.tensor_copy(k.src_i[:, :], k.srcf[:, :]))
                c.mark(dve.tensor_scalar(k.dst_i[:, :], k.key[:, :], -1.0, 0.0, ALU.add, ALU.max))
                dve.wait_ge(turned, 1)
                dve.tensor_copy(keyrow[:, :], keyp[:, 0:SL]).then_inc(copied, 1)
                c.then(dve.tensor_tensor(ging[:, :, :], k.iotaf[:, 0:NB].unsqueeze(2).broadcast_to([P, NB, NG]),
                                         gend[:, :].unsqueeze(1).broadcast_to([P, NB, NG]), ALU.is_ge))
                c.then(dve.tensor_reduce(k.group[:, :], ging[:, :, :], AX.X, ALU.add))
                c.then(dve.tensor_scalar(k.group[:, :], k.group[:, :], float(NG - 1), None, ALU.min))
                c.mark(dve.tensor_scalar(k.group_i[:, :], k.group[:, :], float(D), None, ALU.mult))
                c.then(dve.tensor_scalar(k.local[:, :], k.group[:, :], float(-P), -1.0, ALU.mult, ALU.add))
                c.then(dve.tensor_tensor(k.local[:, :], k.local[:, :], k.key[:, :], ALU.add))

            @block.sync
            def _(sp):
                row = keys_t.rearrange("(a n) -> a n", a=1)
                sp.wait_ge(guarded, 2)
                sp.dma_start(row[:, 0:1], guard[:, 0:1]).then_inc(stored, 16)
                sp.dma_start(row[:, EP + 1:EP + 2], guard[:, 1:2]).then_inc(stored, 16)
                sp.wait_ge(copied, 1)
                sp.dma_start(keys_t[1:EP + 1].rearrange("(s n) -> s n", s=SEG), keyrow[:, :]).then_inc(stored, 16)
                sp.wait_ge(stored, 48)


class Keep:
    pass


def keep(nc, ctx):
    k = Keep()
    m = Mem(nc, ctx, "k")
    k.ident = m.sb("ident", [P, P])
    k.ident_b = m.sb("ident_b", [P, P], BF16)
    k.ones = m.sb("ones", [P, P])
    k.ones_b = m.sb("ones_b", [P, P], BF16)
    k.before = m.sb("before", [P, P])
    k.before_b = m.sb("before_b", [P, P], BF16)
    k.notbefore_b = m.sb("notbefore_b", [P, P], BF16)
    k.later = m.sb("later", [P, P])
    k.iota16 = m.sb("iota16", [P, N], F16)
    k.iotaf = m.sb("iotaf", [P, N])
    k.lane_i = m.sb("lane_i", [P, 1], I32)
    k.lane = m.sb("lane", [P, 1])
    k.group = m.sb("group", [P, NB])
    k.group_i = m.sb("group_i", [P, NB], I32)
    k.srcf = m.sb("srcf", [P, NB])
    k.src_i = m.sb("src_i", [P, NB], I32)
    k.dst_i = m.sb("dst_i", [P, NB], I32)
    k.local = m.sb("local", [P, NB])
    k.key = m.sb("key", [P, NB])
    return k


def block_groups(nc, k, first, count):
    _, values = nc.values_load_multi_w_load_instructions(
        k.group_i[0:1, bass.ds(first, count)], engines=[mybir.EngineType.PE], min_val=0, max_val=(NG - 1) * D,
        skip_runtime_bounds_check_because="k.group_i is clamped to the last group where it is made")
    return values


def adjacency(nc, k, adj, rs):
    with ExitStack() as ctx:
        m = Mem(nc, ctx, "adj")
        U, TURN = 8, 16
        zb = m.sb("zb", [P, D], BF16)
        cnt = m.sb("cnt", [P, NG, N], BF16)
        zeroed, made, used, capped, turned_down, far, aimed = (m.sem(x) for x in (
            "zeroed", "made", "used", "capped", "turned_down", "far", "aimed"))
        turned, summed, steps = (m.sem(x) for x in ("turned", "summed", "steps"))
        with ExitStack() as inner:
            mi = Mem(nc, inner, "adjc")
            acc = mi.ps("acc", [P, NG * D])
            to = mi.sb("to", [P, NB * P], BF16)
            minus = adj[:, 0, 0:NB]
            away = adj[:, 1, 0:U // 2 * P].rearrange("p (u d) -> p u d", d=P)
            frm = mi.sb("frm", [P, U, D], BF16)
            with nc.Block() as block:
                @block.vector
                def _(dve):
                    dve.memset(zb[:, :], 0.0).then_inc(zeroed, 1)
                    dve.tensor_scalar(minus[:, :], k.local[:, :], -1.0, None, ALU.mult).then_inc(turned_down, 1)

                    def onehots(n, u, h):
                        if h == 0 and u % 2 == 0:
                            dve.tensor_scalar(to[:, bass.ds(n * P, P)], k.iota16[:, 0:P], k.local[:, bass.ds(n, 1)], None,
                                              ALU.is_equal)
                        dve.tensor_scalar(frm[:, u, :], k.iota16[:, h * D:(h + 1) * D], k.srcf[:, bass.ds(n, 1)], None,
                                          ALU.is_equal).then_inc(made, 1)
                    for h in range(2):
                        for u in range(U):
                            if h:
                                dve.wait_ge(used, NB * h)
                            onehots(u, u, h)
                        with dve.Fori(1, NB // U) as t:
                            for u in range(U):
                                dve.wait_ge(used, U * t + (u + 1 - U + NB * h))
                                onehots(U * t + u, u, h)
                        dve.wait_ge(used, NB * (h + 1))
                        for g in range(NG):
                            dve.tensor_scalar(cnt[:, g, h * D:(h + 1) * D], acc[:, g * D:(g + 1) * D], 3.0, None,
                                              ALU.min).then_inc(capped, 1)

                @block.scalar
                def _(act):
                    act.wait_ge(turned_down, 1)
                    with act.Fori(0, NB // U) as t:
                        for u in range(1, U, 2):
                            act.activation(away[:, u // 2, :], k.iota16[:, 0:P], ACT.Abs,
                                           bias=minus[:, bass.ds(U * t + u, 1)]).then_inc(far, 1)
                            act.wait_ge(far, U // 2 * t + (u // 2 + 1))
                            act.activation(to[:, bass.ds((U * t + u) * P, P)], away[:, u // 2, :], ACT.Relu, scale=-1.0,
                                           bias=k.ones[:, 0:1]).then_inc(aimed, 1)

                @block.tensor
                def _(pe):
                    pe.wait_ge(zeroed, 1)
                    for h in range(2):
                        if h:
                            pe.wait_ge(capped, NG)
                        for g in range(NG):
                            pe.matmul(acc[:, g * D:(g + 1) * D], k.ones_b[:, :], zb[:, :], start=True, stop=False,
                                      skip_group_check=True)
                        with pe.Fori(0, NB // TURN) as t:
                            groups = block_groups(nc, k, TURN * t, TURN)
                            for i in range(TURN):
                                g, u = groups[i], i % U
                                pe.wait_ge(made, TURN * t + i + (1 + NB * h))
                                if h == 0 and i % 2:
                                    pe.wait_ge(aimed, TURN // 2 * t + (i // 2 + 1))
                                pe.matmul(acc[:, bass.ds(g, D)], to[:, bass.ds(P * (TURN * t + i), P)], frm[:, u, :], start=False, stop=False,
                                          skip_group_check=True).then_inc(used, 1)
        both = m.sb("both", [P, 2, N], BF16)
        two = m.sb("two", [P, P], BF16)
        tp = m.ps("tp", [P, 2, N], BF16)
        with nc.Block() as block:
            @block.tensor
            def _(pe):
                for i in range(NT):
                    if i >= 2:
                        pe.wait_ge(summed, i - 1)
                    for j in range(NT):
                        t = pe.transpose(tp[:, i % 2, j * P:(j + 1) * P], cnt[:, j, i * P:(i + 1) * P], k.ident_b[:, :])
                    t.then_inc(turned, 1)

            @block.vector
            def _(dve):
                c = Chain(dve, steps)
                c.then(dve.tensor_scalar(two[:, :], k.ident[:, :], 2.0, None, ALU.mult))
                for i in range(NT):
                    here = slice(i * P, (i + 1) * P)
                    dve.wait_ge(turned, i + 1)
                    dve.tensor_tensor(both[:, i % 2, :], cnt[:, i, :], tp[:, i % 2, :], ALU.add).then_inc(summed, 1)
                    dve.wait_ge(summed, i + 1)
                    c.then(dve.tensor_tensor(both[:, i % 2, here], both[:, i % 2, here], two[:, :], ALU.subtract))
                    c.then(dve.tensor_scalar(adj[:, i, :], both[:, i % 2, :], 0.0, None, ALU.is_gt))
                    c.then(dve.tensor_tensor(adj[:, i, here], adj[:, i, here], k.ident[:, :], ALU.add))
                c.then(dve.tensor_reduce(rs[:, :], adj[:, :, :], AX.X, ALU.add))
                c.then(dve.tensor_scalar(rs[:, :], rs[:, :], 1.0, None, ALU.max))
                c.then(dve.reciprocal(rs[:, :], rs[:, :]))


def products(nc, name, count, produce, evacuate, width=D, dt=F32, ring=4, vector=True, scalar=True, before=None):
    with ExitStack() as ctx:
        m = Mem(nc, ctx, name)
        bank = [m.ps(f"bank{i}", [P, D if dt == F32 else 2 * D], dt) for i in range(ring)]
        full = m.sem("full")
        free = [m.sem("free_even"), m.sem("free_odd")]
        both = vector and scalar
        with nc.Block() as block:
            @block.tensor
            def _(pe):
                for n in range(count):
                    if n >= ring:
                        done = n - ring + 1
                        pe.wait_ge(free[(n - ring) % 2] if both else free[0], (done + 1) // 2 if both and (n - ring) % 2 == 0
                                   else done // 2 if both else done)
                    produce(pe, n, bank[n % ring]).then_inc(full, 1)

            def drain(eng, which):
                for n in range(count):
                    if not both or n % 2 == which:
                        eng.wait_ge(full, n + 1)
                        evacuate(eng, n, bank[n % ring]).then_inc(free[which if both else 0], 1)

            if vector:
                @block.vector
                def _(dve):
                    if before is not None:
                        before(dve)
                    drain(dve, 0)
            if scalar:
                @block.scalar
                def _(act):
                    drain(act, 1)


def copy(eng, out, in_):
    return eng.activation(out, in_, ACT.Copy) if isinstance(eng, bass.BassScalarEngine) else eng.tensor_copy(out, in_)


def accumulate(pe, bank, terms):
    for i, (lhsT, rhs) in enumerate(terms):
        last = pe.matmul(bank, lhsT, rhs, start=(i == 0), stop=(i == len(terms) - 1))
    return last


def turn(nc, k, name, src, dst):
    def produce(pe, n, bank):
        for c in range(KD):
            t = pe.transpose(bank[:, c * P:(c + 1) * P], src[:, n, c * P:(c + 1) * P], k.ident[:, :])
        return t
    products(nc, name, NT, produce, lambda eng, n, bank: copy(
        eng, dst[:, :, n * P:(n + 1) * P], bank[:, :].rearrange("p (c t) -> p c t", c=KD)))


def unturn(nc, k, name, src, dst):
    def produce(pe, n, bank):
        for c in range(KD):
            t = pe.transpose(bank[:, c * P:(c + 1) * P], src[:, c, n * P:(n + 1) * P], k.ident[:, :])
        return t
    products(nc, name, NT, produce, lambda eng, n, bank: copy(eng, dst[:, n, :], bank[:, :]))


def load(nc, name, pairs):
    with ExitStack() as ctx:
        landed = Mem(nc, ctx, name).sem("landed")
        with nc.Block() as block:
            @block.sync
            def _(sp):
                for out, in_ in pairs:
                    sp.dma_start(out, in_).then_inc(landed, 16)
                sp.wait_ge(landed, 16 * len(pairs))


class Ahead:

    def __init__(self, nc, name, pairs):
        self.pairs, self.landed = pairs, nc.alloc_semaphore(name=f"{name}_landed")

    def start(self, sp):
        for out, in_ in self.pairs:
            sp.dma_start(out, in_).then_inc(self.landed, 16)


def fetch_ahead(nc, name, pairs):
    ahead = Ahead(nc, name, pairs)
    with nc.Block() as block:
        @block.sync
        def _(sp):
            ahead.start(sp)
    return ahead


def fetched(nc, ahead):
    with nc.Block() as block:
        @block.sync
        def _(sp):
            sp.wait_ge(ahead.landed, 16 * len(ahead.pairs))


def layernorm(nc, k, name, x, out, extra=None):
    with ExitStack() as ctx:
        m = Mem(nc, ctx, name)
        stats = m.sb("stats", [P, NT, 6])
        mv = m.sb("mv", [P, NT, 2])
        v = m.sb("v", [P, NT])
        r = m.sb("r", [P, NT])
        w = m.sb("w", [P, NT])
        steps, var, root = m.sem("steps"), m.sem("var"), m.sem("root")
        with nc.Block() as block:
            @block.vector
            def _(dve):
                c = Chain(dve, steps)
                for i in range(NT):
                    c.mark(dve.bn_stats(stats[:, i, :], x[:, i, :]))
                dve.wait_ge(steps, c.n)
                for i in range(NT):
                    c.mark(dve.bn_aggr(mv[:, i, :], stats[:, i, :]))
                dve.wait_ge(steps, c.n)
                dve.tensor_scalar(v[:, :], mv[:, :, 1], 1e-5, None, ALU.add).then_inc(var, 1)
                dve.wait_ge(root, 1)
                c.then(dve.reciprocal(r[:, :], r[:, :]))
                dve.wait_ge(var, 1)
                c.then(dve.tensor_tensor(w[:, :], r[:, :], r[:, :], ALU.mult))
                c.then(dve.tensor_tensor(w[:, :], w[:, :], v[:, :], ALU.mult))
                c.then(dve.tensor_scalar(w[:, :], w[:, :], -0.5, 1.5, ALU.mult, ALU.add))
                c.then(dve.tensor_tensor(r[:, :], r[:, :], w[:, :], ALU.mult))
                for i in range(NT):
                    c.mark(dve.tensor_scalar(out[:, i, :], x[:, i, :], mv[:, i, 0:1], r[:, i:i + 1], ALU.subtract, ALU.mult))
                if extra is not None:
                    dve.wait_ge(steps, c.n)
                    for row, op in zip(extra, (ALU.mult, ALU.add)):
                        for i in range(NT):
                            c.mark(dve.tensor_tensor(out[:, i, :], out[:, i, :], row[:, :], op))
                        dve.wait_ge(steps, c.n)

            @block.scalar
            def _(act):
                act.wait_ge(var, 1)
                act.activation(r[:, :], v[:, :], ACT.Sqrt).then_inc(root, 1)


def softmax_rows(nc, name, x, rows, width, scale):
    with ExitStack() as ctx:
        m = Mem(nc, ctx, name)
        top = m.sb("top", [P, rows])
        total = m.sb("total", [P, rows])
        steps, raised, summed = m.sem("steps"), m.sem("raised"), m.sem("summed")
        with nc.Block() as block:
            @block.vector
            def _(dve):
                c = Chain(dve, steps)
                c.then(dve.tensor_reduce(top[:, :], x[:, :, :], AX.X, ALU.max))
                dve.tensor_scalar(top[:, :], top[:, :], -1.0, None, ALU.mult).then_inc(raised, 1)
                for i in range(rows):
                    dve.wait_ge(summed, i + 1)
                    c.then(dve.reciprocal(total[:, i:i + 1], total[:, i:i + 1]))
                    c.mark(dve.tensor_scalar(x[:, i, :], x[:, i, :], total[:, i:i + 1], scale, ALU.mult, ALU.mult))

            @block.scalar
            def _(act):
                act.wait_ge(raised, 1)
                for i in range(rows):
                    act.activation(x[:, i, :], x[:, i, :], ACT.Exp, bias=top[:, i:i + 1],
                                   accum_out=total[:, i:i + 1]).then_inc(summed, 1)


def chunks(w):
    return w.rearrange("(c p) n -> p c n", p=P)


def tile_terms(lhsT, rhs, n, kd=KD):
    return [(lhsT[:, c, n * P:(n + 1) * P], rhs[:, c, :]) for c in range(kd)]


def layer0_gnn(nc, k, a, x, xn, xt, x1):
    with ExitStack() as ctx:
        m = Mem(nc, ctx, "gnn0")
        adj = m.sb("adj", [P, NT, N])
        rs = m.sb("rs", [P, NT])
        w, b = xn[:, 0:KD, :], xn[0:1, KD, :]
        dw = m.sb("dw", [P, 4])
        weights = fetch_ahead(nc, "gnn0_w", [
            (w[:, :, :], chunks(a["L0_gnn_W"])), (b, a["L0_gnn_b"].rearrange("(a n) -> a n", a=1)),
            (dw[:, :], a["L0_gnn_diffusion_weights"].rearrange("(a n) -> a n", a=1).broadcast_to([P, 4]))])
        adjacency(nc, k, adj, rs)
        cur = [m.sb(f"cur{i}", [P, NT, D]) for i in range(2)]
        acc = m.sb("acc", [P, NT, D])
        fetched(nc, weights)
        products(nc, "gnn0_h", NT,
                 lambda pe, n, bank: accumulate(pe, bank[:, :], tile_terms(xt, w, n) + [(k.ones[0:1, :], b)]),
                 lambda eng, n, bank: copy(eng, cur[0][:, n, :], bank[:, :]))
        summed = m.sem("summed")
        flat = lambda z: z[:, :, :].rearrange("p t d -> p (t d)")

        def first_terms(dve):
            dve.tensor_scalar(flat(acc), flat(cur[0]), dw[:, 0:1], None, ALU.mult).then_inc(summed, 1)

        def term(step, src):
            def add(dve):
                dve.wait_ge(summed, step)
                dve.scalar_tensor_tensor(flat(acc), flat(src), dw[:, step:step + 1], flat(acc), ALU.mult, ALU.add).then_inc(summed, 1)
            return add
        before = first_terms
        for step in range(3):
            src, dst = cur[step % 2], cur[(step + 1) % 2]
            products(nc, f"gnn0_s{step}", NT,
                     lambda pe, n, bank: accumulate(pe, bank[:, :], tile_terms(adj, src, n, NT)),
                     lambda eng, n, bank: eng.activation(dst[:, n, :], bank[:, :], ACT.Copy, scale=rs[:, n:n + 1])
                     if isinstance(eng, bass.BassScalarEngine)
                     else eng.tensor_scalar(dst[:, n, :], bank[:, :], rs[:, n:n + 1], None, ALU.mult), before=before)
            before = term(step + 1, dst)
        with nc.Block() as block:
            @block.vector
            def _(dve):
                before(dve)
                dve.wait_ge(summed, 4)
                dve.scalar_tensor_tensor(flat(acc), flat(acc), 0.0, flat(x), ALU.max, ALU.add).then_inc(summed, 1)
                dve.wait_ge(summed, 5)
                dve.tensor_tensor(flat(x1), flat(x1), flat(acc), ALU.add).then_inc(summed, 1)


def layer0_mix(nc, k, xn, xt, x1, w, ahead):
    with ExitStack() as ctx:
        m = Mem(nc, ctx, "mix0")
        q = m.sb("q", [P, NT, D])
        qt = m.sb("qt", [P, KD, N])
        kt = m.sb("kt", [P, KD, N])
        kk = m.sb("kk", [P, NT, D])
        v = m.sb("v", [P, NT, D])
        context = q[:, 0:KD, :]
        fetched(nc, ahead)
        wk = w[:, 1, :, :]
        products(nc, "mix0_q", NT, lambda pe, n, bank: accumulate(pe, bank[:, :], tile_terms(xt, w[:, 0, :, :], n)),
                 lambda eng, n, bank: copy(eng, q[:, n, :], bank[:, :]))

        def halves(out, lhs, rhs, name, extra=None):
            products(nc, name, 2 * KD,
                     lambda pe, n, bank: accumulate(pe, bank[:, :], [
                         (lhs[:, c, (n // 2) * P:(n // 2 + 1) * P], rhs[:, c, (n % 2) * D:(n % 2 + 1) * D]) for c in range(KD)]),
                     lambda eng, n, bank: copy(eng, out[:, n // 2, (n % 2) * D:(n % 2 + 1) * D], bank[:, :])
                     if extra is None else eng.tensor_tensor(
                         out[:, n // 2, (n % 2) * D:(n % 2 + 1) * D], bank[:, :],
                         extra[:, n // 2, (n % 2) * D:(n % 2 + 1) * D], ALU.add), scalar=extra is None)
        halves(kt, wk, xt, "mix0_k")
        products(nc, "mix0_v", NT, lambda pe, n, bank: accumulate(pe, bank[:, :], tile_terms(xt, w[:, 2, :, :], n)),
                 lambda eng, n, bank: copy(eng, v[:, n, :], bank[:, :]))
        softmax_rows(nc, "mix0_sq", q, NT, D, float(D) ** -0.5)
        softmax_rows(nc, "mix0_sk", kt, KD, N, 1.0)
        unturn(nc, k, "mix0_kk", kt, kk)
        turn(nc, k, "mix0_qt", q, qt)
        products(nc, "mix0_c", KD, lambda pe, n, bank: accumulate(pe, bank[:, :], [
            (kk[:, i, n * P:(n + 1) * P], v[:, i, :]) for i in range(NT)]),
                 lambda eng, n, bank: copy(eng, context[:, n, :], bank[:, :]))
        yt, zt = kt, qt
        halves(yt, context, qt, "mix0_a", extra=xt)
        halves(zt, w[:, 3, :, :], yt, "mix0_1")
        products(nc, "mix0_2", NT,
                 lambda pe, n, bank: (accumulate(pe, bank[:, :], tile_terms(zt, w[:, 4, :, :], n)), [
                     pe.matmul(bank[:, c * P:(c + 1) * P], yt[:, c, n * P:(n + 1) * P], k.ident[:, :], start=False,
                               stop=(c == KD - 1), skip_group_check=True) for c in range(KD)][-1])[1],
                 lambda eng, n, bank: copy(eng, x1[:, n, :], bank[:, :]))


NE = 8
CAP = 256
FF = 1024
CT = CAP // P

T = 64
DH = P
GRID = 16
CL = 8
BT = 32
LB = P // BT
NL = (T * BT + N) // P
NBK = NL * LB
W_UP, W_BASE, W_SLOPE, W_SCALE = D, 2 * D, 2 * D + GRID, 2 * D + 2 * GRID
ROW = W_SCALE + 4


def sign(c, dve, x, scratch, out):
    c.then(dve.tensor_scalar(scratch, x, 0.0, None, ALU.is_lt))
    c.then(dve.scalar_tensor_tensor(out, x, 0.0, scratch, ALU.is_gt, ALU.subtract))


class Signatures:

    def __init__(self, nc, ctx, table, sig):
        m = Mem(nc, ctx, "sig")
        self.G = T // NE
        self.sig, self.v = sig, table.rearrange("(t p) r -> p t r", p=P)
        self.w = m.sb("w", [P, self.G, D])
        self.sums = m.sb("sums", [P, T * KD])
        self.scratch = m.sb("scratch", [P, T * KD])
        self.csum = m.sb("csum", [P, CL, KD])
        self.cneg = m.sb("cneg", [P, CL, KD])
        self.got = m.sem("got")
        self.read, self.steps = m.sem("read"), m.sem("steps")

    def load(self, sp, e, again=True):
        if again:
            sp.wait_ge(self.read, e)
        sp.dma_start(self.w[:, :, :], self.v[:, bass.ds(e * self.G, self.G), 0:D]).then_inc(self.got, 16)

    def reduce(self, dve, e):
        dve.wait_ge(self.got, 16 * e + 16)
        dve.tensor_reduce(self.sums[:, bass.ds(e * (self.G * KD), self.G * KD)],
                          self.w[:, :, :].rearrange("p g (c h) -> p (g c) h", h=DH), AX.X, ALU.add).then_inc(self.read, 1)

    def finish(self, dve):
        sums, csum, sig = self.sums, self.csum, self.sig
        c = Chain(dve, self.steps)
        dve.wait_ge(self.read, NE)
        sign(c, dve, sums[:, :], self.scratch[:, :], sums[:, :])
        c.mark(dve.tensor_copy(sig[:, :, 0:T], sums[:, :].rearrange("p (t c) -> p c t", c=KD)))
        c.then(dve.tensor_reduce(csum[:, :, :], sums[:, :].rearrange("p (g u c) -> p g c u", g=CL, c=KD), AX.X, ALU.add))
        sign(c, dve, csum[:, :, :], self.cneg[:, :, :], csum[:, :, :])
        c.mark(dve.tensor_copy(sig[:, :, T:T + CL], csum[:, :, :].rearrange("p g c -> p c g")))


def expert_choice(nc, k, a, ew, xt, scores_t, picks, chosen_i, gate):
    with ExitStack() as ctx:
        m = Mem(nc, ctx, "pick")
        wg = m.sb("wg", [P, KD, NE])
        s = m.sb("s", [P, NT, NE])
        w = m.sb("w", [P, NT, NE])
        top = m.sb("top", [P, NT])
        st = m.sb("st", [NE, N])
        sb = m.sb("sb", [P, NE, N])
        junk = m.sb("junk", [P, 4, N], BF16)
        rank = m.sb("rank", [P, NT])
        first = m.sb("first", [P, NE])
        spare = m.sb("spare", [P, 1])
        gt = m.sb("gt", [P, NT, NE])
        ge = m.sb("ge", [P, NT, NE])
        tie = m.sb("tie", [P, NT, NE])
        token = m.sb("token", [P, NT])
        slot_i = m.sb("slot_i", [P, NT * NE], I32)
        recs = m.sb("recs", [P, NT * NE, 2])
        idx = m.sb("idx", [P, 2, 8], I32)
        buf = m.sb("buf", [P, 2, 8, 2])
        back = m.sb("back", [P, NE, CT, 2])
        lg = m.ps("lg", [P, D])
        tp = m.ps("tp", [NE, N])
        loaded, logits, steps, exped, shifted, norm, turned = (m.sem(x) for x in (
            "loaded", "logits", "steps", "exped", "shifted", "norm", "turned"))
        copied, stored, ranked, slots, staged, fetched, out = (m.sem(x) for x in (
            "copied", "stored", "ranked", "slots", "staged", "fetched", "out"))
        sent = [m.sem(f"sent{i}") for i in range(2)]
        EARLY = 2
        spread = [m.sem("spread_early"), m.sem("spread_late")]
        with nc.Block() as block:
            @block.sync
            def _(sp):
                sp.dma_start(wg[:, :, :], chunks(a["L0_ffn_Wg"])).then_inc(loaded, 16)
                sp.wait_ge(copied, 2)
                sp.dma_start(scores_t, st[:, :]).then_inc(stored, 16)
                sp.wait_ge(stored, 16)
                for e in range(NE):
                    sp.dma_start(sb[:, e, :], scores_t[e:e + 1, :].broadcast_to([P, N])).then_inc(spread[e >= EARLY], 16)
                for b in range(2):
                    ew.fetch(sp, b, b)

            @block.tensor
            def _(pe):
                pe.wait_ge(loaded, 16)
                for i in range(NT):
                    t = accumulate(pe, lg[:, i * NE:(i + 1) * NE], [(xt[:, c, i * P:(i + 1) * P], wg[:, c, :]) for c in range(KD)])
                t.then_inc(logits, 1)
                pe.wait_ge(norm, 1)
                for i in range(NT):
                    t = pe.transpose(tp[:, i * P:(i + 1) * P], s[:, i, :], k.ident[:, :])
                t.then_inc(turned, 1)

            @block.scalar
            def _(act):
                act.wait_ge(shifted, 1)
                act.activation(w[:, :, :], s[:, :, :], ACT.Exp).then_inc(exped, 1)

            @block.vector
            def _(dve):
                c = Chain(dve, steps)
                wide = [P, NT, NE]
                dve.wait_ge(logits, 1)
                c.then(dve.tensor_copy(s[:, :, :].rearrange("p t e -> p (t e)"), lg[:, 0:NT * NE]))
                c.then(dve.tensor_reduce(top[:, :], s[:, :, :], AX.X, ALU.max))
                dve.tensor_tensor(s[:, :, :], s[:, :, :], top[:, :].unsqueeze(2).broadcast_to(wide), ALU.subtract).then_inc(shifted, 1)
                dve.wait_ge(exped, 1)
                c.then(dve.tensor_reduce(top[:, :], w[:, :, :], AX.X, ALU.add))
                c.then(dve.reciprocal(top[:, :], top[:, :]))
                dve.tensor_tensor(s[:, :, :], w[:, :, :], top[:, :].unsqueeze(2).broadcast_to(wide), ALU.mult).then_inc(norm, 1)
                dve.wait_ge(turned, 1)
                for h in range(2):
                    dve.tensor_copy(st[:, h * D:(h + 1) * D], tp[:, h * D:(h + 1) * D]).then_inc(copied, 1)
                c.mark(dve.memset(ge[:, 0, :], 0.0))
                c.mark(dve.tensor_scalar(first[:, :], k.iotaf[:, 0:NE], float(N), None, ALU.mult))
                dve.sem_inc(slots, 1)
                dve.wait_ge(norm, 1)
                for i in range(NT):
                    c.mark(dve.tensor_scalar(token[:, i:i + 1], k.lane[:, :], float(i * P), None, ALU.add))
                dve.wait_ge(steps, c.n)
                c.mark(dve.tensor_copy(recs[:, :, 0].rearrange("p (e t) -> p t e", t=NT), token[:, :].unsqueeze(2).broadcast_to(wide)))
                c.mark(dve.tensor_copy(recs[:, :, 1].rearrange("p (e t) -> p t e", t=NT), s[:, :, :]))
                dve.wait_ge(steps, c.n)
                def rank_tokens(e):
                    for i in range(NT):
                        mine = s[:, i, bass.ds(e, 1)]
                        lo = i * P
                        row = lambda x, n: sb[:, :, :].rearrange("p e n -> p (e n)")[:, bass.ds(e * N + x, n)]
                        j, jj = junk[:, i % 2, :], junk[:, 2 + i % 2, 0:P]
                        if i > 1:
                            dve.wait_ge(ranked, 3 * NT * e + 3 * (i - 1))
                        elif i == 0:
                            dve.wait_ge(slots, 2 * e + 1)
                        if i:
                            dve.tensor_scalar(j[:, 0:lo], row(0, lo), mine, 0.0, ALU.is_ge, ALU.add,
                                              accum_out=ge[:, i, bass.ds(e, 1)]).then_inc(ranked, 1)
                        else:
                            dve.tensor_copy(spare[:, :], k.lane[:, :]).then_inc(ranked, 1)
                        dve.tensor_scalar(j[:, lo:N], row(lo, N - lo), mine, 0.0, ALU.is_gt, ALU.add,
                                          accum_out=gt[:, i, bass.ds(e, 1)]).then_inc(ranked, 1)
                        dve.scalar_tensor_tensor(jj, row(lo, P), mine, k.later[:, :], ALU.is_equal, ALU.mult,
                                                 accum_out=tie[:, i, bass.ds(e, 1)]).then_inc(ranked, 1)
                    column = lambda x: x[:, :, bass.ds(e, 1)].rearrange("p t e -> p (t e)")
                    dve.wait_ge(ranked, 3 * NT * e + 3 * NT)
                    dve.scalar_tensor_tensor(rank[:, :], column(gt), first[:, bass.ds(e, 1)], column(ge), ALU.add, ALU.add).then_inc(slots, 1)
                    dve.wait_ge(slots, 2 * e + 2)
                    dve.tensor_tensor(slot_i[:, bass.ds(e * NT, NT)], rank[:, :], column(tie), ALU.add).then_inc(slots, 1)
                dve.wait_ge(spread[0], 16 * EARLY)
                with dve.Fori(0, EARLY) as e:
                    rank_tokens(e)
                dve.wait_ge(spread[1], 16 * (NE - EARLY))
                with dve.Fori(EARLY, NE) as e:
                    rank_tokens(e)

            @block.gpsimd
            def _(pool):
                def stage(n, b):
                    pool.tensor_copy(idx[:, b, :], slot_i[:, bass.ds(NT * n, NT)]).then_inc(staged, 1)
                    pool.tensor_copy(buf[:, b, :, :], recs[:, bass.ds(NT * n, NT), :]).then_inc(staged, 1)

                def send(n, b):
                    pool.wait_ge(staged, 2 * n + 2)
                    for j in range(NT):
                        pool.indirect_dma_start(out=picks, out_offset=bass.IndirectOffsetOnAxis(ap=idx[:, b, j:j + 1], axis=0),
                                                in_=buf[:, b, j, :], in_offset=None).then_inc(sent[b], 16)
                for e in range(NE):
                    if e >= 2:
                        pool.wait_ge(sent[e % 2], 16 * NT * (e // 2))
                    pool.wait_ge(slots, 2 * e + 3)
                    stage(e, e % 2)
                    send(e, e % 2)
                for b in range(2):
                    pool.wait_ge(sent[b], 16 * NT * (NE // 2))
        with nc.Block() as block:
            @block.sync
            def _(sp):
                for t in range(CT):
                    sp.dma_start(back[:, :, t, :], picks.rearrange("(e t p) c -> p e t c", e=NE, p=P)[:, :, t, :]).then_inc(fetched, 16)

            @block.vector
            def _(dve):
                dve.wait_ge(fetched, 16 * CT)
                dve.tensor_copy(chosen_i[:, :, :], back[:, :, :, 0]).then_inc(out, 1)
                dve.tensor_copy(gate[:, :, :], back[:, :, :, 1]).then_inc(out, 1)


class ExpertWeights:

    def __init__(self, nc, ctx, a):
        m = Mem(nc, ctx, "moew")
        self.a = a
        self.w1 = m.sb("w1", [P, 2, KD, FF])
        self.w2 = m.sb("w2", [P, 2, FF // P, D])
        self.b2 = m.sb("b2", [1, 2, D])
        self.w_in = [m.sem(f"in{i}") for i in range(2)]

    def fetch(self, sp, e, b):
        a = self.a
        for out, in_ in ((self.w1[:, b, :, :], a["L0_ffn_W1"]), (self.w2[:, b, :, :], a["L0_ffn_W2"])):
            sp.dma_start(out, in_[bass.ds(e, 1), :, :].rearrange("a (c p) f -> p (a c) f", p=P)).then_inc(self.w_in[b], 16)
        sp.dma_start(self.b2[:, b, :], a["L0_ffn_b2"][bass.ds(e, 1), :]).then_inc(self.w_in[b], 16)


def experts(nc, k, a, w, rows, total, chosen_i, gate, sig):
    with ExitStack() as ctx:
        m = Mem(nc, ctx, "moe")
        b1 = m.sb("b1", [P, NE, FF // P])
        ex = m.sb("ex", [P, 2, CT, D])
        ext = m.sb("ext", [P, KD, CAP])
        hid = m.sb("hid", [P, FF // P, CAP])
        y = m.sb("y", [P, 2, CT, D])
        R = 4
        tb = [m.ps(f"tb{i}", [P, D]) for i in range(CT)]
        hb = [m.ps(f"hb{i}", [P, D]) for i in range(R)]
        ob = [m.ps(f"ob{i}", [P, D]) for i in range(CT)]
        w1, w2, b2, w_in = w.w1, w.w2, w.b2, w.w_in
        got = [m.sem(f"got{i}") for i in range(2)]
        added = [m.sem(f"added{i}") for i in range(CT)]
        b_in, y_free, turned, laid, hidden, act_done, summed, weighed = (m.sem(x) for x in (
            "b_in", "y_free", "turned", "laid", "hidden", "act_done", "summed", "weighed"))
        FT = FF // P
        signs = Signatures(nc, ctx, a["tile_table"], sig)
        with nc.Block() as block:
            @block.sync
            def _(sp):
                sp.dma_start(b1[:, :, :], a["L0_ffn_b1"]).then_inc(b_in, 16)
                for b in range(2):
                    signs.load(sp, b, again=b > 0)
                with sp.Fori(1, NE // 2) as t:
                    for b in range(2):
                        sp.wait_ge(summed, CT * (2 * t) + (CT * (b - 1) + 1))
                        w.fetch(sp, 2 * t + b, b)
                        signs.load(sp, 2 * t + b)

            @block.gpsimd
            def _(pool):
                def gather(e):
                    if e >= 2:
                        pool.wait_ge(turned, CT * (e - 1))
                    for t in range(CT):
                        pool.indirect_dma_start(out=ex[:, e % 2, t, :], out_offset=None, in_=rows,
                                                in_offset=bass.IndirectOffsetOnAxis(ap=chosen_i[:, e, t:t + 1], axis=0)).then_inc(got[e % 2], 16)
                pool.sem_inc(y_free, 2)
                gather(0)
                for e in range(NE):
                    if e + 1 < NE:
                        gather(e + 1)
                    for t in range(CT):
                        pool.wait_ge(weighed, CT * e + t + 1 + CT)
                        if e and t == 0:
                            for o in range(CT):
                                pool.wait_ge(added[o], 16 * e)
                            pool.sem_inc(y_free, 1)
                        pool.indirect_dma_start(out=total, out_offset=bass.IndirectOffsetOnAxis(ap=chosen_i[:, e, t:t + 1], axis=0),
                                                in_=y[:, e % 2, t, :], in_offset=None, compute_op=ALU.add).then_inc(added[t], 16)
                for o in range(CT):
                    pool.wait_ge(added[o], 16 * NE)

            @block.tensor
            def _(pe):
                pe.sem_inc(hidden, 1)
                pe.sem_inc(summed, 1)
                with pe.Fori(0, NE // 2) as tt:
                    for b in range(2):
                        e = 2 * tt + b
                        pe.wait_ge(got[b], 16 * CT * (tt + 1))
                        pe.wait_ge(laid, CT * e + CT)
                        for t in range(CT):
                            for c in range(KD):
                                i = pe.transpose(tb[t][:, c * P:(c + 1) * P], ex[:, b, t, c * P:(c + 1) * P], k.ident[:, :])
                            i.then_inc(turned, 1)
                        pe.wait_ge(w_in[b], 48 * (tt + 1))
                        pe.wait_ge(laid, CT * e + 2 * CT)
                        for f in range(FT):
                            pe.wait_ge(act_done, FT * e + (f + 1))
                            accumulate(pe, hb[f % R][:, 0:CAP],
                                       [(w1[:, b, c, f * P:(f + 1) * P], ext[:, c, :]) for c in range(KD)]).then_inc(hidden, 1)
                        pe.wait_ge(act_done, FT * e + (FT + R))
                        for t in range(CT):
                            pe.wait_ge(weighed, CT * e + t + 1)
                            pe.matmul(ob[t][:, :], k.ones[0:1, :], b2[0:1, b, :], start=True, stop=False)
                            for f in range(FT):
                                i = pe.matmul(ob[t][:, :], hid[:, f, t * P:(t + 1) * P], w2[:, b, f, :], start=False, stop=(f == FT - 1))
                            i.then_inc(summed, 1)

            @block.vector
            def _(dve):
                dve.sem_inc(laid, CT)
                dve.sem_inc(weighed, CT)
                with dve.Fori(0, NE // 2) as tt:
                    for b in range(2):
                        e = 2 * tt + b
                        for t in range(CT):
                            dve.wait_ge(turned, CT * e + t + 1)
                            if t == 0:
                                dve.wait_ge(hidden, FT * e + 1)
                            dve.tensor_copy(ext[:, :, t * P:(t + 1) * P], tb[t][:, :].rearrange("p (c t) -> p c t", c=KD)).then_inc(laid, 1)
                        signs.reduce(dve, e)
                        for t in range(CT):
                            dve.wait_ge(summed, CT * e + t + 2)
                            dve.wait_ge(y_free, e + 1)
                            dve.tensor_scalar(y[:, b, t, :], ob[t][:, :], gate[:, bass.ds(e, 1), t:t + 1].rearrange("p a b -> p (a b)"), None, ALU.mult).then_inc(weighed, 1)
                signs.finish(dve)

            @block.scalar
            def _(act):
                act.wait_ge(b_in, 16)
                act.sem_inc(act_done, R)
                with act.Fori(0, NE // 2) as tt:
                    for b in range(2):
                        e = 2 * tt + b
                        for f in range(FT):
                            act.wait_ge(hidden, FT * e + f + 2)
                            if f == 0:
                                act.wait_ge(summed, CT * e + 1)
                            act.activation(hid[:, f, :], hb[f % R][:, 0:CAP], ACT.Gelu,
                                           bias=b1[:, bass.ds(e, 1), f:f + 1].rearrange("p a b -> p (a b)")).then_inc(act_done, 1)


def store(nc, name, pairs):
    load(nc, name, pairs)


def layer0_ffn(nc, k, a, x1, xn, xt, sig):
    with ExitStack() as ctx:
        m = Mem(nc, ctx, "ffn0")
        chosen_i = m.sb("chosen_i", [P, NE, CT], I32)
        gate = m.sb("gate", [P, NE, CT])
        rows = nc.dram_tensor("expert_rows", (N, D), F32).ap()
        total = nc.dram_tensor("expert_total", (N, D), F32).ap()
        scores_t = nc.dram_tensor("expert_scores", (NE, N), F32).ap()
        picks = nc.dram_tensor("expert_picks", (NE * N, 2), F32).ap()
        layernorm(nc, k, "ln1", x1, xn)
        kept = fetch_ahead(nc, "ffn0_store", [(chunks(rows), xn[:, :, :]), (chunks(total), x1[:, :, :])])
        turn(nc, k, "turn1", xn, xt)
        w = ExpertWeights(nc, ctx, a)
        expert_choice(nc, k, a, w, xt, scores_t, picks, chosen_i, gate)
        fetched(nc, kept)
        experts(nc, k, a, w, rows, total, chosen_i, gate, sig)
        load(nc, "ffn0_load", [(x1[:, :, :], chunks(total))])


LOT = 2
LOTS = NB // LOT
RING = 4


def gat_gather(pool, tables, indices, idx, bufs, staged, got, free):
    k, I = len(tables), 2 * RING

    def stage(n, i):
        for j, col in enumerate(indices):
            pool.tensor_copy(idx[:, i, j, :], col[:, bass.ds(LOT * n, LOT)]).then_inc(staged, 1)

    def fetch(i):
        for j, table in enumerate(tables):
            for u in range(LOT):
                pool.indirect_dma_start(out=bufs[j][:, i % RING, u, :], out_offset=None, in_=table,
                                        in_offset=bass.IndirectOffsetOnAxis(ap=idx[:, i, j, u:u + 1], axis=0)).then_inc(got[i % RING], 16)

    def step(n, i, more=True):
        pool.wait_ge(staged, k * n + k)
        pool.wait_ge(free, n + 1)
        if more:
            stage(n + 1, (i + 1) % I)
        fetch(i)
    stage(0, 0)
    with pool.Fori(0, LOTS // I - 1) as t:
        for i in range(I):
            step(I * t + i, i)
    for i in range(I):
        step(LOTS - I + i, i, i + 1 < I)


def gat_scores(nc, k, a, xl_t, xr_t, alpha, xt, x2):
    with ExitStack() as ctx:
        m = Mem(nc, ctx, "score")
        left = m.sb("left", [P, RING, LOT, D])
        right = m.sb("right", [P, RING, LOT, D])
        att = m.sb("att", [P, D])
        idx = m.sb("idx", [P, 2 * RING, 2, LOT], I32)
        loaded, staged, free, steps = (m.sem(x) for x in ("loaded", "staged", "free", "steps"))
        got = [m.sem(f"got{i}") for i in range(RING)]
        mix = Layer1Mix(nc, ctx, k, a, xt, x2)
        with nc.Block() as block:
            @block.sync
            def _(sp):
                sp.dma_start(att[:, :], a["L1_gnn_att"].rearrange("(a h) c -> a (h c)", a=1).broadcast_to([P, D])).then_inc(loaded, 16)
                mix.load(sp)

            @block.gpsimd
            def _(pool):
                mix.constants(pool)
                gat_gather(pool, [xl_t, xr_t], [k.src_i, k.dst_i], idx, [left, right], staged, got, free)

            @block.tensor
            def _(pe):
                mix.multiply(pe)

            @block.scalar
            def _(act):
                mix.evacuate(act)

            @block.vector
            def _(dve):
                dve.sem_inc(free, RING)
                dve.wait_ge(loaded, 16)

                flat = lambda x, b: x[:, b, :, :].rearrange("p u d -> p (u d)")

                def add(b, full):
                    dve.wait_ge(got[b], 16 * 2 * LOT * full)
                    dve.tensor_tensor(flat(left, b), flat(left, b), flat(right, b), ALU.add).then_inc(steps, 1)

                def rectify(b, added):
                    dve.wait_ge(steps, added)
                    dve.scalar_tensor_tensor(flat(right, b), flat(left, b), 0.2, flat(left, b), ALU.mult, ALU.max).then_inc(steps, 1)

                def weigh(b, rectified):
                    dve.wait_ge(steps, rectified)
                    dve.tensor_tensor(left[:, b, :, :], right[:, b, :, :], att[:, :].unsqueeze(1).broadcast_to([P, LOT, D]),
                                      ALU.mult).then_inc(steps, 1)

                def total(n, b, weighed):
                    dve.wait_ge(steps, weighed)
                    dve.tensor_reduce(alpha[:, bass.ds(n * (LOT * H8), LOT * H8)],
                                      flat(left, b).rearrange("p (q c) -> p q c", c=HC), AX.X, ALU.add).then_inc(free, 1)

                def lots(t, count):
                    for i in range(count):
                        n, b, last = RING * t + (i + 1), (i + 1) % RING, i
                        add(b, t + (1 + (i + 1) // RING))
                        weigh(last, 3 * n - 1)
                        rectify(b, 3 * n)
                        total(n - 1, last, 3 * n + 1)
                add(0, 1)
                rectify(0, 1)
                rings = LOTS // RING - 1
                with dve.Fori(0, rings // 2) as t:
                    lots(t, RING)
                mix.divide(dve)
                with dve.Fori(rings // 2, rings) as t:
                    lots(t, RING)
                lots(rings, RING - 1)
                weigh(RING - 1, 3 * LOTS - 1)
                total(LOTS - 1, RING - 1, 3 * LOTS)


def segment_softmax(nc, k, keys_t, alpha):
    with ExitStack() as ctx:
        m = Mem(nc, ctx, "seg")
        raw = m.sb("raw", [P, 3, SL])
        same_prev = m.sb("same_prev", [P, SL])
        same_next = m.sb("same_next", [P, SL])
        brk = m.sb("brk", [P, SL])
        last = m.sb("last", [P, SL])
        al = m.sb("al", [P, SL])
        run = m.sb("run", [P, SL])
        x = m.sb("x", [P, SL])
        fac = m.sb("fac", [P, 1])
        ends = m.sb("ends", [1, 2, P])
        st = m.sb("st", [1, P])
        carry_row = m.sb("carry_row", [1, P])
        carry = m.sb("carry", [P, 1])
        bank = [m.ps(f"bank{i}", [P, D]) for i in range(2)]
        rows = m.ps("rows", [1, D])
        col = m.ps("col", [P, D])
        loaded, steps, turned, brought, rowed, summed, colled, shifted, exped = (m.sem(x) for x in (
            "loaded", "steps", "turned", "brought", "rowed", "summed", "colled", "shifted", "exped"))
        QB = -(-BS // 4)
        lanes = alpha[:, :].rearrange("p (s i h) -> p i h s", s=SEG, i=BS)
        with nc.Block() as block:
            @block.sync
            def _(sp):
                for o in range(3):
                    v = keys_t[o:EP + o].rearrange("(s n) -> s n", s=SEG)
                    for h in range(H8):
                        sp.dma_start(raw[h * SEG:(h + 1) * SEG, o, :], v).then_inc(loaded, 16)

            @block.tensor
            def _(pe):
                pe.wait_ge(steps, 1)
                for i in range(BS):
                    if i % 4 == 0 and i >= 8:
                        pe.wait_ge(brought, i // 4 - 1)
                    pe.transpose(bank[i // 4 % 2][:, i % 4 * P:(i % 4 + 1) * P], x[:, i * P:(i + 1) * P], k.ident[:, :]).then_inc(turned, 1)
                for r in range(4):
                    pe.wait_ge(rowed, 3 * r + 1)
                    pe.transpose(rows[0:1, 0:P], run[:, SL - 1:SL] if r % 2 == 0 else run[:, 0:1], k.ident[:, :])
                    pe.transpose(rows[0:1, P:2 * P], fac[:, :], k.ident[:, :]).then_inc(summed, 1)
                    pe.wait_ge(rowed, 3 * r + 2)
                    pe.transpose(col[:, 0:1], carry_row[0:1, :], k.ident[0:1, 0:1]).then_inc(colled, 1)

            @block.scalar
            def _(act):
                act.wait_ge(shifted, 1)
                act.activation(al[:, :], al[:, :], ACT.Exp).then_inc(exped, 1)

            @block.vector
            def _(dve):
                c = Chain(dve, steps)
                c.mark(dve.tensor_copy(x[:, :].rearrange("p (i h s) -> p i h s", i=BS, h=H8), lanes))
                for q, i in enumerate(range(0, BS, 4)):
                    w = min(4, BS - i)
                    dve.wait_ge(turned, i + w)
                    dve.tensor_copy(al[:, i * P:(i + w) * P], bank[q % 2][:, 0:w * P]).then_inc(brought, 1)
                dve.wait_ge(loaded, 16 * 3 * H8)
                v = [raw[:, o, :] for o in range(3)]
                c.mark(dve.tensor_tensor(same_prev[:, :], v[1], v[0], ALU.is_equal))
                c.then(dve.tensor_tensor(same_next[:, :], v[1], v[2], ALU.is_equal))
                c.mark(dve.tensor_scalar(brk[:, :], same_prev[:, :], -1.0, BIG, ALU.add, ALU.mult))
                c.then(dve.tensor_scalar(last[:, :], same_next[:, :], -1.0, 1.0, ALU.mult, ALU.add))
                dve.wait_ge(brought, QB)

                def recurrence(r, keepers, add, ops, start, back):
                    way = slice(None, None, -1) if back else slice(None)
                    c.then(dve.tensor_tensor_scan(run[:, way], keepers[:, way], add[:, way], start, *ops))
                    dve.tensor_reduce(fac[:, :], keepers[:, :], AX.X, ALU.min).then_inc(rowed, 1)
                    dve.wait_ge(summed, r + 1)
                    c.then(dve.tensor_copy(ends[:, :, :].rearrange("a b p -> a (b p)"), rows[0:1, 0:2 * P]))
                    first, over = (SEG - 1, slice(0, P - 1)) if back else (0, slice(1, P))
                    c.then(dve.memset(ends[0:1, 1, first::SEG], -BIG if ops[0] == ALU.add else 0.0))
                    c.then(dve.tensor_tensor_scan(st[0:1, way], ends[0:1, 1, way], ends[0:1, 0, way], start, *ops))
                    c.then(dve.tensor_copy(carry_row[0:1, over], st[0:1, 1:P] if back else st[0:1, 0:P - 1]))
                    dve.memset(carry_row[0:1, first::SEG], start).then_inc(rowed, 1)
                    dve.wait_ge(colled, r + 1)
                    dve.tensor_copy(carry[:, :], col[:, 0:1]).then_inc(rowed, 1)
                    dve.wait_ge(rowed, 3 * r + 3)
                    c.then(dve.tensor_tensor_scan(run[:, way], keepers[:, way], add[:, way], carry[:, :], *ops))

                linear = (ALU.mult, ALU.add)
                recurrence(0, brk, al, (ALU.add, ALU.max), -BIG, False)
                c.then(dve.tensor_tensor(x[:, :], last[:, :], run[:, :], ALU.mult))
                recurrence(1, same_next, x, linear, 0.0, True)
                dve.tensor_tensor(al[:, :], al[:, :], run[:, :], ALU.subtract).then_inc(shifted, 1)
                dve.wait_ge(exped, 1)
                recurrence(2, same_prev, al, linear, 0.0, False)
                c.then(dve.tensor_tensor(x[:, :], last[:, :], run[:, :], ALU.mult))
                recurrence(3, same_next, x, linear, 0.0, True)
                c.then(dve.tensor_scalar(run[:, :], run[:, :], 1e-16, None, ALU.max))
                c.then(dve.reciprocal(run[:, :], run[:, :]))
                c.then(dve.tensor_tensor(al[:, :], al[:, :], run[:, :], ALU.mult))
        turned, brought = m.sem("turned_b"), m.sem("brought_b")
        with nc.Block() as block:
            @block.tensor
            def _(pe):
                for i in range(BS):
                    if i % 4 == 0 and i >= 8:
                        pe.wait_ge(brought, i // 4 - 1)
                    pe.transpose(bank[i // 4 % 2][:, i % 4 * P:(i % 4 + 1) * P], al[:, i * P:(i + 1) * P], k.ident[:, :]).then_inc(turned, 1)

            @block.vector
            def _(dve):
                for q, i in enumerate(range(0, BS, 4)):
                    w = min(4, BS - i)
                    dve.wait_ge(turned, i + w)
                    dve.tensor_copy(lanes[:, i:i + w, :, :], bank[q % 2][:, 0:w * P].rearrange("p (i h s) -> p i h s", i=w, h=H8)).then_inc(brought, 1)


def gat_sum(nc, k, a, xl_t, alpha, xn, out):
    with ExitStack() as ctx:
        m = Mem(nc, ctx, "agg")
        left = m.sb("left", [P, RING, LOT, D])
        wx = m.sb("wx", [P, RING, LOT, D])
        to = m.sb("to", [P, RING, LOT, P])
        idx = m.sb("idx", [P, 2 * RING, 1, LOT], I32)
        bias = m.sb("bias", [1, D])
        neg = m.sb("neg", [P, 2, D])
        acc = m.ps("acc", [P, NG * D])
        loaded, staged, free, ready, used, rested = (m.sem(x) for x in ("loaded", "staged", "free", "ready", "used", "rested"))
        steps, low, exped = (m.sem(x) for x in ("steps", "low", "exped"))
        got = [m.sem(f"got{i}") for i in range(RING)]
        with nc.Block() as block:
            @block.sync
            def _(sp):
                sp.dma_start(bias[:, :], a["L1_gnn_bias"].rearrange("(a n) -> a n", a=1)).then_inc(loaded, 16)

            @block.gpsimd
            def _(pool):
                gat_gather(pool, [xl_t], [k.src_i], idx, [left], staged, got, free)

            @block.vector
            def _(dve):
                dve.tensor_tensor(out[:, :, :], out[:, :, :], xn[:, :, :], ALU.add).then_inc(rested, 1)
                dve.sem_inc(free, RING)
                with dve.Fori(0, LOTS // RING) as t:
                    for b in range(RING):
                        n = RING * t + b
                        dve.wait_ge(used, n + 1)
                        for u in range(LOT):
                            dve.tensor_scalar(to[:, b, u, :], k.iotaf[:, 0:P], k.local[:, bass.ds(LOT * n + u, 1)], None,
                                              ALU.is_equal).then_inc(ready, 1)
                        dve.wait_ge(got[b], 16 * LOT * (t + 1))
                        dve.tensor_tensor(wx[:, b, :, :].rearrange("p u (h c) -> p (u h) c", c=HC),
                                          left[:, b, :, :].rearrange("p u (h c) -> p (u h) c", c=HC),
                                          alpha[:, bass.ds(n * (LOT * H8), LOT * H8)].unsqueeze(2).broadcast_to([P, LOT * H8, HC]),
                                          ALU.mult).then_inc(free, 1)

            @block.tensor
            def _(pe):
                pe.wait_ge(loaded, 16)
                pe.sem_inc(used, RING)
                for g in range(NG):
                    pe.matmul(acc[:, g * D:(g + 1) * D], k.ones[0:1, :], bias[:, :], start=True, stop=False, skip_group_check=True)
                with pe.Fori(0, LOTS // RING) as t:
                    groups = block_groups(nc, k, RING * LOT * t, RING * LOT)
                    for b in range(RING):
                        n = RING * t + b
                        for u in range(LOT):
                            g = groups[LOT * b + u]
                            if u == 0:
                                pe.wait_ge(ready, LOT * n + LOT)
                                pe.wait_ge(free, n + (RING + 1))
                            i = pe.matmul(acc[:, bass.ds(g, D)], to[:, b, u, :], wx[:, b, u, :], start=False, stop=False,
                                          skip_group_check=True)
                        i.then_inc(used, 1)
        with nc.Block() as block:
            @block.vector
            def _(dve):
                def below(g):
                    if g >= 2:
                        dve.wait_ge(steps, 2 * (g - 1))
                    dve.tensor_scalar(neg[:, g % 2, :], acc[:, g * D:(g + 1) * D], 0.0, None, ALU.min).then_inc(low, 1)
                below(0)
                dve.wait_ge(rested, 1)
                for g in range(NG):
                    if g + 1 < NG:
                        below(g + 1)
                    dve.wait_ge(exped, g + 1)
                    z = neg[:, g % 2, :]
                    dve.scalar_tensor_tensor(z, acc[:, g * D:(g + 1) * D], 0.0, z, ALU.max, ALU.add).then_inc(steps, 1)
                    dve.wait_ge(steps, 2 * g + 1)
                    dve.scalar_tensor_tensor(out[:, g, :], z, -1.0, out[:, g, :], ALU.add, ALU.add).then_inc(steps, 1)

            @block.scalar
            def _(act):
                for g in range(NG):
                    act.wait_ge(low, g + 1)
                    act.activation(neg[:, g % 2, :], neg[:, g % 2, :], ACT.Exp).then_inc(exped, 1)


def layer1_gnn(nc, k, a, keys_t, x1, xn, xt):
    with ExitStack() as ctx:
        m = Mem(nc, ctx, "gat")
        alpha = m.sb("alpha", [P, NB * H8])
        xl_t = nc.dram_tensor("gat_left", (N, D), F32).ap()
        xr_t = nc.dram_tensor("gat_right", (N, D), F32).ap()
        with ExitStack() as inner:
            mi = Mem(nc, inner, "gatp")
            w = mi.sb("w", [P, 2, KD, D])
            y = mi.sb("y", [P, 2, NT, D])
            weights = fetch_ahead(nc, "gat_load", [(w[:, 0, :, :], chunks(a["L1_gnn_W_l"])), (w[:, 1, :, :], chunks(a["L1_gnn_W_r"]))])
            layernorm(nc, k, "ln2", x1, xn)
            turn(nc, k, "turn2", xn, xt)
            fetched(nc, weights)
            stores = []
            for side, table in enumerate((xl_t, xr_t)):
                products(nc, f"gat_p{side}", NT,
                         lambda pe, n, bank: accumulate(pe, bank[:, :], tile_terms(xt, w[:, side, :, :], n)),
                         lambda eng, n, bank: copy(eng, y[:, side, n, :], bank[:, :]))
                stores.append(fetch_ahead(nc, f"gat_store{side}", [(chunks(table), y[:, side, :, :])]))
            for x in stores:
                fetched(nc, x)
        gat_scores(nc, k, a, xl_t, xr_t, alpha, xt, x1)
        segment_softmax(nc, k, keys_t, alpha)
        gat_sum(nc, k, a, xl_t, alpha, xn, x1)


NH = 16
HD = D // NH


class Ring:

    def __init__(self, m, ring):
        self.bank = [m.ps(f"bank{i}", [P, D]) for i in range(ring)]
        self.full, self.free, self.made, self.brought = m.sem("full"), m.sem("free"), 0, 0

    def make(self, pe, count, product):
        for n in range(count):
            if self.made >= len(self.bank):
                pe.wait_ge(self.free, self.made - len(self.bank) + 1)
            product(pe, n, self.bank[self.made % len(self.bank)]).then_inc(self.full, 1)
            self.made += 1

    def settle(self, pe):
        pe.wait_ge(self.free, self.made)

    def bring(self, act, count, out):
        for n in range(count):
            act.wait_ge(self.full, self.brought + 1)
            out(act, n, self.bank[self.brought % len(self.bank)]).then_inc(self.free, 1)
            self.brought += 1


class Layer1Mix:
    EVACUATED = 2 * KD + 2 * NT + KD + NT * KD

    def __init__(self, nc, ctx, k, a, xt, x2):
        m = Mem(nc, ctx, "mix1")
        self.k, self.a, self.xt, self.x2 = k, a, xt, x2
        self.w = m.sb("w", [P, 3, KD, D])
        self.bias = m.sb("bias", [1, D])
        self.qt = m.sb("qt", [P, KD, N])
        self.kk = m.sb("kk", [P, NT, D])
        self.v = m.sb("v", [P, NT, D + 1])
        self.kv = m.sb("kv", [P, KD, P + 4])
        self.den = m.sb("den", [P, NT, NH])
        self.pr, self.pt = self.kk, self.qt
        self.ring = Ring(m, 4)
        self.landed, self.proj_in, self.laid, self.steps, self.divided = (m.sem(x) for x in (
            "landed", "proj_in", "laid", "steps", "divided"))

    def load(self, sp):
        w, a = self.w, self.a
        for i in range(3):
            sp.dma_start(w[:, i, :, :], chunks(a["L1_mix_qkv_weight"])[:, :, i * D:(i + 1) * D]).then_inc(self.landed, 16)
        sp.dma_start(self.bias[:, :], a["L1_mix_proj_bias"].rearrange("(a n) -> a n", a=1)).then_inc(self.landed, 16)
        sp.wait_ge(self.ring.free, 2 * KD)
        sp.dma_start(w[:, 0, :, :], chunks(a["L1_mix_proj_weight"])).then_inc(self.proj_in, 16)

    def constants(self, pool):
        pool.memset(self.v[:, :, D:D + 1], 1.0).then_inc(self.laid, 1)
        pool.memset(self.kv[:, :, :], 0.0).then_inc(self.laid, 1)

    def multiply(self, pe):
        w, xt, qt, kk, v, kv, k, ring = self.w, self.xt, self.qt, self.kk, self.v, self.kv, self.k, self.ring

        def sums(pe, n, bank):
            here = slice(n * P, (n + 1) * P)
            for i in range(NT):
                pe.matmul(bank[:, 0:P], kk[:, i, here], v[:, i, here], start=(i == 0), stop=(i == NT - 1))
            for i in range(NT):
                t = pe.matmul(bank[:, P:P + 1], kk[:, i, here], v[:, i, D:D + 1], start=(i == 0), stop=(i == NT - 1))
            return t

        def turned(pe, n, bank):
            for c in range(KD):
                t = pe.transpose(bank[:, c * P:(c + 1) * P], self.pr[:, n, c * P:(c + 1) * P], k.ident[:, :])
            return t
        pe.wait_ge(self.landed, 16 * 4)
        ring.make(pe, 2 * KD, lambda pe, n, bank: accumulate(pe, bank[:, :], [
            (w[:, 0, c, (n // 2) * P:(n // 2 + 1) * P], xt[:, c, (n % 2) * D:(n % 2 + 1) * D]) for c in range(KD)]))
        ring.make(pe, 2 * NT, lambda pe, n, bank: accumulate(pe, bank[:, :], tile_terms(xt, w[:, 1 + n % 2, :, :], n // 2)))
        ring.settle(pe)
        pe.wait_ge(self.laid, 1)
        ring.make(pe, KD, sums)
        ring.settle(pe)
        ring.make(pe, NT * KD, lambda pe, n, bank: pe.matmul(
            bank[:, 0:P + 4], qt[:, n % KD, (n // KD) * P:(n // KD + 1) * P], kv[:, n % KD, :], start=True, stop=True))
        pe.wait_ge(self.divided, NT)
        ring.make(pe, NT, turned)
        ring.settle(pe)
        pe.wait_ge(self.proj_in, 16)
        ring.make(pe, NT, lambda pe, n, bank: accumulate(pe, bank[:, :], tile_terms(self.pt, w[:, 0, :, :], n) + [
            (k.ones[0:1, :], self.bias[:, :]), (k.ident[:, :], self.x2[:, n, :])]))

    def evacuate(self, act):
        ring, kv, den, pr = self.ring, self.kv, self.den, self.pr

        def heads(act, n, bank):
            for h in range(P // HD):
                here = slice(h * HD, (h + 1) * HD)
                act.activation(kv[here, n, here], bank[here, here], ACT.Copy)
                i = act.activation(kv[here, n, P + h:P + h + 1], bank[here, P:P + 1], ACT.Copy)
            return i

        def attended(act, n, bank):
            i, g = n // KD, n % KD
            act.activation(den[:, i, 4 * g:4 * g + 4], bank[:, P:P + 4], ACT.Copy)
            return act.activation(pr[:, i, g * P:(g + 1) * P], bank[:, 0:P], ACT.Copy)
        ring.bring(act, 2 * KD, lambda act, n, bank: act.activation(
            self.qt[:, n // 2, (n % 2) * D:(n % 2 + 1) * D], bank[:, :], ACT.Relu))
        ring.bring(act, 2 * NT, lambda act, n, bank: act.activation(self.kk[:, n // 2, :], bank[:, :], ACT.Relu) if n % 2 == 0
                   else act.activation(self.v[:, n // 2, 0:D], bank[:, :], ACT.Copy))
        act.wait_ge(self.laid, 2)
        ring.bring(act, KD, heads)
        ring.bring(act, NT * KD, attended)
        ring.bring(act, NT, lambda act, n, bank: act.activation(
            self.pt[:, :, n * P:(n + 1) * P], bank[:, :].rearrange("p (c t) -> p c t", c=KD), ACT.Copy))
        ring.bring(act, NT, lambda act, n, bank: act.activation(self.x2[:, n, :], bank[:, :], ACT.Copy))

    def divide(self, dve):
        den = self.den
        c = Chain(dve, self.steps)
        dve.wait_ge(self.ring.free, self.EVACUATED)
        c.then(dve.tensor_scalar(den[:, :, :], den[:, :, :], 1e-15, None, ALU.add))
        c.then(dve.reciprocal(den[:, :, :], den[:, :, :]))
        for i in range(NT):
            heads = self.pr[:, i, :].rearrange("p (h c) -> p h c", c=HD)
            dve.tensor_tensor(heads, heads, den[:, i, :].unsqueeze(2).broadcast_to([P, NH, HD]), ALU.mult).then_inc(self.divided, 1)


BELOW = 15.999999


def route(nc, k, xt, sig, token_t, slot_i, weight_i, token_i):
    with ExitStack() as ctx:
        m = Mem(nc, ctx, "route")
        st = m.sb("st", [P, KD, N], BF16)
        neg = m.sb("neg", [P, KD, N], BF16)
        sc = m.sb("sc", [P, NT, T + CL])
        top = m.sb("top", [P, NT])
        best = m.sb("best", [P, NT])
        one = m.sb("one", [P, NT, T])
        w = m.sb("w", [P, NT, T])
        oneb = m.sb("oneb", [P, NT, T], BF16)
        cnt = m.sb("cnt", [P, T], I32)
        nblk = m.sb("nblk", [P, T])
        end = m.sb("end", [P, T])
        start = m.sb("start", [P, T])
        past = m.sb("past", [P, NBK, T])
        tile_of = m.sb("tile_of", [P, NBK])
        rows = m.sb("rows", [P, NT, 2], I32)
        zero = m.sb("zero", [P, 2 * NL], I32)
        lot = m.sb("lot", [P, NL, 2], I32)
        sb_ = [m.ps(f"s{i}", [P, D]) for i in range(2)]
        rank = m.ps("rank", [P, D])
        tot = m.ps("tot", [P, D])
        steps, signed, scored, hot, ranked, zeroed, filled, slotted, sent, back = (m.sem(x) for x in (
            "steps", "signed", "scored", "hot", "ranked", "zeroed", "filled", "slotted", "sent", "back"))
        wide, cwide = [P, NT, T], [P, NT, CL]
        with nc.Block() as block:
            @block.sync
            def _(sp):
                sp.wait_ge(zeroed, 1)
                sp.dma_start(token_t.rearrange("(p l) c -> p (l c)", p=P), zero[:, :]).then_inc(filled, 16)
                sp.wait_ge(sent, 16 * NT)
                sp.dma_start(lot[:, :, :], token_t.rearrange("(l p) c -> p l c", p=P)).then_inc(back, 16)

            @block.gpsimd
            def _(pool):
                pool.wait_ge(filled, 16)
                pool.wait_ge(slotted, 1)
                for i in range(NT):
                    pool.indirect_dma_start(out=token_t, out_offset=bass.IndirectOffsetOnAxis(ap=slot_i[:, i:i + 1], axis=0),
                                            in_=rows[:, i, :], in_offset=None).then_inc(sent, 16)
                pool.wait_ge(sent, 16 * NT)

            @block.tensor
            def _(pe):
                pe.wait_ge(signed, 1)
                for i in range(NT):
                    o = (i % 4) * (T + CL)
                    t = accumulate(pe, sb_[i // 4][:, o:o + T + CL], [(st[:, c, i * P:(i + 1) * P], sig[:, c, :]) for c in range(KD)])
                t.then_inc(scored, 1)
                pe.wait_ge(hot, 1)
                for i in range(NT):
                    t = accumulate(pe, rank[:, i * T:(i + 1) * T],
                                   [(k.ones_b[:, :], oneb[:, j, :]) for j in range(i)] + [(k.before_b[:, :], oneb[:, i, :])])
                t = accumulate(pe, tot[:, 0:T], [(k.ones_b[:, :], oneb[:, j, :]) for j in range(NT)])
                t.then_inc(ranked, 1)

            @block.vector
            def _(dve):
                c = Chain(dve, steps)
                dve.memset(zero[:, :], 0).then_inc(zeroed, 1)
                c.then(dve.tensor_scalar(neg[:, :, :], xt, 0.0, None, ALU.is_lt))
                c.then(dve.tensor_scalar(st[:, :, :], xt, 0.0, None, ALU.is_gt))
                dve.tensor_tensor(st[:, :, :], st[:, :, :], neg[:, :, :], ALU.subtract).then_inc(signed, 1)
                dve.wait_ge(scored, 1)
                for h in range(2):
                    c.mark(dve.tensor_copy(sc[:, 4 * h:4 * h + 4, :].rearrange("p i s -> p (i s)"), sb_[h][:, 0:4 * (T + CL)]))
                dve.wait_ge(steps, c.n)

                def first_best(x, width, shape, out):
                    c.then(dve.tensor_reduce(top[:, :], x, AX.X, ALU.max))
                    c.then(dve.tensor_tensor(w[:, :, 0:width], x, top[:, :].unsqueeze(2).broadcast_to(shape), ALU.is_equal))
                    c.then(dve.tensor_scalar(w[:, :, 0:width], w[:, :, 0:width], -1000.0, 1000.0, ALU.mult, ALU.add))
                    c.then(dve.tensor_tensor(w[:, :, 0:width], w[:, :, 0:width],
                                             k.iotaf[:, 0:width].unsqueeze(1).broadcast_to(shape), ALU.add))
                    c.then(dve.tensor_reduce(out, w[:, :, 0:width], AX.X, ALU.min))
                first_best(sc[:, :, T:T + CL], CL, cwide, best[:, :])
                c.then(dve.tensor_tensor(w[:, :, 0:CL], k.iotaf[:, 0:CL].unsqueeze(1).broadcast_to(cwide),
                                         best[:, :].unsqueeze(2).broadcast_to(cwide), ALU.is_equal))
                c.then(dve.tensor_scalar(w[:, :, 0:CL], w[:, :, 0:CL], -1.0, 10000.0, ALU.add, ALU.mult))
                for i in range(NT):
                    c.mark(dve.tensor_tensor(one[:, i, :].rearrange("p (g u) -> p g u", g=CL), sc[:, i, 0:T].rearrange("p (g u) -> p g u", g=CL),
                                             w[:, i, 0:CL].unsqueeze(2).broadcast_to([P, CL, T // CL]), ALU.add))
                dve.wait_ge(steps, c.n)
                first_best(one[:, :, :], T, wide, best[:, :])
                c.then(dve.tensor_tensor(one[:, :, :], k.iotaf[:, 0:T].unsqueeze(1).broadcast_to(wide),
                                         best[:, :].unsqueeze(2).broadcast_to(wide), ALU.is_equal))
                dve.tensor_copy(oneb[:, :, :], one[:, :, :]).then_inc(hot, 1)
                dve.wait_ge(ranked, 1)
                c.then(dve.tensor_scalar(cnt[:, :], tot[:, 0:T], float(BT - 1), None, ALU.add))
                c.then(dve.tensor_scalar(cnt[:, :], cnt[:, :], BT.bit_length() - 1, None, ALU.arith_shift_right))
                c.then(dve.tensor_copy(nblk[:, :], cnt[:, :]))
                c.then(dve.tensor_tensor_scan(end[:, :], nblk[:, :], k.ones[:, 0:T], 0.0, ALU.add, ALU.mult))
                c.then(dve.tensor_tensor(start[:, :], end[:, :], nblk[:, :], ALU.subtract))
                c.then(dve.tensor_scalar(start[:, :], start[:, :], float(BT), None, ALU.mult))
                c.then(dve.tensor_tensor(w[:, :, :], rank[:, 0:NT * T].rearrange("p (i t) -> p i t", t=T),
                                         start[:, :].unsqueeze(1).broadcast_to(wide), ALU.add))
                c.then(dve.tensor_tensor(w[:, :, :], w[:, :, :], one[:, :, :], ALU.mult))
                c.then(dve.tensor_reduce(top[:, :], w[:, :, :], AX.X, ALU.add))
                c.mark(dve.tensor_copy(slot_i[:, :], top[:, :]))
                c.mark(dve.memset(rows[:, :, 1], 0))
                for i in range(NT):
                    c.mark(dve.tensor_scalar(rows[:, i, 0:1], k.lane[:, :], float(i * P), None, ALU.add))
                dve.wait_ge(steps, c.n)
                dve.sem_inc(slotted, 1)
                c.then(dve.tensor_tensor(past[:, :, :], k.iotaf[:, 0:NBK].unsqueeze(2).broadcast_to([P, NBK, T]),
                                         end[:, :].unsqueeze(1).broadcast_to([P, NBK, T]), ALU.is_ge))
                c.then(dve.tensor_reduce(tile_of[:, :], past[:, :, :], AX.X, ALU.add))
                c.then(dve.tensor_scalar(tile_of[:, :], tile_of[:, :], float(T - 1), float(P), ALU.min, ALU.mult))
                c.then(dve.tensor_scalar(weight_i[:, :], tile_of[:, :], k.lane[:, :], None, ALU.add))
                dve.wait_ge(back, 16)
                c.then(dve.tensor_copy(token_i[:, :], lot[:, :, 0]))


def tile_ffn(nc, k, table, rows_t, y_t, weight_i, token_i, room):
    with ExitStack() as ctx:
        m = Mem(nc, ctx, "tile")
        R4, TURN = 4, 8
        w = m.sb("w", [P, R4, LB, ROW])
        x = m.sb("x", [P, R4, D])
        xt = m.sb("xt", [P, 2, KD, P])
        hn = m.sb("hn", [P, R4, P])
        s = m.sb("s", [P, 2, P])
        r = m.sb("r", [P, P])
        above = m.sb("above", [P, P])
        cell = m.sb("cell", [P, 2, P], F16)
        at = m.sb("at", [P, P])
        one = m.sb("one", [P, P, GRID], F16)
        pick = room.rearrange("p c n -> p (c n)").rearrange("p (a b g) -> p a b g", a=2, g=GRID)
        spline = m.sb("spline", [P, 2, P])
        slope = m.sb("slope", [P, P])
        hs = m.sb("hs", [P, 2, P])
        y = m.sb("y", [P, 2, D])
        idx = m.sb("idx", [P, TURN, LB + 1], I32)
        tb = [m.ps(f"tb{i}", [P, D]) for i in range(2)]
        hb = [m.ps(f"hb{i}", [P, D]) for i in range(2)]
        yb = [m.ps(f"yb{i}", [P, D]) for i in range(2)]
        gb = [m.ps(f"gb{i}", [P, D]) for i in range(2)]
        got = [m.sem(f"got{i}") for i in range(R4)]
        stored = [m.sem(f"stored{i}") for i in range(2)]
        staged, turned, laid, hidden, squashed, splined, summed, brought, y_free, steps, split, scaled, sloped, gathered = (m.sem(x) for x in (
            "staged", "turned", "laid", "hidden", "squashed", "splined", "summed", "brought", "y_free", "steps", "split", "scaled",
            "sloped", "gathered"))
        with nc.Block() as block:
            @block.gpsimd
            def _(pool):
                def stage(n, i):
                    pool.tensor_copy(idx[:, i, 0:LB], weight_i[:, bass.ds(LB * n, LB)]).then_inc(staged, 1)
                    pool.tensor_copy(idx[:, i, LB:LB + 1], token_i[:, bass.ds(n, 1)]).then_inc(staged, 1)

                def fetch(i):
                    b = i % R4
                    pool.indirect_dma_start(out=x[:, b, :], out_offset=None, in_=rows_t,
                                            in_offset=bass.IndirectOffsetOnAxis(ap=idx[:, i, LB:LB + 1], axis=0)).then_inc(got[b], 16)
                    for u in range(LB):
                        pool.indirect_dma_start(out=w[:, b, u, :], out_offset=None, in_=table,
                                                in_offset=bass.IndirectOffsetOnAxis(ap=idx[:, i, u:u + 1], axis=0)).then_inc(got[b], 16)

                def step(n, i, more=True):
                    pool.wait_ge(staged, 2 * n + 2)
                    pool.wait_ge(summed, n + 1)
                    if more:
                        stage(n + 1, (i + 1) % TURN)
                    fetch(i)
                stage(0, 0)
                with pool.Fori(0, NL // TURN - 1) as t:
                    for i in range(TURN):
                        step(TURN * t + i, i)
                for i in range(TURN):
                    step(NL - TURN + i, i, i + 1 < TURN)

            @block.tensor
            def _(pe):
                pe.sem_inc(hidden, 2)
                pe.sem_inc(summed, R4)

                def down(n, i, got_count):
                    b, r = i % 2, i % R4
                    pe.wait_ge(got[r], got_count)
                    pe.wait_ge(laid, n + 1)
                    for c in range(KD):
                        i = pe.transpose(tb[b][:, c * P:(c + 1) * P], x[:, r, c * P:(c + 1) * P], k.ident[:, :])
                    i.then_inc(turned, 1)
                    pe.wait_ge(laid, n + 3)
                    pe.wait_ge(squashed, n + 1)
                    for u in range(LB):
                        i = accumulate(pe, hb[b][:, u * BT:(u + 1) * BT], [
                            (w[:, r, u, c * P:(c + 1) * P], xt[:, b, c, u * BT:(u + 1) * BT]) for c in range(KD)])
                    i.then_inc(hidden, 1)

                def up(n, i):
                    b, r = i % 2, i % R4
                    pe.wait_ge(sloped, n + 1)
                    pe.wait_ge(split, n + 3)
                    accumulate(pe, gb[b][:, 0:P], [(k.ident[:, :], pick[:, 1, :, g]) for g in range(GRID)]).then_inc(gathered, 1)
                    pe.wait_ge(scaled, n + 3)
                    pe.wait_ge(brought, n + 1)
                    for u in range(LB):
                        i = pe.matmul(yb[b][u * BT:(u + 1) * BT, :], hs[:, b, u * BT:(u + 1) * BT], w[:, r, u, W_UP:W_UP + D],
                                      start=True, stop=True, tile_position=(0, u * BT))
                    i.then_inc(summed, 1)
                lot = 16 * (LB + 1)
                down(0, 0, lot)
                down(1, 1, lot)
                with pe.Fori(0, NL // TURN - 1) as t:
                    for i in range(TURN):
                        down(TURN * t + (i + 2), (i + 2) % TURN, lot * (TURN // R4 * t + ((i + 2) // R4 + 1)))
                        up(TURN * t + i, i)
                for i in range(TURN):
                    n = NL - TURN + i
                    if i + 2 < TURN:
                        down(n + 2, i + 2, lot * ((n + 2) // R4 + 1))
                    up(n, i)

            @block.scalar
            def _(act):
                for q in (laid, squashed, scaled, brought):
                    act.sem_inc(q, 2)

                def into(n, i):
                    b = i % 2
                    act.wait_ge(turned, n + 1)
                    act.wait_ge(hidden, n + 1)
                    act.activation(xt[:, b, :, :].rearrange("p c t -> p (c t)"), tb[b][:, :], ACT.Copy).then_inc(laid, 1)
                    act.wait_ge(hidden, n + 3)
                    act.wait_ge(split, n + 1)
                    act.activation(hn[:, i % R4, :], hb[b][:, 0:P], ACT.Sigmoid).then_inc(squashed, 1)

                def out(n, b, r):
                    act.wait_ge(splined, n + 3)
                    for u in range(LB):
                        i = act.activation(hs[:, b, u * BT:(u + 1) * BT], spline[:, b, u * BT:(u + 1) * BT], ACT.Copy,
                                           scale=w[:, r, u, W_SCALE:W_SCALE + 1])
                    i.then_inc(scaled, 1)
                    act.wait_ge(summed, n + (R4 + 1))
                    act.wait_ge(y_free, n + 1)
                    act.activation(y[:, b, :], yb[b][:, :], ACT.Copy).then_inc(brought, 1)
                into(0, 0)
                into(1, 1)
                with act.Fori(0, NL // TURN - 1) as t:
                    for i in range(TURN):
                        into(TURN * t + (i + 2), i + 2)
                        out(TURN * t + i, i % 2, i % R4)
                for i in range(TURN):
                    n = NL - TURN + i
                    if i + 2 < TURN:
                        into(n + 2, i + 2)
                    out(n, i % 2, i % R4)

            @block.vector
            def _(dve):
                dve.sem_inc(splined, 2)
                dve.sem_inc(split, R4)
                grid = k.iota16[:, 0:GRID].unsqueeze(1).broadcast_to([P, P, GRID])
                blk = lambda z, u: z[:, u * BT:(u + 1) * BT]
                A, B = 5, 2 * LB + 2

                def cells(b, r4):
                    def one(): return dve.tensor_scalar(s[:, b, :], hn[:, r4, :], float(GRID), BELOW, ALU.mult, ALU.min)
                    def two(): return dve.tensor_scalar(r[:, :], s[:, b, :], 8388608.0, None, ALU.add)
                    def three(): return dve.tensor_scalar(r[:, :], r[:, :], 8388608.0, None, ALU.subtract)
                    def four(): return dve.tensor_tensor(above[:, :], r[:, :], s[:, b, :], ALU.is_gt)
                    def five(): return dve.tensor_tensor(cell[:, b, :], r[:, :], above[:, :], ALU.subtract)
                    return one, two, three, four, five

                def lot(n, b, r4, full):
                    base = (A + B) * n + A
                    ahead = cells(1 - b, (r4 + 1) % R4) if full else [None] * A
                    count = [0]

                    def mark(ins):
                        ins.then_inc(steps, 1)
                        count[0] += 1
                        return count[0]

                    def cell_step(j, after):
                        if not full:
                            return 0
                        if j == 0:
                            dve.wait_ge(squashed, n + 4)
                        if after:
                            dve.wait_ge(steps, base + after)
                        return mark(ahead[j]())
                    weights = lambda u, o: w[:, r4, u, o:o + GRID].unsqueeze(1).broadcast_to([P, BT, GRID])
                    hot = mark(dve.tensor_tensor(one[:, :, :], grid, cell[:, b, :].unsqueeze(2).broadcast_to([P, P, GRID]), ALU.is_equal))
                    mark(dve.scalar_tensor_tensor(at[:, :], hn[:, r4, :], float(GRID), cell[:, b, :], ALU.mult, ALU.subtract))
                    c1 = cell_step(0, 0)
                    dve.wait_ge(steps, base + hot)
                    for u in range(LB):
                        i = dve.tensor_tensor(blk(pick[:, 1], u), blk(one, u), weights(u, W_SLOPE), ALU.mult)
                        if u < LB - 1:
                            mark(i)
                        else:
                            i.then_inc(sloped, 1)
                    c2 = cell_step(1, c1)
                    for u in range(LB):
                        picked_b = mark(dve.tensor_tensor(blk(pick[:, 0], u), blk(one, u), weights(u, W_BASE), ALU.mult))
                    c3 = cell_step(2, c2)
                    c4 = cell_step(3, c3)
                    dve.wait_ge(steps, base + picked_b)
                    dve.wait_ge(scaled, n + 1)
                    base_in = mark(dve.tensor_reduce(spline[:, b, :], pick[:, 0], AX.X, ALU.add))
                    cell_step(4, c4)
                    dve.wait_ge(steps, base + base_in)
                    dve.wait_ge(gathered, n + 1)
                    dve.tensor_tensor(slope[:, :], gb[b][:, 0:P], at[:, :], ALU.mult).then_inc(split, 1)
                    dve.wait_ge(split, n + (R4 + 1))
                    dve.tensor_tensor(spline[:, b, :], spline[:, b, :], slope[:, :], ALU.add).then_inc(splined, 1)
                    assert count[0] == (A if full else 0) + B, count
                dve.wait_ge(squashed, 3)
                for j, step in enumerate(cells(0, 0)):
                    step().then_inc(steps, 1)
                    dve.wait_ge(steps, j + 1)
                with dve.Fori(0, NL // TURN - 1) as t:
                    for i in range(TURN):
                        lot(TURN * t + i, i % 2, i % R4, True)
                for i in range(TURN):
                    lot(NL - TURN + i, i % 2, i % R4, i + 1 < TURN)

            @block.sync
            def _(sp):
                sp.sem_inc(y_free, 2)
                v = y_t.rearrange("(l p) d -> p l d", p=P)

                def put(n, b):
                    sp.wait_ge(brought, n + 3)
                    sp.dma_start(v[:, bass.ds(n, 1), :].rearrange("p a d -> p (a d)"), y[:, b, :]).then_inc(stored[b], 16)
                put(0, 0)
                with sp.Fori(0, NL // 2 - 1) as t:
                    put(2 * t + 1, 1)
                    sp.wait_ge(stored[0], 16 * t + 16)
                    sp.sem_inc(y_free, 1)
                    put(2 * t + 2, 0)
                    sp.wait_ge(stored[1], 16 * t + 16)
                    sp.sem_inc(y_free, 1)
                put(NL - 1, 1)
                for b in range(2):
                    sp.wait_ge(stored[b], 16 * (NL // 2))


def layer1_ffn(nc, k, a, x3, xn, xt, sig, out):
    with ExitStack() as ctx:
        m = Mem(nc, ctx, "ffn1")
        xa = m.sb("xa", [P, NT, D])
        slot_i = m.sb("slot_i", [P, NT], I32)
        weight_i = m.sb("weight_i", [P, NBK], I32)
        token_i = m.sb("token_i", [P, NL], I32)
        gamma = m.sb("gamma", [P, D])
        beta = m.sb("beta", [P, D])
        rows_t = nc.dram_tensor("tile_rows", (N, D), F32).ap()
        token_t = nc.dram_tensor("tile_tokens", (NL * P, 2), I32).ap()
        y_t = nc.dram_tensor("tile_out", (NL * P, D), F32).ap()
        table = a["tile_table"]
        scales = fetch_ahead(nc, "ffn1_load", [(gamma[:, :], a["L1_ffn_gamma"].rearrange("(a n) -> a n", a=1).broadcast_to([P, D])),
                               (beta[:, :], a["L1_ffn_beta"].rearrange("(a n) -> a n", a=1).broadcast_to([P, D]))])
        layernorm(nc, k, "ln3", x3, xa)
        fetched(nc, scales)
        layernorm(nc, k, "ln4", xa, xn, extra=(gamma, beta))
        kept = fetch_ahead(nc, "ffn1_store", [(chunks(rows_t), xn[:, :, :])])
        turn(nc, k, "turn3", xn, xt)
        route(nc, k, xt, sig, token_t, slot_i, weight_i, token_i)
        fetched(nc, kept)
        tile_ffn(nc, k, table, rows_t, y_t, weight_i, token_i, xt)
        got, stored = [m.sem(f"got{h}") for h in range(2)], m.sem("stored")
        rested, summed = m.sem("rested"), m.sem("summed")
        y = xn
        half = [slice(h * NT // 2, (h + 1) * NT // 2) for h in range(2)]
        with nc.Block() as block:
            @block.gpsimd
            def _(pool):
                for i in range(NT):
                    pool.indirect_dma_start(out=y[:, i, :], out_offset=None, in_=y_t,
                                            in_offset=bass.IndirectOffsetOnAxis(ap=slot_i[:, i:i + 1], axis=0)).then_inc(got[2 * i // NT], 16)

            @block.vector
            def _(dve):
                dve.tensor_tensor(xa[:, :, :], xa[:, :, :], x3[:, :, :], ALU.add).then_inc(rested, 1)
                dve.wait_ge(rested, 1)
                for h in range(2):
                    dve.wait_ge(got[h], 16 * NT // 2)
                    dve.tensor_tensor(xa[:, half[h], :], xa[:, half[h], :], y[:, half[h], :], ALU.add).then_inc(summed, 1)

            @block.sync
            def _(sp):
                for h in range(2):
                    sp.wait_ge(summed, h + 1)
                    sp.dma_start(chunks(out)[:, half[h], :], xa[:, half[h], :]).then_inc(stored, 16)
                sp.wait_ge(stored, 32)


USED = ("x", "src", "dst", "L0_gnn_W", "L0_gnn_b", "L0_gnn_diffusion_weights",
        "L0_mix_Wq", "L0_mix_Wk", "L0_mix_Wv", "L0_mix_W1", "L0_mix_W2",
        "L0_ffn_Wg", "L0_ffn_W1", "L0_ffn_b1", "L0_ffn_W2", "L0_ffn_b2",
        "L1_gnn_W_l", "L1_gnn_W_r", "L1_gnn_att", "L1_gnn_bias",
        "L1_mix_qkv_weight", "L1_mix_proj_weight", "L1_mix_proj_bias",
        "L1_ffn_gamma", "L1_ffn_beta", "tile_table")


def program(nc, a, out):
    with ExitStack() as ctx:
        k = keep(nc, ctx)
        m = Mem(nc, ctx, "x")
        x, xn, xt, x1 = (m.sb(s, [P, NT, D]) for s in ("x", "xn", "xt", "x1"))
        xt = xt[:, :, :].rearrange("p a b -> p (a b)").rearrange("p (c n) -> p c n", c=KD)
        sig = m.sb("sig", [P, KD, T + CL], BF16)
        keys_t = nc.dram_tensor("edge_keys", (EP + 2,), F32).ap()
        with part(nc):
            constants(nc, k)
            tokens = Ahead(nc, "x", [(x[:, :, :], chunks(a["x"]))])
            with ExitStack() as mixing:
                w = Mem(nc, mixing, "mix0").sb("w", [P, 5, KD, D])
                weights = Ahead(nc, "mix0_w", [(w[:, i, :, :], chunks(a[f"L0_mix_{s}"]))
                                               for i, s in enumerate(("Wq", "Wk", "Wv", "W1", "W2"))])
                sort_edges(nc, k, a["src"], a["dst"], keys_t, [tokens, weights])
                fetched(nc, tokens)
                layernorm(nc, k, "ln0", x, xn)
                turn(nc, k, "turn0", xn, xt)
                layer0_mix(nc, k, xn, xt, x1, w, weights)
            layer0_gnn(nc, k, a, x, xn, xt, x1)
        with part(nc):
            layer0_ffn(nc, k, a, x1, xn, xt, sig)
            layer1_gnn(nc, k, a, keys_t, x1, xn, xt)
        with part(nc):
            layer1_ffn(nc, k, a, x1, xn, xt, sig, out)


def lay_out(name, v):
    if name in ("L0_mix_Wq", "L0_mix_Wk", "L0_mix_Wv", "L0_mix_W1", "L0_mix_W2", "L1_mix_qkv_weight", "L1_mix_proj_weight"):
        return v.T
    if name == "L0_ffn_b1":
        return v.reshape(NE, FF // P, P).transpose(2, 0, 1)
    return v


def kernel(**inputs):
    import numpy as np
    import concourse.bacc as bacc
    from concourse.bass_utils import run_bass_kernel_spmd as run

    nc = bacc.Bacc("TRN2", target_bir_lowering=False, num_devices=1)
    arrays, a = {}, {}
    for n in USED:
        if n == "tile_table":
            v = np.concatenate([
                inputs["L1_ffn_Wd"].reshape(T, DH, KD, P).transpose(0, 3, 2, 1).reshape(T, P, D),
                inputs["L1_ffn_Wu"].transpose(0, 2, 1), inputs["L1_ffn_spline_bases"], inputs["L1_ffn_spline_slopes"],
                np.broadcast_to(inputs["L1_ffn_scale"][:, None, None], (T, P, ROW - W_SCALE))], axis=2).reshape(T * P, ROW)
        else:
            v = lay_out(n, inputs[n])
        v = np.ascontiguousarray(v)
        arrays[f"in_{n}"] = v
        a[n] = nc.dram_tensor(f"in_{n}", v.shape, mybir.dt.from_np(v.dtype), kind="ExternalInput").ap()
    out = nc.dram_tensor("result", (N, D), F32, kind="ExternalOutput").ap()
    program(nc, a, out)
    r = run(nc, [arrays], core_ids=[0])
    return r.results[0]["result"]
```
